# Optimizing a Trainium2 kernel written in Bass

```python
import numpy as np
import jax
import jax.numpy as jnp

def _softmax(x, axis=-1):
    return jax.nn.softmax(x, axis=axis)

def _gelu(x):
    return jax.nn.gelu(x, approximate=True)

def _silu(x):
    return jax.nn.silu(x)

def _sigmoid(x):
    return jax.nn.sigmoid(x)

def _layernorm(x, axis=-1, eps=1e-05):
    m = jnp.mean(x, axis=axis, keepdims=True)
    v = jnp.var(x, axis=axis, keepdims=True)
    return (x - m) / jnp.sqrt(v + eps)

def _scatter_add(tgt, idx, src, axis=0):
    return tgt.at[idx].add(src)

def _segment_sum(src, seg, n):
    return jax.ops.segment_sum(src, seg, n)
kernel_name = 'mk_early_fusion_embed_d1_tok_img768_r4_dbb2b8'

def setup_inputs(seed: int=0):
    np.random.seed(seed)
    _w = jnp.asarray

    def _rec_inputs():
        import jax
        import jax.numpy as jnp
        _rk = jax.random.key(seed)
        x = -0.000153849 + 1.00027 * jax.random.normal(jax.random.fold_in(_rk, 1), (32, 3, 84, 84), jnp.float32)
        x_txt = jax.random.randint(jax.random.fold_in(_rk, 51), (32, 128), 0, 8000, jnp.int32)
        return (x, x_txt)
    x, x_txt = _rec_inputs()

    def _L0_tok_setup():
        import jax, jax.numpy as jnp
        import numpy as np
        EMB = 192
        HEADS = 12
        PATCH = 16
        IN_CH = 3
        key = jax.random.key(seed)
        ks = jax.random.split(key, 11)
        x = jax.random.normal(ks[0], (8, IN_CH, 128, 128), dtype=jnp.float32)
        s_conv = 1.0 / np.sqrt(IN_CH * PATCH * PATCH)
        s_lin = 1.0 / np.sqrt(EMB)
        conv_w = jax.random.uniform(ks[1], (EMB, IN_CH, PATCH, PATCH), jnp.float32, -s_conv, s_conv)
        conv_b = jax.random.uniform(ks[2], (EMB,), jnp.float32, -s_conv, s_conv)
        wq = jax.random.uniform(ks[3], (EMB, EMB), jnp.float32, -s_lin, s_lin)
        bq = jax.random.uniform(ks[4], (EMB,), jnp.float32, -s_lin, s_lin)
        wk = jax.random.uniform(ks[5], (EMB, EMB), jnp.float32, -s_lin, s_lin)
        bk = jax.random.uniform(ks[6], (EMB,), jnp.float32, -s_lin, s_lin)
        wv = jax.random.uniform(ks[7], (EMB, EMB), jnp.float32, -s_lin, s_lin)
        bv = jax.random.uniform(ks[8], (EMB,), jnp.float32, -s_lin, s_lin)
        wo = jax.random.uniform(ks[9], (EMB, EMB), jnp.float32, -s_lin, s_lin)
        bo = jax.random.uniform(ks[10], (EMB,), jnp.float32, -s_lin, s_lin)
        return {'x': x, 'conv_w': conv_w, 'conv_b': conv_b, 'wq': wq, 'bq': bq, 'wk': wk, 'bk': bk, 'wv': wv, 'bv': bv, 'wo': wo, 'bo': bo}
    _L0_tok_all = _L0_tok_setup()
    _L0_tok_in = {k: v for k, v in _L0_tok_all.items() if k in ('conv_w', 'conv_b', 'wq', 'bq', 'wk', 'bk', 'wv', 'bv', 'wo', 'bo')}
    del _L0_tok_all

    def _L0_txt_setup():
        import jax, jax.numpy as jnp
        import numpy as np
        N_QUBITS = 6
        N_LAYERS = 3
        DIM = 1 << N_QUBITS
        VOCAB = 8000
        EMBED = 192
        B, S = (16, 1024)

        def _cnot_perm(control, target):
            idx = np.arange(DIM)
            cbit = idx >> N_QUBITS - 1 - control & 1
            flipped = idx ^ 1 << N_QUBITS - 1 - target
            return np.where(cbit == 1, flipped, idx)
        _idx = np.arange(DIM)
        Z_SIGNS = np.stack([1.0 - 2.0 * (_idx >> N_QUBITS - 1 - q & 1) for q in range(N_QUBITS)], axis=1).astype(np.float32)

        def _apply_ry(state, theta, q):
            T = state.shape[0]
            left, right = (1 << q, 1 << N_QUBITS - 1 - q)
            s = state.reshape(T, left, 2, right)
            c = jnp.cos(theta * 0.5)[:, None, None]
            sn = jnp.sin(theta * 0.5)[:, None, None]
            a0, a1 = (s[:, :, 0, :], s[:, :, 1, :])
            out = jnp.stack([c * a0 - sn * a1, sn * a0 + c * a1], axis=2)
            return out.reshape(T, DIM)

        def _apply_rz(state, theta, q):
            T = state.shape[0]
            left, right = (1 << q, 1 << N_QUBITS - 1 - q)
            s = state.reshape(T, left, 2, right)
            ph = jnp.exp(1j * (theta * 0.5)).astype(state.dtype)[:, None, None]
            out = jnp.stack([jnp.conj(ph) * s[:, :, 0, :], ph * s[:, :, 1, :]], axis=2)
            return out.reshape(T, DIM)

        def _circuit_expvals(params):
            T = params.shape[0]
            state = jnp.zeros((T, DIM), dtype=jnp.complex64).at[:, 0].set(1.0)
            for layer in range(N_LAYERS):
                for q in range(N_QUBITS):
                    state = _apply_ry(state, params[:, layer, q, 0], q)
                    state = _apply_rz(state, params[:, layer, q, 1], q)
                if layer < N_LAYERS - 1:
                    for q in range(N_QUBITS - 1):
                        state = state[:, _cnot_perm(q, q + 1)]
                    if N_QUBITS > 2:
                        state = state[:, _cnot_perm(N_QUBITS - 1, 0)]
            probs = state.real ** 2 + state.imag ** 2
            return probs @ jnp.asarray(Z_SIGNS)
        key = jax.random.key(seed)
        k1, k2, k3, k4 = jax.random.split(key, 4)
        token_ids = jax.random.randint(k1, (B, S), 0, VOCAB)
        quantum_params = jax.random.normal(k2, (VOCAB, N_LAYERS, N_QUBITS, 2), dtype=jnp.float32) * 0.1
        post_w = jax.random.normal(k3, (EMBED, N_QUBITS), dtype=jnp.float32) / np.sqrt(N_QUBITS)
        post_b = jax.random.normal(k4, (EMBED,), dtype=jnp.float32) * 0.01
        return {'token_ids': token_ids, 'quantum_params': quantum_params, 'post_w': post_w, 'post_b': post_b}
    _L0_txt_all = _L0_txt_setup()
    _L0_txt_in = {k: v for k, v in _L0_txt_all.items() if k in ('quantum_params', 'post_w', 'post_b')}
    del _L0_txt_all

    def _L0_attn_setup():
        import jax, jax.numpy as jnp
        import numpy as np
        B, T, D = (8, 512, 192)
        NUM_HEADS, KEY_DIM, VAL_DIM = (12, 64, 64)
        QKV_OUT = NUM_HEADS * (2 * KEY_DIM + VAL_DIM)
        MHK = NUM_HEADS * KEY_DIM
        key = jax.random.key(seed)
        k = jax.random.split(key, 5)
        x = jax.random.normal(k[0], (B, T, D), dtype=jnp.float32)
        w_qkv = jax.random.normal(k[1], (D, QKV_OUT), dtype=jnp.float32) * (1.0 / np.sqrt(D))
        b_qkv = jax.random.normal(k[2], (QKV_OUT,), dtype=jnp.float32) * 0.02
        w_out = jax.random.normal(k[3], (NUM_HEADS * VAL_DIM, D), dtype=jnp.float32) * (1.0 / np.sqrt(NUM_HEADS * VAL_DIM))
        b_out = jax.random.normal(k[4], (D,), dtype=jnp.float32) * 0.02
        return {'x': x, 'w_qkv': w_qkv, 'b_qkv': b_qkv, 'w_out': w_out, 'b_out': b_out}
    _L0_attn_all = _L0_attn_setup()
    _L0_attn_in = {k: v for k, v in _L0_attn_all.items() if k in ('w_qkv', 'b_qkv', 'w_out', 'b_out')}
    del _L0_attn_all

    def _L0_ffn_setup():
        import jax, jax.numpy as jnp
        import numpy as np
        DIM = 192
        HID = 128
        E = 16
        G = 8
        TOPK_G = 4
        TOPK_E = 4
        SCALE = 2.5
        B, S = (2, 512)
        key = jax.random.key(seed)
        ks = jax.random.split(key, 9)
        init = lambda k, shape: jax.random.normal(k, shape, dtype=jnp.float32) * 0.02
        z = lambda shape: jnp.zeros(shape, jnp.float32)
        return {'x': jax.random.normal(ks[0], (B, S, DIM), dtype=jnp.float32), 'gate_w': init(ks[1], (DIM, E)), 'gate_b': z((E,)), 'bias': z((E,)), 'Wu': init(ks[2], (E, DIM, HID)), 'bu': z((E, HID)), 'Wg': init(ks[3], (E, DIM, HID)), 'bg': z((E, HID)), 'Wd': init(ks[4], (E, HID, DIM)), 'bd': z((E, DIM)), 'sWu': init(ks[5], (DIM, HID)), 'sbu': z((HID,)), 'sWg': init(ks[6], (DIM, HID)), 'sbg': z((HID,)), 'sWd': init(ks[7], (HID, DIM)), 'sbd': z((DIM,))}
    _L0_ffn_all = _L0_ffn_setup()
    _L0_ffn_in = {k: v for k, v in _L0_ffn_all.items() if k in ('gate_w', 'gate_b', 'bias', 'Wu', 'bu', 'Wg', 'bg', 'Wd', 'bd', 'sWu', 'sbu', 'sWg', 'sbg', 'sWd', 'sbd')}
    del _L0_ffn_all
    return {'x': x, 'x_txt': x_txt, 'L0_tok_conv_w': _L0_tok_in['conv_w'], 'L0_tok_conv_b': _L0_tok_in['conv_b'], 'L0_tok_wq': _L0_tok_in['wq'], 'L0_tok_bq': _L0_tok_in['bq'], 'L0_tok_wk': _L0_tok_in['wk'], 'L0_tok_bk': _L0_tok_in['bk'], 'L0_tok_wv': _L0_tok_in['wv'], 'L0_tok_bv': _L0_tok_in['bv'], 'L0_tok_wo': _L0_tok_in['wo'], 'L0_tok_bo': _L0_tok_in['bo'], 'L0_txt_quantum_params': _L0_txt_in['quantum_params'], 'L0_txt_post_w': _L0_txt_in['post_w'], 'L0_txt_post_b': _L0_txt_in['post_b'], 'L0_attn_w_qkv': _L0_attn_in['w_qkv'], 'L0_attn_b_qkv': _L0_attn_in['b_qkv'], 'L0_attn_w_out': _L0_attn_in['w_out'], 'L0_attn_b_out': _L0_attn_in['b_out'], 'L0_ffn_gate_w': _L0_ffn_in['gate_w'], 'L0_ffn_gate_b': _L0_ffn_in['gate_b'], 'L0_ffn_bias': _L0_ffn_in['bias'], 'L0_ffn_Wu': _L0_ffn_in['Wu'], 'L0_ffn_bu': _L0_ffn_in['bu'], 'L0_ffn_Wg': _L0_ffn_in['Wg'], 'L0_ffn_bg': _L0_ffn_in['bg'], 'L0_ffn_Wd': _L0_ffn_in['Wd'], 'L0_ffn_bd': _L0_ffn_in['bd'], 'L0_ffn_sWu': _L0_ffn_in['sWu'], 'L0_ffn_sbu': _L0_ffn_in['sbu'], 'L0_ffn_sWg': _L0_ffn_in['sWg'], 'L0_ffn_sbg': _L0_ffn_in['sbg'], 'L0_ffn_sWd': _L0_ffn_in['sWd'], 'L0_ffn_sbd': _L0_ffn_in['sbd']}

def reference(x, x_txt, L0_tok_conv_w, L0_tok_conv_b, L0_tok_wq, L0_tok_bq, L0_tok_wk, L0_tok_bk, L0_tok_wv, L0_tok_bv, L0_tok_wo, L0_tok_bo, L0_txt_quantum_params, L0_txt_post_w, L0_txt_post_b, L0_attn_w_qkv, L0_attn_b_qkv, L0_attn_w_out, L0_attn_b_out, L0_ffn_gate_w, L0_ffn_gate_b, L0_ffn_bias, L0_ffn_Wu, L0_ffn_bu, L0_ffn_Wg, L0_ffn_bg, L0_ffn_Wd, L0_ffn_bd, L0_ffn_sWu, L0_ffn_sbu, L0_ffn_sWg, L0_ffn_sbg, L0_ffn_sWd, L0_ffn_sbd):
    import jax
    import jax.numpy as jnp

    def _L0_tok_ref(x, conv_w, conv_b, wq, bq, wk, bk, wv, bv, wo, bo):
        import jax, jax.numpy as jnp
        import numpy as np
        EMB = 192
        HEADS = 12
        PATCH = 16
        IN_CH = 3
        t = jax.lax.conv_general_dilated(x, conv_w, window_strides=(PATCH, PATCH), padding='VALID', dimension_numbers=('NCHW', 'OIHW', 'NCHW')) + conv_b[None, :, None, None]
        B, C, Hp, Wp = t.shape
        N = Hp * Wp
        t = t.reshape(B, C, N).transpose(0, 2, 1)
        D = C // HEADS
        scale = D ** (-0.5)
        q = (t @ wq.T + bq).reshape(B, N, HEADS, D).transpose(0, 2, 1, 3)
        k = (t @ wk.T + bk).reshape(B, N, HEADS, D).transpose(0, 2, 1, 3)
        v = (t @ wv.T + bv).reshape(B, N, HEADS, D).transpose(0, 2, 1, 3)
        attn = jax.nn.softmax(jnp.einsum('bhnd,bhmd->bhnm', q, k) * scale, axis=-1)
        out = jnp.einsum('bhnm,bhmd->bhnd', attn, v)
        out = out.transpose(0, 2, 1, 3).reshape(B, N, C)
        out = out @ wo.T + bo
        return out

    def _L0_txt_ref(token_ids, quantum_params, post_w, post_b):
        import jax, jax.numpy as jnp
        import numpy as np
        N_QUBITS = 6
        N_LAYERS = 3
        DIM = 1 << N_QUBITS
        VOCAB = 8000
        EMBED = 192
        B, S = (16, 1024)

        def _cnot_perm(control, target):
            idx = np.arange(DIM)
            cbit = idx >> N_QUBITS - 1 - control & 1
            flipped = idx ^ 1 << N_QUBITS - 1 - target
            return np.where(cbit == 1, flipped, idx)
        _idx = np.arange(DIM)
        Z_SIGNS = np.stack([1.0 - 2.0 * (_idx >> N_QUBITS - 1 - q & 1) for q in range(N_QUBITS)], axis=1).astype(np.float32)

        def _apply_ry(state, theta, q):
            T = state.shape[0]
            left, right = (1 << q, 1 << N_QUBITS - 1 - q)
            s = state.reshape(T, left, 2, right)
            c = jnp.cos(theta * 0.5)[:, None, None]
            sn = jnp.sin(theta * 0.5)[:, None, None]
            a0, a1 = (s[:, :, 0, :], s[:, :, 1, :])
            out = jnp.stack([c * a0 - sn * a1, sn * a0 + c * a1], axis=2)
            return out.reshape(T, DIM)

        def _apply_rz(state, theta, q):
            T = state.shape[0]
            left, right = (1 << q, 1 << N_QUBITS - 1 - q)
            s = state.reshape(T, left, 2, right)
            ph = jnp.exp(1j * (theta * 0.5)).astype(state.dtype)[:, None, None]
            out = jnp.stack([jnp.conj(ph) * s[:, :, 0, :], ph * s[:, :, 1, :]], axis=2)
            return out.reshape(T, DIM)

        def _circuit_expvals(params):
            T = params.shape[0]
            state = jnp.zeros((T, DIM), dtype=jnp.complex64).at[:, 0].set(1.0)
            for layer in range(N_LAYERS):
                for q in range(N_QUBITS):
                    state = _apply_ry(state, params[:, layer, q, 0], q)
                    state = _apply_rz(state, params[:, layer, q, 1], q)
                if layer < N_LAYERS - 1:
                    for q in range(N_QUBITS - 1):
                        state = state[:, _cnot_perm(q, q + 1)]
                    if N_QUBITS > 2:
                        state = state[:, _cnot_perm(N_QUBITS - 1, 0)]
            probs = state.real ** 2 + state.imag ** 2
            return probs @ jnp.asarray(Z_SIGNS)
        b, s = token_ids.shape
        params = quantum_params[token_ids.reshape(-1)]
        ev = _circuit_expvals(params)
        emb = ev @ post_w.T + post_b
        return emb.reshape(b, s, -1)

    def _L0_attn_ref(x, w_qkv, b_qkv, w_out, b_out):
        import jax, jax.numpy as jnp
        import numpy as np
        B, T, D = (8, 512, 192)
        NUM_HEADS, KEY_DIM, VAL_DIM = (12, 64, 64)
        QKV_OUT = NUM_HEADS * (2 * KEY_DIM + VAL_DIM)
        MHK = NUM_HEADS * KEY_DIM
        qkv = jnp.einsum('btd,de->bte', x, w_qkv) + b_qkv
        q = qkv[:, :, :MHK]
        k = qkv[:, :, MHK:2 * MHK]
        v = qkv[:, :, 2 * MHK:]
        scores = jnp.einsum('bqd,bkd->bqk', q, k) / jnp.sqrt(jnp.float32(KEY_DIM))
        attn = jax.nn.softmax(scores, axis=-1)
        out = jnp.einsum('bqk,bkd->bqd', attn, v)
        return jnp.einsum('btd,de->bte', out, w_out) + b_out

    def _L0_ffn_ref(x, gate_w, gate_b, bias, Wu, bu, Wg, bg, Wd, bd, sWu, sbu, sWg, sbg, sWd, sbd):
        import jax, jax.numpy as jnp
        import numpy as np
        DIM = 192
        HID = 128
        E = 16
        G = 8
        TOPK_G = 4
        TOPK_E = 4
        SCALE = 2.5
        B, S = (2, 512)
        orig_shape = x.shape
        xt = x.reshape(-1, DIM)
        T = xt.shape[0]
        scores = jax.nn.softmax(xt @ gate_w + gate_b, axis=-1)
        orig_scores = jax.lax.stop_gradient(scores)
        s = scores + bias[None, :]
        s3 = s.reshape(T, G, E // G)
        group_scores = jax.lax.top_k(s3, 2)[0].sum(-1)
        gidx = jax.lax.top_k(group_scores, TOPK_G)[1]
        gmask = jnp.any(jnp.arange(G)[None, None, :] == gidx[:, :, None], axis=1)
        s_masked = jnp.where(gmask[:, :, None], s3, -jnp.inf).reshape(T, E)
        _, idx = jax.lax.top_k(s_masked, TOPK_E)
        w = jnp.take_along_axis(orig_scores, idx, axis=1) * SCALE
        w_full = jnp.zeros((T, E), xt.dtype).at[jnp.arange(T)[:, None], idx].add(w)
        up = jax.nn.silu(jnp.einsum('td,edh->teh', xt, Wu) + bu)
        gt = jnp.einsum('td,edh->teh', xt, Wg) + bg
        act = up * gt * w_full[:, :, None]
        y = jnp.einsum('teh,ehd->td', act, Wd) + w_full @ bd
        sh = jax.nn.silu(xt @ sWu + sbu) * (xt @ sWg + sbg)
        y = y + sh @ sWd + sbd
        return y.reshape(orig_shape)
    h = _L0_tok_ref(x, L0_tok_conv_w, L0_tok_conv_b, L0_tok_wq, L0_tok_bq, L0_tok_wk, L0_tok_bk, L0_tok_wv, L0_tok_bv, L0_tok_wo, L0_tok_bo)
    h = jnp.concatenate([h, _L0_txt_ref(x_txt, L0_txt_quantum_params, L0_txt_post_w, L0_txt_post_b)], axis=1)
    h = h + _L0_attn_ref(_layernorm(h, axis=-1), L0_attn_w_qkv, L0_attn_b_qkv, L0_attn_w_out, L0_attn_b_out)
    h = h + _L0_ffn_ref(_layernorm(h, axis=-1), L0_ffn_gate_w, L0_ffn_gate_b, L0_ffn_bias, L0_ffn_Wu, L0_ffn_bu, L0_ffn_Wg, L0_ffn_bg, L0_ffn_Wd, L0_ffn_bd, L0_ffn_sWu, L0_ffn_sbu, L0_ffn_sWg, L0_ffn_sbg, L0_ffn_sWd, L0_ffn_sbd)
    return h

_drawn_inputs = setup_inputs


def setup_inputs(seed=0):
    import zlib

    import numpy as np

    out = dict(_drawn_inputs(seed))
    spreads = {'L0_ffn_gate_b': (0.0, 0.8),
     'L0_ffn_bias': (0.0, 0.273),
     'L0_ffn_bu': (0.0, 0.8),
     'L0_ffn_bg': (0.0, 0.8),
     'L0_ffn_bd': (0.0, 0.289),
     'L0_ffn_sbu': (0.0, 0.8),
     'L0_ffn_sbg': (0.0, 0.8),
     'L0_ffn_sbd': (0.0, 0.691)}
    factors = {'L0_tok_wq': 3.509,
     'L0_tok_bq': 8.0,
     'L0_tok_wk': 3.378,
     'L0_tok_bk': 64.0,
     'L0_txt_quantum_params': 3.925,
     'L0_txt_post_b': 5.385,
     'L0_attn_b_qkv': 3.509,
     'L0_attn_b_out': 3.639,
     'L0_ffn_gate_w': 8.0,
     'L0_ffn_Wu': 8.0,
     'L0_ffn_Wg': 8.0,
     'L0_ffn_Wd': 8.0,
     'L0_ffn_sWu': 6.43,
     'L0_ffn_sWg': 6.727,
     'L0_ffn_sWd': 6.697}
    for name, (base, spread) in spreads.items():
        noise = np.random.default_rng([zlib.crc32(name.encode()), seed]).standard_normal(out[name].shape)
        drawn = base * np.exp(spread * noise) if base else spread * noise
        out[name] = jnp.asarray(drawn.astype(out[name].dtype))
    for name, factor in factors.items():
        out[name] = (out[name] * factor).astype(out[name].dtype)
    return out
```

```python
from contextlib import ExitStack

import numpy as np
import concourse.bass as bass
from concourse import mybir

F32 = mybir.dt.float32
I32 = mybir.dt.int32
U32 = mybir.dt.uint32
ALU = mybir.AluOpType
ACT = mybir.ActivationFunctionType
AX = mybir.AxisListType

P = 128
NB = 32
BB = 4
TURNS = NB // BB
TXT = 128
IMG = 25
SLOT = 32
SEQ = TXT + IMG
SPAN = TXT + SLOT
TILES = BB + 1
D = 192
DB = D - P
PIX = 768
KP = PIX // P
HEADS, HD = 12, 16
HT = HEADS // 4
QK = 768
KQ = QK // P
E, HID = 16, 128
ES = E + 1
G = 8
NQ = 6
NS = 1 << NQ
FF = BB * SEQ
HALF = FF // 2
FFPAD = TILES * P
NPROD = 512
RB = NPROD // P
TWO_PI = 6.283185
ROUND = 12582912.0
BIG = 3.0e38
EPS = 1e-5

C1, S1, CP1, SP1, C2, S2, CP2, SP2, C3, S3 = [NQ * i for i in range(10)]
NTRIG = NQ * 10

DVE_CHAIN = 124
POOL_CHAIN = 146
ACT_CHAIN = 2


class Chain:

    def __init__(self, eng, sem, turn=None, per=0):
        self.eng, self.sem, self.turn, self.per, self.n = eng, sem, turn, per, 0

    def mark(self, ins):
        self.n += 1
        ins.then_inc(self.sem, 1)

    def wait(self):
        base = 0 if self.turn is None else self.turn * self.per
        self.eng.wait_ge(self.sem, base + self.n)

    def link(self, ins):
        self.mark(ins)
        self.wait()


def early_fusion(nc, patches, tokens, conv_w, conv_b, wq, wk, wv, wo, tok_const, params, post_w,
                 wq_big, wk_big, wv_big, wout_big, bout_big, gate_w, bias, wu, bu, wg, bg, wd, bd,
                 reduce_w, sel_e, ident_in, out):
    ctx = ExitStack()
    with ctx:
        def sb(name, shape, dt=F32):
            return ctx.enter_context(nc.sbuf_tensor(name, shape, dt))

        def sem(name):
            return ctx.enter_context(nc.semaphore(name))

        bank = [ctx.enter_context(nc.psum_tensor(f"bank{i}", [P, 512], F32)) for i in range(8)]

        ident = sb("ident", [P, P])
        conv_sb = sb("conv_sb", [P, KP, D])
        conv_bA = sb("conv_bA", [P, 1])
        conv_bB = sb("conv_bB", [DB, 1])
        KB = DB + 1 + 2 * BB
        wqA, wqB = sb("wqA", [P, HT * P]), sb("wqB", [KB, HT * P])
        wkA, wkB = sb("wkA", [P, HT * P]), sb("wkB", [KB, HT * P])
        wvA, wvB = sb("wvA", [P, D]), sb("wvB", [DB + 1, D])
        woA, woB = sb("woA", [P, D]), sb("woB", [DB + 1, D])
        pw_sb = sb("pw_sb", [NQ + 1, D])
        red_sb = sb("red_sb", [P, RB, 2 * NQ])
        gwA, gwB = sb("gwA", [P, E]), sb("gwB", [DB + 1, E])
        bias_sb = sb("bias_sb", [P, E])
        sel_sb = sb("sel_sb", [ES, ES * P])
        wuA, wuB = sb("wuA", [P, ES * HID]), sb("wuB", [DB, ES * HID])
        wgA, wgB = sb("wgA", [P, ES * HID]), sb("wgB", [DB, ES * HID])
        wd_sb = sb("wd_sb", [HID, ES * D])
        bd_sb = sb("bd_sb", [ES, D])
        bu_sb, bg_sb = sb("bu_sb", [HID, ES]), sb("bg_sb", [HID, ES])
        MA, MB = sb("MA", [P, D + 1]), sb("MB", [DB + 1, D + 1])
        OA, OB = sb("OA", [P, D]), sb("OB", [DB + 1, D])
        idx_sb = sb("idx_sb", [P, NB], I32)
        par_sb = sb("par_sb", [P, NB, 36])
        trig = sb("trig", [P, NTRIG, NB])
        V1 = sb("V1", [P, 2, NQ, BB])
        EA = sb("EA", [P, 2, NS // 2, BB])
        EB = sb("EB", [P, 2, NS // 2, BB])
        GG = sb("GG", [P, 2, 4, BB])
        X0 = sb("X0", [P, 2, NS, BB])
        X1 = sb("X1", [P, 2, NS, BB])
        ST = sb("ST", [P, 2, NS, BB])
        prods = sb("prods", [P, BB, NPROD])
        patch_sb = sb("patch_sb", [P, KP, P])
        tA, tB = sb("tA", [P, P]), sb("tB", [KB, P])
        qT = sb("qT", [P, HT * P])
        kdiag = sb("kdiag", [P, HT, 4, P])
        v_sb = sb("v_sb", [P, D])
        imax = sb("imax", [P, HEADS])
        isum = sb("isum", [P, HEADS])
        irec = sb("irec", [P, HEADS])
        iprob = sb("iprob", [P, HEADS, P])
        iprobT = sb("iprobT", [P, HEADS, P])
        io = sb("io", [P, D])
        ioA, ioB = sb("ioA", [P, P]), sb("ioB", [DB + 1, P])
        prodT = sb("prodT", [P, RB, BB, P])
        trig_k = prodT[:, :, :, :].rearrange("p r t n -> p (r t n)")[:, 0:NTRIG * NB]
        wbig = [x[:, :, :].rearrange("p h n -> p (h n)")[:, 0:KQ * (D + 1)] for x in (iprob, iprobT)]
        evt = sb("evt", [P, 2, BB, NQ])
        ev = sb("ev", [P, BB, NQ + 1])
        evT = sb("evT", [NQ + 1, BB * P])
        h = sb("h", [P, TILES, D])
        stats = sb("stats", [P, TILES, 6])
        mv = sb("mv", [P, TILES, 2])
        vare = sb("vare", [P, TILES])
        lnv = sb("lnv", [P, TILES])
        rstd = sb("rstd", [P, TILES])
        nt = sb("nt", [P, TILES])
        xn = sb("xn", [P, TILES, D + 1])
        xTA, xTB = sb("xTA", [P, BB, SPAN]), sb("xTB", [DB + 1, BB, SPAN])
        yA, yB = sb("yA", [P, BB, SPAN]), sb("yB", [DB + 1, BB, SPAN])
        nmax = sb("nmax", [P, TILES])
        nbias = sb("nbias", [P, TILES])
        asum = sb("asum", [P, TILES])
        arec = sb("arec", [P, TILES])
        prob = sb("prob", [P, TILES, SEQ])
        pimg = sb("pimg", [P, TILES, P])
        pTA, pTB = sb("pTA", [P, BB, SPAN]), sb("pTB", [P, BB, SPAN])
        zA, zB = sb("zA", [P, FFPAD]), sb("zB", [DB + 1, FFPAD])
        h2 = sb("h2", [P, TILES, D])
        xm = sb("xm", [P, TILES, D + 1])
        x2A, x2B = sb("x2A", [P, FFPAD]), sb("x2B", [DB + 1, FFPAD])
        lmax = sb("lmax", [P, TILES])
        lg = sb("lg", [P, TILES, E])
        lsum = sb("lsum", [P, TILES])
        score = sb("score", [P, TILES, E])
        sbias = sb("sbias", [P, TILES, E])
        gsum = sb("gsum", [P, TILES, G])
        top8 = sb("top8", [P, TILES, 8])
        cmp_g = sb("cmp_g", [P, TILES, E])
        cmp_e = sb("cmp_e", [P, TILES, E])
        scan_a = sb("scan_a", [P, TILES, E])
        scan_b = sb("scan_b", [P, TILES, E])
        ngt = sb("ngt", [P, TILES])
        keep = sb("keep", [P, TILES, E])
        wfull = sb("wfull", [P, TILES, ES])
        wT = sb("wT", [ES, FFPAD])
        sl = sb("sl", [HID, 2, HALF])
        gated = sb("gated", [HID, 2, HALF])
        act_w = sb("act_w", [HID, 2, HALF])
        yTA, yTB = sb("yTA", [P, FFPAD]), sb("yTB", [DB, FFPAD])
        spare = sb("spare", [P, 1])
        o_sb = sb("o_sb", [P, TILES, D])
        bo_row = o_sb[0:DB + 1, 0, :]

        names = """loads_tok loads_txt loads_big loads_ffn idx_in par_in consts_ready products_ready mm_big
            trig_ready trig_raw patches_in conv_done t_ready tproj_done tqkv_ready iscore_done iprob_sub iprob_exp
            iprobT_done iprobT_ready ipv_done io_ready ioT_done ioT_ready iout_done
            prods_ready prodT_done prodT_ready expval_done ev_ready evT_done evT_ready emb_done h_ready
            var_ready rstd0_ready xn_ready xT_done xT_ready y_done y_ready ascore_done nbias_ready prob_ready pimg_ready
            pT_done pT_ready z_done z_ready aout_done h2_ready xm_ready x2_done x2_ready gate_done lsub_ready lexp_ready
            wfull_ready wT_done wT_ready u_done g_done w_done sl_ready act_ready down_done ycols_ready
            fin_done o_ready out_stored dve_own dve_setup pool_own pool_setup act_own act_setup u_free w_free""".split()
        S = {n: sem(n) for n in names}

        AHEAD = ("tproj_done", "iscore_done", "prodT_done", "expval_done", "o_ready", "out_stored")

        def start(eng, *ahead):
            for name in ahead:
                eng.sem_inc(S[name], 1)

        def at(eng, name, it, per, n=None):
            eng.wait_ge(S[name], it * per + (per if n is None else n) + (name in AHEAD))

        def ln_root(act, own, it, which):
            at(act, "var_ready", it, 2, which + 1)
            own.link(nc.scalar.activation(lnv[:, :], vare[:, :], ACT.Ln))
            nc.scalar.activation(rstd[:, :], lnv[:, :], ACT.Exp, scale=-0.5).then_inc(S["rstd0_ready"], 1)

        block = ctx.enter_context(nc.Block())

        @block.sync
        def _(sp):
            def load(dst, src, name):
                sp.dma_start(dst, src).then_inc(S[name], 16)

            start(sp, "out_stored")
            load(idx_sb[:, :], tokens, "idx_in")
            load(ident[:, :], ident_in, "loads_tok")
            load(conv_sb[:, :, :], conv_w, "loads_tok")
            load(patch_sb[:, :, :], patches[0], "patches_in")
            load(conv_bA[:, :], conv_b[0:P, :], "loads_tok")
            load(conv_bB[:, :], conv_b[P:D, :], "loads_tok")
            for w, a, b in ((wq, wqA, wqB), (wk, wkA, wkB), (wv, wvA, wvB), (wo, woA, woB)):
                load(a[:, :], w[0:P, :], "loads_tok")
                load(b[:, :], w[P:w.shape[0], :], "loads_tok")
            load(tB[DB:KB, :], tok_const, "loads_tok")
            load(ioB[DB:DB + 1, :], tok_const[0:1, :], "loads_tok")
            load(wbig[0], wq_big, "loads_big")
            load(wbig[1], wk_big, "loads_big")
            load(bo_row[DB:DB + 1, :], bout_big, "loads_big")
            load(pw_sb[:, :], post_w, "loads_txt")
            load(red_sb[:, :, :], reduce_w, "loads_txt")
            load(gwA[:, :], gate_w[0:P, :], "loads_ffn")
            load(gwB[:, :], gate_w[P:D + 1, :], "loads_ffn")
            load(bias_sb[:, :], bias.partition_broadcast(P), "loads_ffn")
            load(sel_sb[:, :], sel_e, "loads_ffn")
            for w, a, b in ((wu, wuA, wuB), (wg, wgA, wgB)):
                load(a[:, :], w[0:P, :], "loads_ffn")
                load(b[:, :], w[P:D, :], "loads_ffn")
            load(wd_sb[:, :], wd, "loads_ffn")
            load(bd_sb[:, :], bd, "loads_ffn")
            load(bu_sb[:, :], bu, "loads_ffn")
            load(bg_sb[:, :], bg, "loads_ffn")
            sp.wait_ge(S["mm_big"], 2)
            load(wbig[0], wv_big, "loads_big")
            load(wbig[1][:, 0:KQ * D], wout_big, "loads_big")

            def store(it):
                at(sp, "o_ready", it, 3)
                sp.dma_start(out[bass.ds(it * BB, BB), IMG:SEQ, :].rearrange("b s d -> s b d"),
                             o_sb[:, 0:BB, :]).then_inc(S["out_stored"], 16)
                for j in range(BB):
                    sp.dma_start(out[bass.ds(it * BB + j, 1), 0:IMG, :].rearrange("b s d -> (b s) d"),
                                 o_sb[j * SLOT:j * SLOT + IMG, BB, :]).then_inc(S["out_stored"], 16)

            with sp.Fori(0, TURNS - 1) as it:
                at(sp, "conv_done", it, 1)
                sp.dma_start(patch_sb[:, :, :], patches[bass.ds(it + 1, 1)].rearrange("a p k n -> (a p) k n"))\
                  .then_inc(S["patches_in"], 16)
                store(it)
            store(TURNS - 1)
            sp.wait_ge(S["out_stored"], 16 * (BB + 1) * TURNS + 1)

        @block.gpsimd
        def _(pool):
            setup = Chain(pool, S["pool_setup"])
            pool.wait_ge(S["idx_in"], 16)
            for t in range(NB):
                pool.indirect_dma_start(out=par_sb[:, t, :], out_offset=None, in_=params,
                                        in_offset=bass.IndirectOffsetOnAxis(ap=idx_sb[:, t:t + 1].bitcast(U32), axis=0))\
                    .then_inc(S["par_in"], 16)
            for buf in (kdiag[:, :, :, :], pimg[:, :, :], yTA[:, :], yTB[:, :], x2A[:, :], x2B[:, :]):
                setup.mark(pool.memset(buf, 0.0))
            for buf in (ev[:, :, NQ:NQ + 1], xn[:, :, D:D + 1], xm[:, :, D:D + 1], wfull[:, :, E:ES]):
                setup.mark(pool.memset(buf, 1.0))
            setup.mark(pool.memset(EA[:, 1, :, :], 0.0))
            pool.memset(nt[:, :], 0.0).then_inc(S["consts_ready"], 1)
            pool.wait_ge(S["trig_ready"], 1)

            with pool.Fori(0, TURNS) as it:
                own = Chain(pool, S["pool_own"], it, POOL_CHAIN)

                def co(row, shape):
                    a = trig[:, row, bass.ds(it * BB, BB)]
                    for n in shape:
                        a = a.unsqueeze(1)
                    return a.to_broadcast([P, *shape, BB])

                def bc(ap, shape):
                    for n in shape:
                        ap = ap.unsqueeze(1)
                    return ap.to_broadcast([P, *shape, BB])

                def tt(out_, a, b, op):
                    own.mark(pool.tensor_tensor(out_, a, b, op))

                t6 = slice(0, NQ)
                for c, row in ((0, CP1), (1, SP1)):
                    tt(V1[:, c, :, :], trig[:, S1:S1 + NQ, bass.ds(it * BB, BB)],
                       trig[:, row:row + NQ, bass.ds(it * BB, BB)], ALU.mult)
                own.wait()
                for i in (0, 3):
                    own.mark(pool.tensor_copy(EA[:, 0, i, :], co(C1 + 5, [])))
                    own.mark(pool.memset(EA[:, 1, i, :], 0.0))
                for i in (1, 2):
                    for c in range(2):
                        own.mark(pool.tensor_copy(EA[:, c, i, :], V1[:, c, 5, :]))
                own.wait()
                src, dst, n = EA, EB, 4
                for k in (4, 3, 2):
                    hn = n // 2
                    for c in range(2):
                        o = dst[:, c, 0:2 * n, :].rearrange("p (a r) t -> p a r t", r=hn)[:, 0:4:3]
                        tt(o, src[:, c, 0:n, :].rearrange("p (b r) t -> p b r t", b=2), co(C1 + k, [2, hn]), ALU.mult)
                    for c, x in ((0, X0), (1, X1)):
                        for cc in range(2):
                            tt(x[:, cc, 0:n, :], src[:, cc, 0:n, :], bc(V1[:, c, k, :], [n]), ALU.mult)
                    own.wait()
                    for c, op, other in ((0, ALU.subtract, 1), (1, ALU.add, 0)):
                        for b in range(2):
                            o0 = n if b == 0 else hn
                            tt(dst[:, c, o0:o0 + hn, :], X0[:, c, b * hn:(b + 1) * hn, :],
                               X1[:, other, b * hn:(b + 1) * hn, :], op)
                    own.wait()
                    src, dst, n = dst, src, 2 * n
                c0, c1 = co(C1, []), co(C1 + 1, [])
                v = lambda c, k: V1[:, c, k, :]
                tt(GG[:, 0, 0, :], c0, c1, ALU.mult)
                own.mark(pool.memset(GG[:, 1, 0, :], 0.0))
                for c in range(2):
                    tt(GG[:, c, 1, :], c0, v(c, 1), ALU.mult)
                    tt(GG[:, c, 3, :], c1, v(c, 0), ALU.mult)
                for c in range(2):
                    tt(X0[:, c, 0, :], v(0, 0), v(c, 1), ALU.mult)
                    tt(X1[:, c, 0, :], v(1, 0), v(c, 1), ALU.mult)
                own.wait()
                tt(GG[:, 0, 2, :], X0[:, 0, 0, :], X1[:, 1, 0, :], ALU.subtract)
                tt(GG[:, 1, 2, :], X0[:, 1, 0, :], X1[:, 0, 0, :], ALU.add)
                own.wait()
                for g, x in ((0, X0), (1, X1)):
                    for c in range(2):
                        for b0 in range(2):
                            gg = GG[:, g, 2 * b0:2 * b0 + 2, :].unsqueeze(2).to_broadcast([P, 2, 16, BB])
                            tt(x[:, c, 32 * b0:32 * b0 + 32, :].rearrange("p (a r) t -> p a r t", a=2),
                               src[:, c, 0:32, :].rearrange("p (a r) t -> p a r t", a=2), gg, ALU.mult)
                own.wait()
                for c, op, other in ((0, ALU.subtract, 1), (1, ALU.add, 0)):
                    for p5 in range(2):
                        for b0 in range(2):
                            p0 = b0 ^ p5
                            pick = lambda x, cc, b: x[:, cc, 32 * b + p5:32 * b + 32:2, :]
                            tt(pick(ST, c, p0), pick(X0, c, b0), pick(X1, other, b0), op)
                own.wait()
                for k in range(NQ):
                    flat = lambda x: x[:, :, :, :].rearrange("p c s t -> p (c s) t")
                    tt(flat(X0), flat(ST), co(C2 + k, [2 * NS]), ALU.mult)
                    tt(flat(X1), flat(ST), co(S2 + k, [2 * NS]), ALU.mult)
                    own.wait()
                    half = lambda x, b: x[:, :, :, :].rearrange("p c (l b r) t -> p (c l) b (r t)", l=1 << k, b=2)[:, :, b]
                    tt(half(ST, 0), half(X0, 0), half(X1, 1), ALU.subtract)
                    tt(half(ST, 1), half(X0, 1), half(X1, 0), ALU.add)
                    own.wait()
                for k in range(NQ):
                    L, R = 1 << k, NS >> (k + 1)
                    one = lambda x, c: x[:, c, :, :].rearrange("p (l b r) t -> p l b r t", l=L, b=2)[:, :, 1]
                    for c in range(2):
                        for x, row in ((X0, CP2), (X1, SP2)):
                            o = x[:, c, 0:32, :].rearrange("p (l r) t -> p l r t", l=L)
                            tt(o, one(ST, c), co(row + k, [L, R]), ALU.mult)
                    own.wait()
                    for c, op, other in ((0, ALU.subtract, 1), (1, ALU.add, 0)):
                        tt(one(ST, c), X0[:, c, 0:32, :].rearrange("p (l r) t -> p l r t", l=L),
                           X1[:, other, 0:32, :].rearrange("p (l r) t -> p l r t", l=L), op)
                    own.wait()
                at(pool, "prodT_done", it, RB, 0)
                pt = prods[:, :, :].rearrange("p t n -> p n t")
                stf = ST[:, :, :, :].rearrange("p c s t -> p (c s) t")
                tt(pt[:, 0:2 * NS, :], stf, stf, ALU.mult)
                for k in range(NQ - 1):
                    L, R = 2 << k, NS >> (k + 2)
                    for b in range(2):
                        w = ST[:, :, :, :].rearrange("p c (l q r) t -> p (c l) q r t", l=1 << k, q=4)
                        base = 2 * NS + NS * k
                        o = pt[:, base:base + NS, :].rearrange("p (l q r) t -> p l q r t", l=L, q=2)
                        tt(o[:, :, b], w[:, :, b], w[:, :, 3 - b], ALU.mult)
                for c in range(2):
                    for d in range(2):
                        for b in range(2):
                            w = ST[:, c, :, :].rearrange("p (a b m d) t -> p a b m d t", a=2, b=2, m=8)
                            base = 2 * NS + NS * (NQ - 1) + 32 * c + 16 * d + 8 * b
                            ins = pool.tensor_tensor(pt[:, base:base + 8, :], w[:, 0, b, :, d], w[:, 1, 1 - b, :, 1 - d], ALU.mult)
                            if (c, d, b) == (1, 1, 1):
                                own.wait()
                                ins.then_inc(S["prods_ready"], 1)
                            else:
                                own.mark(ins)
                pool.wait_ge(S["prods_ready"], it + 1)
            assert own.n == POOL_CHAIN, f"POOL_CHAIN = {own.n}"

        @block.scalar
        def _(act):
            setup = Chain(act, S["act_setup"])
            act.wait_ge(S["trig_raw"], 1)
            nc.scalar.activation(trig[:, :, :], trig_k.rearrange("p (a t) -> p a t", t=NB), ACT.Sin, scale=TWO_PI)\
              .then_inc(S["trig_ready"], 1)
            act.wait_ge(S["consts_ready"], 1)

            with act.Fori(0, TURNS) as it:
                own = Chain(act, S["act_own"], it, ACT_CHAIN)

                def copy(dst, src, name):
                    nc.scalar.copy(dst, src).then_inc(S[name], 1)

                at(act, "conv_done", it, 1)
                at(act, "tproj_done", it, 1, 0)
                nc.scalar.activation(tA[:, :], bank[0][:, 0:P], ACT.Identity, bias=conv_bA[:, 0:1]).then_inc(S["t_ready"], 1)
                at(act, "tproj_done", it, 1)
                at(act, "iscore_done", it, 1, 0)
                copy(qT[:, :], bank[2][:, 0:HT * P], "tqkv_ready")
                copy(v_sb[:, :], bank[4][:, 0:D], "tqkv_ready")
                for t in range(HT):
                    at(act, "iprob_sub", it, HT, t + 1)
                    nc.scalar.activation(iprob[:, 4 * t:4 * t + 4, :], iprob[:, 4 * t:4 * t + 4, :], ACT.Exp, scale=HD ** -0.5)\
                      .then_inc(S["iprob_exp"], 1)
                for t in (0, 2):
                    at(act, "iprobT_done", it, HT, t + 1)
                    copy(iprobT[:, 4 * t:4 * t + 4, :], bank[t][:, :].rearrange("p (h q) -> p h q", h=4), "iprobT_ready")
                at(act, "ioT_done", it, 1)
                copy(ioA[:, :], bank[4][:, 0:P], "ioT_ready")
                for r in (0, 2):
                    at(act, "prodT_done", it, RB, r + 1)
                    at(act, "expval_done", it, 1, 0)
                    copy(prodT[:, r, :, :], bank[(1, 2, 5, 6)[r]][:, :].rearrange("p (t n) -> p t n", t=BB), "prodT_ready")
                at(act, "evT_done", it, 1)
                copy(evT[:, :], bank[1][0:NQ + 1, :], "evT_ready")
                ln_root(act, own, it, 0)
                at(act, "xT_done", it, 1)
                copy(xTA[:, :, 0:TXT], bank[0][:, :].rearrange("p (b q) -> p b q", b=BB), "xT_ready")
                copy(xTB[:, :, 0:TXT], bank[3][0:DB + 1, :].rearrange("p (b q) -> p b q", b=BB), "xT_ready")
                at(act, "y_done", it, 1)
                yf = yA[:, :, :].rearrange("p b s -> p (b s)")
                copy(yf[:, 0:320], bank[2][:, 0:320], "y_ready")
                copy(yf[:, 320:640], bank[5][:, 0:320], "y_ready")
                at(act, "nbias_ready", it, 1)
                for t in range(TILES):
                    src = bank[0][:, t * SEQ:(t + 1) * SEQ] if t < 3 else bank[1][:, (t - 3) * SEQ:(t - 2) * SEQ]
                    nc.scalar.activation(prob[:, t, :], src, ACT.Exp, bias=nbias[:, t:t + 1], scale=0.125,
                                         accum_out=asum[:, t:t + 1]).then_inc(S["prob_ready"], 1)
                at(act, "pT_done", it, 1)
                copy(pTA[:, :, 0:TXT], bank[2][:, :].rearrange("p (b q) -> p b q", b=BB), "pT_ready")
                copy(pTA[:, :, TXT:SPAN], bank[3][:, 0:P].rearrange("p (b q) -> p b q", b=BB), "pT_ready")
                at(act, "z_done", it, 1)
                copy(zA[:, 0:BB * TXT], bank[6][:, :], "z_ready")
                copy(zA[:, BB * TXT:FFPAD], bank[7][:, 0:P], "z_ready")
                ln_root(act, own, it, 1)
                at(act, "x2_done", it, 1)
                copy(x2A[:, 0:BB * TXT], bank[0][:, :], "x2_ready")
                copy(x2B[:, 0:BB * TXT], bank[5][0:DB + 1, :], "x2_ready")
                at(act, "lsub_ready", it, 1)
                nc.scalar.activation(lg[:, :, :], lg[:, :, :], ACT.Exp).then_inc(S["lexp_ready"], 1)
                at(act, "wT_done", it, 1)
                copy(wT[:, 0:BB * TXT], bank[2][0:ES, :], "wT_ready")
                for s in range(2 * ES):
                    e = s % ES
                    at(act, "u_done", it, 2 * ES, s + 1)
                    if s >= 2:
                        at(act, "act_ready", it, 2 * ES, s - 1)
                    nc.scalar.activation(sl[:, s % 2, :], bank[s % 2][:, 0:HALF], ACT.Silu, bias=bu_sb[:, e:e + 1])\
                      .then_inc(S["sl_ready"], 1)
            assert own.n == ACT_CHAIN, f"ACT_CHAIN = {own.n}"

        @block.vector
        def _(dve):
            v = nc.vector
            setup = Chain(dve, S["dve_setup"])
            start(dve, "o_ready")
            dve.wait_ge(S["par_in"], 16 * NB)
            pv = par_sb[:, :, :].rearrange("p t (l q k) -> p l k q t", l=3, k=2)
            half, full = 1 / (4 * np.pi), 1 / (2 * np.pi)
            for row, layer, kind, scale, lead in (
                    (C1, 0, 0, half, .25), (S1, 0, 0, half, 0.), (CP1, 0, 1, full, .25), (SP1, 0, 1, full, 0.),
                    (C2, 1, 0, half, .25), (S2, 1, 0, half, 0.), (CP2, 1, 1, full, .25), (SP2, 1, 1, full, 0.),
                    (C3, 2, 0, full, .25), (S3, 2, 0, full, 0.)):
                setup.mark(v.tensor_scalar(trig[:, row:row + NQ, :], pv[:, layer, kind], float(scale), lead, ALU.mult, ALU.add))
            setup.wait()
            tf = trig[:, :, :].rearrange("p a t -> p (a t)")
            setup.link(v.tensor_scalar(trig_k, tf, ROUND, None, ALU.add))
            setup.link(v.tensor_scalar(trig_k, trig_k, ROUND, None, ALU.subtract))
            v.tensor_tensor(trig_k, tf, trig_k, ALU.subtract).then_inc(S["trig_raw"], 1)
            dve.wait_ge(S["mm_big"], 2)
            v.tensor_copy(MA[:, :], bank[0][:, 0:D + 1]).then_inc(S["products_ready"], 1)
            v.tensor_copy(MB[:, :], bank[1][0:DB + 1, 0:D + 1]).then_inc(S["products_ready"], 1)
            dve.wait_ge(S["mm_big"], 4)
            v.tensor_copy(OA[:, :], bank[2][:, 0:D]).then_inc(S["products_ready"], 1)
            setup.link(v.tensor_copy(OB[:, :], bank[3][0:DB + 1, 0:D]))
            v.tensor_tensor(OB[DB:DB + 1, :], OB[DB:DB + 1, :], bo_row[DB:DB + 1, :], ALU.add)\
             .then_inc(S["products_ready"], 1)
            dve.wait_ge(S["loads_tok"], 16 * 14)
            dve.wait_ge(S["loads_ffn"], 16 * 12)
            dve.wait_ge(S["consts_ready"], 1)

            with dve.Fori(0, TURNS) as it:
                own = Chain(dve, S["dve_own"], it, DVE_CHAIN)

                def copy(dst, src, name):
                    v.tensor_copy(dst, src).then_inc(S[name], 1)

                def carry_wait():
                    own.mark(v.memset(spare[:, :], 0.0))

                def layernorm(src, dst, which, name, c):
                    for t in range(TILES):
                        own.mark(v.bn_stats(stats[:, t, :], src[:, t, :]))
                    own.wait()
                    carry_wait()
                    for t in range(TILES):
                        own.mark(v.bn_aggr(mv[:, t, :], stats[:, t, :]))
                    own.wait()
                    v.tensor_scalar(vare[:, :], mv[:, :, 1], EPS, None, ALU.add).then_inc(S["var_ready"], 1)
                    at(dve, "rstd0_ready", it, 2, which + 1)
                    own.link(v.tensor_tensor(nt[:, :], rstd[:, :], rstd[:, :], ALU.mult))
                    own.link(v.tensor_tensor(nt[:, :], nt[:, :], vare[:, :], ALU.mult))
                    own.link(v.tensor_scalar(nt[:, :], nt[:, :], -0.5, 1.5, ALU.mult, ALU.add))
                    own.link(v.tensor_tensor(rstd[:, :], rstd[:, :], nt[:, :], ALU.mult))
                    for t in range(TILES):
                        v.tensor_scalar(dst[:, t, 0:D], src[:, t, :], mv[:, t, 0:1], rstd[:, t:t + 1],
                                        ALU.subtract, ALU.mult).then_inc(S[name], 1)

                at(dve, "conv_done", it, 1)
                v.tensor_scalar(tB[0:DB, :], bank[1][0:DB, 0:P], conv_bB[:, 0:1], None, ALU.add).then_inc(S["t_ready"], 1)
                at(dve, "tproj_done", it, 1)
                for j in range(4):
                    v.tensor_copy(kdiag[32 * j:32 * j + 32, :, j, :],
                                  bank[3][32 * j:32 * j + 32, 0:HT * P].rearrange("p (t k) -> p t k", t=HT))\
                     .then_inc(S["tqkv_ready"], 1)
                at(dve, "iscore_done", it, 1)
                for t in range(HT):
                    own.mark(v.tensor_reduce(imax[:, 4 * t:4 * t + 4], bank[5 + t][:, :].rearrange("p (h k) -> p h k", h=4),
                                             AX.X, ALU.max))
                own.wait()
                for t in range(HT):
                    v.tensor_tensor(iprob[:, 4 * t:4 * t + 4, :], bank[5 + t][:, :].rearrange("p (h k) -> p h k", h=4),
                                    imax[:, 4 * t:4 * t + 4].unsqueeze(2).to_broadcast([P, 4, P]), ALU.subtract)\
                     .then_inc(S["iprob_sub"], 1)
                at(dve, "iprob_exp", it, HT)
                own.link(v.tensor_reduce(isum[:, :], iprob[:, :, :], AX.X, ALU.add))
                own.mark(v.reciprocal(irec[:, :], isum[:, :]))
                at(dve, "iprobT_done", it, HT, 2)
                copy(iprobT[:, 4:8, :], bank[1][:, :].rearrange("p (h q) -> p h q", h=4), "iprobT_ready")
                at(dve, "ipv_done", it, 1)
                own.wait()
                v.tensor_tensor(io[:, :].rearrange("p (h d) -> p h d", h=HEADS),
                                bank[3][:, 0:D].rearrange("p (h d) -> p h d", h=HEADS),
                                irec[:, :].unsqueeze(2).to_broadcast([P, HEADS, HD]), ALU.mult).then_inc(S["io_ready"], 1)
                at(dve, "ioT_done", it, 1)
                copy(ioB[0:DB, :], bank[1][0:DB, 0:P], "ioT_ready")
                for r in (1, 3):
                    at(dve, "prodT_done", it, RB, r + 1)
                    copy(prodT[:, r, :, :], bank[(1, 2, 5, 6)[r]][:, :].rearrange("p (t n) -> p t n", t=BB), "prodT_ready")
                at(dve, "iout_done", it, 1)
                copy(h[:, BB, :], bank[0][:, 0:D], "h_ready")
                at(dve, "expval_done", it, 1)
                zx = bank[7][:, 0:BB * 2 * NQ].rearrange("p (t c q) -> p c t q", t=BB, c=2)
                for c, row in ((0, C3), (1, S3)):
                    own.mark(v.tensor_tensor(evt[:, c], zx[:, c],
                                             trig[:, row:row + NQ, bass.ds(it * BB, BB)].rearrange("p q t -> p t q"), ALU.mult))
                own.wait()
                v.tensor_tensor(ev[:, :, 0:NQ], evt[:, 0], evt[:, 1], ALU.subtract).then_inc(S["ev_ready"], 1)
                at(dve, "emb_done", it, 1)
                for i, b in ((0, 2), (1, 5)):
                    copy(h[:, 2 * i:2 * i + 2, :], bank[b][:, 0:2 * D].rearrange("p (t d) -> p t d", t=2), "h_ready")
                dve.wait_ge(S["h_ready"], it * 3 + 3)
                layernorm(h, xn, 0, "xn_ready", 0)
                at(dve, "xT_done", it, 1)
                copy(xTA[:, :, TXT:SPAN], bank[1][:, 0:P].rearrange("p (b q) -> p b q", b=BB), "xT_ready")
                copy(xTB[:, :, TXT:SPAN], bank[4][0:DB + 1, 0:P].rearrange("p (b q) -> p b q", b=BB), "xT_ready")
                at(dve, "y_done", it, 1)
                yf = yB[:, :, :].rearrange("p b s -> p (b s)")
                copy(yf[:, 0:320], bank[6][0:DB + 1, 0:320], "y_ready")
                copy(yf[:, 320:640], bank[7][0:DB + 1, 0:320], "y_ready")
                at(dve, "ascore_done", it, 1)
                own.mark(v.tensor_reduce(nmax[:, 0:3], bank[0][:, 0:3 * SEQ].rearrange("p (t k) -> p t k", t=3),
                                         AX.X, ALU.max, negate=True))
                own.link(v.tensor_reduce(nmax[:, 3:5], bank[1][:, 0:2 * SEQ].rearrange("p (t k) -> p t k", t=2),
                                         AX.X, ALU.max, negate=True))
                v.tensor_scalar(nbias[:, :], nmax[:, :], 0.125, None, ALU.mult).then_inc(S["nbias_ready"], 1)
                for b in range(BB):
                    at(dve, "prob_ready", it, TILES, b + 1)
                    v.tensor_copy(pimg[:, b, b * SLOT:b * SLOT + IMG], prob[:, b, TXT:SEQ]).then_inc(S["pimg_ready"], 1)
                at(dve, "prob_ready", it, TILES)
                for b in range(BB):
                    rows = slice(b * SLOT, (b + 1) * SLOT)
                    v.tensor_copy(pimg[rows, BB, b * SLOT:b * SLOT + IMG], prob[rows, BB, TXT:SEQ]).then_inc(S["pimg_ready"], 1)
                own.mark(v.reciprocal(arec[:, :], asum[:, :]))
                at(dve, "pT_done", it, 1)
                copy(pTB[:, :, 0:TXT], bank[4][:, :].rearrange("p (b q) -> p b q", b=BB), "pT_ready")
                copy(pTB[:, :, TXT:SPAN], bank[5][:, 0:P].rearrange("p (b q) -> p b q", b=BB), "pT_ready")
                at(dve, "z_done", it, 1)
                copy(zB[:, 0:BB * TXT], bank[0][0:DB + 1, :], "z_ready")
                copy(zB[:, BB * TXT:FFPAD], bank[1][0:DB + 1, 0:P], "z_ready")
                at(dve, "aout_done", it, 1)
                own.wait()
                for t in range(TILES):
                    b, c = ((2, 0), (2, D), (3, 0), (3, D), (4, 0))[t]
                    v.scalar_tensor_tensor(out=h2[:, t, :], in0=bank[b][:, c:c + D], scalar=arec[:, t:t + 1],
                                           in1=h[:, t, :], op0=ALU.mult, op1=ALU.add).then_inc(S["h2_ready"], 1)
                at(dve, "h2_ready", it, TILES)
                layernorm(h2, xm, 1, "xm_ready", 0)
                at(dve, "x2_done", it, 1)
                for dst, b, rows in ((x2A, 1, P), (x2B, 6, DB + 1)):
                    v.tensor_copy(dst[:, BB * TXT:FF].rearrange("p (b q) -> p b q", b=BB),
                                  bank[b][0:rows, 0:P].rearrange("p (b q) -> p b q", b=BB)[:, :, 0:IMG])\
                     .then_inc(S["x2_ready"], 1)
                at(dve, "gate_done", it, 1)
                lp = bank[7][:, 0:TILES * E].rearrange("p (t e) -> p t e", t=TILES)
                own.link(v.tensor_reduce(lmax[:, :], lp, AX.X, ALU.max))
                v.tensor_tensor(lg[:, :, :], lp, lmax[:, :].unsqueeze(2).to_broadcast([P, TILES, E]), ALU.subtract)\
                 .then_inc(S["lsub_ready"], 1)
                at(dve, "lexp_ready", it, 1)
                own.link(v.tensor_reduce(lsum[:, :], lg[:, :, :], AX.X, ALU.add))
                own.link(v.reciprocal(lsum[:, :], lsum[:, :]))
                own.link(v.tensor_tensor(score[:, :, :], lg[:, :, :], lsum[:, :].unsqueeze(2).to_broadcast([P, TILES, E]), ALU.mult))
                own.link(v.tensor_tensor(sbias[:, :, :], score[:, :, :],
                                         bias_sb[:, :].unsqueeze(1).to_broadcast([P, TILES, E]), ALU.add))

                def top4(vals, n):
                    carry_wait()
                    for t in range(TILES):
                        own.mark(v.max(top8[:, t, :], vals[:, t, 0:n]))
                    own.wait()
                    fourth = top8[:, :, 3:4].to_broadcast([P, TILES, n])
                    own.mark(v.tensor_tensor(cmp_g[:, :, 0:n], vals[:, :, 0:n], fourth, ALU.is_gt))
                    own.mark(v.tensor_tensor(cmp_e[:, :, 0:n], vals[:, :, 0:n], fourth, ALU.is_equal))
                    own.wait()
                    own.mark(v.tensor_reduce(ngt[:, :], cmp_g[:, :, 0:n], AX.X, ALU.add))
                    src, dst, step = cmp_e, scan_a, 1
                    while step < n:
                        own.mark(v.tensor_copy(dst[:, :, 0:step], src[:, :, 0:step]))
                        own.mark(v.tensor_tensor(dst[:, :, step:n], src[:, :, step:n], src[:, :, 0:n - step], ALU.add))
                        own.wait()
                        src, dst, step = dst, (scan_b if dst is scan_a else scan_a), step * 2
                    own.link(v.tensor_tensor(dst[:, :, 0:n], src[:, :, 0:n], ngt[:, :].unsqueeze(2).to_broadcast([P, TILES, n]), ALU.add))
                    own.link(v.tensor_scalar(dst[:, :, 0:n], dst[:, :, 0:n], 4.0, None, ALU.is_le))
                    own.link(v.tensor_tensor(dst[:, :, 0:n], dst[:, :, 0:n], cmp_e[:, :, 0:n], ALU.mult))
                    own.link(v.tensor_tensor(keep[:, :, 0:n], dst[:, :, 0:n], cmp_g[:, :, 0:n], ALU.add))

                sp2 = sbias[:, :, :].rearrange("p t (g i) -> p t g i", i=2)
                own.link(v.tensor_tensor(gsum[:, :, :], sp2[:, :, :, 0], sp2[:, :, :, 1], ALU.add))
                top4(gsum, G)
                kept = keep[:, :, 0:G].unsqueeze(3).to_broadcast([P, TILES, G, 2])
                own.mark(v.tensor_tensor(sp2, sp2, kept, ALU.mult))
                own.link(v.tensor_scalar(scan_b[:, :, 0:G], keep[:, :, 0:G], BIG, -BIG, ALU.mult, ALU.add))
                own.link(v.tensor_tensor(sp2, sp2, scan_b[:, :, 0:G].unsqueeze(3).to_broadcast([P, TILES, G, 2]), ALU.add))
                top4(sbias, E)
                own.link(v.tensor_tensor(score[:, :, :], score[:, :, :], keep[:, :, :], ALU.mult))
                v.tensor_scalar(wfull[:, :, 0:E], score[:, :, :], 2.5, None, ALU.mult).then_inc(S["wfull_ready"], 1)
                at(dve, "wT_done", it, 1)
                copy(wT[:, BB * TXT:FFPAD], bank[3][0:ES, 0:P], "wT_ready")
                for s in range(2 * ES):
                    e, hf = s % ES, s // ES
                    at(dve, "g_done", it, 2 * ES, s + 1)
                    at(dve, "sl_ready", it, 2 * ES, s + 1)
                    own.link(v.scalar_tensor_tensor(out=gated[:, s % 2, :], in0=bank[2 + s % 2][:, 0:HALF], scalar=bg_sb[:, e:e + 1],
                                                    in1=sl[:, s % 2, :], op0=ALU.add, op1=ALU.mult))
                    at(dve, "w_done", it, 2 * ES, s + 1)
                    if s >= 2:
                        at(dve, "down_done", it, 2 * ES, s - 1)
                    v.tensor_tensor(act_w[:, s % 2, :], gated[:, s % 2, :], bank[4 + s % 2][:, 0:HALF], ALU.mult)\
                     .then_inc(S["act_ready"], 1)
                    if e == ES - 1:
                        at(dve, "down_done", it, 2 * ES, s + 1)
                        for dst, b, rows in ((yTA, 6, P), (yTB, 7, DB)):
                            if hf == 0:
                                copy(dst[:, 0:HALF], bank[b][0:rows, 0:HALF], "ycols_ready")
                            else:
                                nt_ = BB * TXT - HALF
                                copy(dst[:, HALF:BB * TXT], bank[b][0:rows, 0:nt_], "ycols_ready")
                                copy(dst[:, BB * TXT:FFPAD].rearrange("p (b q) -> p b q", b=BB)[:, :, 0:IMG],
                                     bank[b][0:rows, nt_:HALF].rearrange("p (b q) -> p b q", b=BB), "ycols_ready")
                at(dve, "fin_done", it, 1)
                at(dve, "out_stored", it, 16 * (BB + 1), 0)
                for i in range(3):
                    n = 2 if i < 2 else 1
                    v.tensor_tensor(o_sb[:, 2 * i:2 * i + n, :], bank[i][:, 0:n * D].rearrange("p (t d) -> p t d", t=n),
                                    h2[:, 2 * i:2 * i + n, :], ALU.add).then_inc(S["o_ready"], 1)
            assert own.n == DVE_CHAIN, f"DVE_CHAIN = {own.n}"

        @block.tensor
        def _(pe):
            mm = nc.tensor.matmul

            def tr(dst, src, n):
                return nc.tensor.transpose(dst, src, ident[0:n, 0:n])

            start(pe, "tproj_done", "iscore_done", "prodT_done", "expval_done")
            for first, w1, last_rows in ((0, D + 1, 2), (2, D, 3)):
                pe.wait_ge(S["loads_big"], 48 if first == 0 else 80)
                l = wbig[0].rearrange("p (k n) -> p k n", k=KQ)
                r = wbig[1][:, 0:KQ * w1].rearrange("p (k n) -> p k n", k=KQ)
                for i, (a, b) in enumerate(((0, P), (P, D + 1))):
                    for k in range(KQ):
                        ins = mm(bank[first + i][0:b - a, 0:w1], l[:, k, a:b], r[:, k, :], start=(k == 0), stop=(k == KQ - 1))
                    ins.then_inc(S["mm_big"], 1)
            pe.wait_ge(S["products_ready"], 4)
            pe.wait_ge(S["loads_tok"], 16 * 14)
            pe.wait_ge(S["loads_txt"], 32)
            pe.wait_ge(S["loads_ffn"], 16 * 12)
            pe.wait_ge(S["consts_ready"], 1)

            with pe.Fori(0, TURNS) as it:
                at(pe, "patches_in", it, 16)
                at(pe, "o_ready", it, 3, 0)
                for b, lo, hi in ((0, 0, P), (1, P, D)):
                    for k in range(KP):
                        ins = mm(bank[b][0:hi - lo, 0:P], conv_sb[:, k, lo:hi], patch_sb[:, k, :], start=(k == 0), stop=(k == KP - 1))
                ins.then_inc(S["conv_done"], 1)
                at(pe, "t_ready", it, 2)
                for b, wa, wb in ((2, wqA, wqB), (3, wkA, wkB)):
                    for t in range(HT):
                        cols = slice(t * P, (t + 1) * P)
                        mm(bank[b][:, cols], wa[:, cols], tA[:, :], start=True, stop=False)
                        mm(bank[b][:, cols], wb[:, cols], tB[:, :], start=False, stop=True)
                mm(bank[4][:, 0:D], tA[:, :], wvA[:, :], start=True, stop=False)
                mm(bank[4][:, 0:D], tB[0:DB + 1, :], wvB[:, :], start=False, stop=True).then_inc(S["tproj_done"], 1)
                at(pe, "tqkv_ready", it, 6)
                for t in range(HT):
                    ins = mm(bank[5 + t][:, :], qT[:, t * P:(t + 1) * P], kdiag[:, t, :, :].rearrange("p h k -> p (h k)"),
                             start=True, stop=True)
                ins.then_inc(S["iscore_done"], 1)
                for t in range(HT):
                    at(pe, "iprob_exp", it, HT, t + 1)
                    for j in range(4):
                        ins = tr(bank[t][:, j * P:(j + 1) * P], iprob[:, 4 * t + j, :], P)
                    ins.then_inc(S["iprobT_done"], 1)
                at(pe, "iprobT_ready", it, HT)
                for hd in range(HEADS):
                    c = slice(hd * HD, (hd + 1) * HD)
                    ins = mm(bank[3][:, c], iprobT[:, hd, :], v_sb[:, c], start=True, stop=True)
                ins.then_inc(S["ipv_done"], 1)
                at(pe, "io_ready", it, 1)
                tr(bank[4][:, 0:P], io[:, 0:P], P)
                tr(bank[1][0:DB, 0:P], io[:, P:D], P).then_inc(S["ioT_done"], 1)
                at(pe, "ioT_ready", it, 2)
                mm(bank[0][:, 0:D], ioA[:, :], woA[:, :], start=True, stop=False)
                mm(bank[0][:, 0:D], ioB[:, :], woB[:, :], start=False, stop=True).then_inc(S["iout_done"], 1)
                at(pe, "prods_ready", it, 1)
                for r in range(RB):
                    for t in range(BB):
                        ins = tr(bank[(1, 2, 5, 6)[r]][:, t * P:(t + 1) * P], prods[:, t, r * P:(r + 1) * P], P)
                    ins.then_inc(S["prodT_done"], 1)
                at(pe, "prodT_ready", it, RB)
                for t in range(BB):
                    for r in range(RB):
                        ins = mm(bank[7][:, t * 2 * NQ:(t + 1) * 2 * NQ], prodT[:, r, t, :], red_sb[:, r, :],
                                 start=(r == 0), stop=(r == RB - 1))
                ins.then_inc(S["expval_done"], 1)
                at(pe, "ev_ready", it, 1)
                for t in range(BB):
                    ins = tr(bank[1][0:NQ + 1, t * P:(t + 1) * P], ev[:, t, :], P)
                ins.then_inc(S["evT_done"], 1)
                at(pe, "evT_ready", it, 1)
                for t in range(BB):
                    ins = mm(bank[(2, 5)[t // 2]][:, (t % 2) * D:(t % 2 + 1) * D], evT[:, t * P:(t + 1) * P], pw_sb[:, :],
                             start=True, stop=True)
                ins.then_inc(S["emb_done"], 1)
                at(pe, "h_ready", it, 3)
                at(pe, "xn_ready", it, TILES)
                for t in range(TILES):
                    a, b, c = (0, 3, t * P) if t < BB else (1, 4, 0)
                    tr(bank[a][:, c:c + P], xn[:, t, 0:P], P)
                    ins = tr(bank[b][0:DB + 1, c:c + P], xn[:, t, P:D + 1], P)
                ins.then_inc(S["xT_done"], 1)
                at(pe, "xT_ready", it, 4)
                xaf, xbf = (x[:, :, :].rearrange("p b s -> p (b s)") for x in (xTA, xTB))
                for lo, hi, banks in ((0, P, (2, 5)), (P, D + 1, (6, 7))):
                    for i in range(2):
                        c = slice(320 * i, 320 * i + 320)
                        mm(bank[banks[i]][0:hi - lo, 0:320], MA[:, lo:hi], xaf[:, c], start=True, stop=False)
                        ins = mm(bank[banks[i]][0:hi - lo, 0:320], MB[:, lo:hi], xbf[:, c], start=False, stop=True)
                ins.then_inc(S["y_done"], 1)
                at(pe, "y_ready", it, 4)
                for b in range(BB):
                    o = bank[0][:, b * SEQ:(b + 1) * SEQ] if b < 3 else bank[1][:, 0:SEQ]
                    mm(o, yA[:, b, 0:TXT], xTA[:, b, 0:SEQ], start=True, stop=False)
                    mm(o, yB[:, b, 0:TXT], xTB[:, b, 0:SEQ], start=False, stop=True)
                for b in range(BB):
                    o = bank[1][b * SLOT:(b + 1) * SLOT, SEQ:2 * SEQ]
                    mm(o, yA[:, b, TXT:SPAN], xTA[:, b, 0:SEQ], start=True, stop=False, tile_position=(0, b * SLOT))
                    ins = mm(o, yB[:, b, TXT:SPAN], xTB[:, b, 0:SEQ], start=False, stop=True, tile_position=(0, b * SLOT))
                ins.then_inc(S["ascore_done"], 1)
                at(pe, "prob_ready", it, TILES)
                for t in range(TILES):
                    a, c = (2, t * P) if t < BB else (3, 0)
                    tr(bank[a][:, c:c + P], prob[:, t, 0:TXT], P)
                at(pe, "pimg_ready", it, 2 * BB)
                for t in range(TILES):
                    a, c = (4, t * P) if t < BB else (5, 0)
                    ins = tr(bank[a][:, c:c + P], pimg[:, t, :], P)
                ins.then_inc(S["pT_done"], 1)
                at(pe, "pT_ready", it, 4)
                for lo, hi, banks in ((0, P, (6, 7)), (P, D + 1, (0, 1))):
                    for b in range(BB):
                        for bk, c, q0, q1 in ((banks[0], b * TXT, 0, TXT), (banks[1], b * SLOT, TXT, SPAN)):
                            o = bank[bk][0:hi - lo, c:c + q1 - q0]
                            mm(o, xn[:, b, lo:hi], pTA[:, b, q0:q1], start=True, stop=False)
                            ins = mm(o, xn[:, BB, lo:hi], pTB[:, b, q0:q1], start=False, stop=True)
                ins.then_inc(S["z_done"], 1)
                at(pe, "z_ready", it, 4)
                for t in range(TILES):
                    b, c = ((2, 0), (2, D), (3, 0), (3, D), (4, 0))[t]
                    q = slice(t * P, (t + 1) * P)
                    mm(bank[b][:, c:c + D], zA[:, q], OA[:, :], start=True, stop=False)
                    ins = mm(bank[b][:, c:c + D], zB[:, q], OB[:, :], start=False, stop=True)
                ins.then_inc(S["aout_done"], 1)
                at(pe, "xm_ready", it, TILES)
                for t in range(TILES):
                    a, b, c = (0, 5, t * P) if t < BB else (1, 6, 0)
                    tr(bank[a][:, c:c + P], xm[:, t, 0:P], P)
                    ins = tr(bank[b][0:DB + 1, c:c + P], xm[:, t, P:D + 1], P)
                ins.then_inc(S["x2_done"], 1)
                at(pe, "x2_ready", it, 4)
                for t in range(TILES):
                    c = slice(t * P, (t + 1) * P)
                    mm(bank[7][:, t * E:(t + 1) * E], x2A[:, c], gwA[:, :], start=True, stop=False)
                    ins = mm(bank[7][:, t * E:(t + 1) * E], x2B[:, c], gwB[:, :], start=False, stop=True)
                ins.then_inc(S["gate_done"], 1)
                at(pe, "wfull_ready", it, 1)
                for t in range(TILES):
                    a, c = (2, t * P) if t < BB else (3, 0)
                    ins = tr(bank[a][0:ES, c:c + P], wfull[:, t, :], P)
                ins.then_inc(S["wT_done"], 1)
                at(pe, "wT_ready", it, 2)

                def down(s):
                    e, hf = s % ES, s // ES
                    cols = slice(hf * HALF, (hf + 1) * HALF)
                    at(pe, "act_ready", it, 2 * ES, s + 1)
                    for b, lo, hi in ((6, 0, P), (7, P, D)):
                        if e == 0:
                            if hf == 1:
                                at(pe, "ycols_ready", it, 6, 2)
                            mm(bank[b][0:hi - lo, 0:HALF], bd_sb[:, lo:hi], wT[:, cols], start=True, stop=False)
                        ins = mm(bank[b][0:hi - lo, 0:HALF], wd_sb[:, e * D + lo:e * D + hi], act_w[:, s % 2, :],
                                 start=False, stop=(e == ES - 1))
                    ins.then_inc(S["down_done"], 1)

                for s in range(2 * ES):
                    e, hf = s % ES, s // ES
                    cols, ec = slice(hf * HALF, (hf + 1) * HALF), slice(e * HID, (e + 1) * HID)
                    if s >= 2:
                        at(pe, "sl_ready", it, 2 * ES, s - 1)
                        at(pe, "act_ready", it, 2 * ES, s - 1)
                    for b, wa, wb, name in ((s % 2, wuA, wuB, "u_done"), (2 + s % 2, wgA, wgB, "g_done")):
                        mm(bank[b][:, 0:HALF], wa[:, ec], x2A[:, cols], start=True, stop=False)
                        mm(bank[b][:, 0:HALF], wb[:, ec], x2B[0:DB, cols], start=False, stop=True).then_inc(S[name], 1)
                    mm(bank[4 + s % 2][:, 0:HALF], sel_sb[:, e * P:(e + 1) * P], wT[:, cols], start=True, stop=True)\
                        .then_inc(S["w_done"], 1)
                    if s >= 1:
                        down(s - 1)
                down(2 * ES - 1)
                at(pe, "ycols_ready", it, 6)
                for t in range(TILES):
                    b, c = t // 2, (t % 2) * D
                    tr(bank[b][:, c:c + P], yTA[:, t * P:(t + 1) * P], P)
                    ins = tr(bank[b][:, c + P:c + D], yTB[:, t * P:(t + 1) * P], DB)
                ins.then_inc(S["fin_done"], 1)


def reduction_matrix():
    basis = np.arange(NS)
    out = np.zeros((NPROD, 2 * NQ), np.float32)
    for q in range(NQ):
        bits = range(1, NQ) if q == 0 else range(q + 1)
        parity = sum((basis >> (NQ - 1 - b)) & 1 for b in bits) % 2
        out[:2 * NS, q] = np.tile(1.0 - 2.0 * parity, 2)
        out[2 * NS + NS * q:2 * NS + NS * (q + 1), NQ + q] = 2.0
    return out


_ORDER = ["patches", "tokens", "conv_w", "conv_b", "wq", "wk", "wv", "wo", "tok_const", "params", "post_w",
          "wq_big", "wk_big", "wv_big", "wout_big", "bout_big", "gate_w", "bias", "wu", "bu", "wg", "bg", "wd", "bd",
          "reduce_w", "sel_e", "ident_in"]


def kernel(**inputs):
    import concourse.bacc as _bacc
    from concourse.bass_utils import run_bass_kernel_spmd as _run

    a = {k: np.asarray(v) for k, v in inputs.items()}
    f = np.float32

    def stack(w, b):
        return np.concatenate([w, b[None]], 0)

    x = a["x"][:, :, :80, :80].reshape(NB, 3, 5, 16, 5, 16).transpose(1, 3, 5, 0, 2, 4).reshape(PIX, NB, IMG)
    pad = np.zeros((PIX, NB, SLOT), f)
    pad[:, :, :IMG] = x
    patches = np.ascontiguousarray(pad.reshape(KP, P, TURNS, BB * SLOT).transpose(2, 1, 0, 3))

    def heads(w, b, extra_row):
        full = stack(w.T, b).reshape(D + 1, HEADS, HD)
        out = np.zeros((D + 1 + 2 * BB, HEADS, 32), f)
        out[:D + 1, :, :HD] = full
        for i in range(BB):
            out[D + 1 + extra_row + i, :, HD + i] = 1.0
        return out.reshape(D + 1 + 2 * BB, HT * P)

    tok_const = np.zeros((1 + 2 * BB, P), f)
    tok_const[0] = 1.0
    tok_const[1 + BB:] = -1e30
    for i in range(BB):
        tok_const[1 + i, i * SLOT:(i + 1) * SLOT] = 1.0
        tok_const[1 + BB + i, i * SLOT:i * SLOT + IMG] = 0.0

    def rows(w, n):
        return np.ascontiguousarray(w.reshape(n, P, -1).transpose(1, 0, 2).reshape(P, -1))

    qkv, bqkv = a["L0_attn_w_qkv"], a["L0_attn_b_qkv"]
    big = [rows(stack(qkv[:, i * QK:(i + 1) * QK], bqkv[i * QK:(i + 1) * QK]).T, KQ) for i in range(3)]

    def experts(w, shared):
        return np.concatenate([w, shared[None]], 0)

    wu, wg, wd = (experts(a[f"L0_ffn_W{n}"], a[f"L0_ffn_sW{n}"]) for n in "ugd")
    bu, bg, bd = (experts(a[f"L0_ffn_b{n}"], a[f"L0_ffn_sb{n}"]) for n in "ugd")
    sel = np.zeros((ES, ES, P), f)
    for e in range(ES):
        sel[e, e] = 1.0
    arrays = {
        "patches": patches,
        "tokens": np.ascontiguousarray(a["x_txt"].T),
        "conv_w": rows(a["L0_tok_conv_w"].reshape(D, PIX).T, KP).reshape(P, KP, D),
        "conv_b": a["L0_tok_conv_b"].reshape(D, 1),
        "wq": heads(a["L0_tok_wq"], a["L0_tok_bq"], 0),
        "wk": heads(a["L0_tok_wk"], a["L0_tok_bk"], BB),
        "wv": stack(a["L0_tok_wv"].T, a["L0_tok_bv"]),
        "wo": stack(a["L0_tok_wo"].T, a["L0_tok_bo"]),
        "tok_const": tok_const,
        "params": a["L0_txt_quantum_params"].reshape(-1, 36),
        "post_w": stack(a["L0_txt_post_w"].T, a["L0_txt_post_b"]),
        "wq_big": big[0], "wk_big": big[1], "wv_big": big[2],
        "wout_big": rows(a["L0_attn_w_out"], KQ),
        "bout_big": a["L0_attn_b_out"].reshape(1, D),
        "gate_w": stack(a["L0_ffn_gate_w"], a["L0_ffn_gate_b"]),
        "bias": a["L0_ffn_bias"],
        "wu": wu.transpose(1, 0, 2).reshape(D, ES * HID), "bu": bu.T,
        "wg": wg.transpose(1, 0, 2).reshape(D, ES * HID), "bg": bg.T,
        "wd": wd.transpose(1, 0, 2).reshape(HID, ES * D), "bd": bd,
        "reduce_w": reduction_matrix().reshape(RB, P, 2 * NQ).transpose(1, 0, 2),
        "sel_e": sel.reshape(ES, ES * P),
        "ident_in": np.eye(P, dtype=f),
    }
    nc = _bacc.Bacc("TRN2", target_bir_lowering=False, num_devices=1)
    feed, args = {}, []
    for name in _ORDER:
        arr = np.ascontiguousarray(arrays[name])
        feed[f"in_{name}_dram"] = arr
        args.append(nc.dram_tensor(f"in_{name}_dram", arr.shape, mybir.dt.from_np(arr.dtype), kind="ExternalInput").ap())
    args.append(nc.dram_tensor("out_0_dram", (NB, SEQ, D), F32, kind="ExternalOutput").ap())
    early_fusion(nc, *args)
    r = _run(nc, [feed], core_ids=[0])
    return r.results[0]["out_0_dram"]
```

```python
from contextlib import ExitStack

import numpy as np
import concourse.bass as bass
from concourse import mybir

F32 = mybir.dt.float32
F32R = mybir.dt.float32r
I32 = mybir.dt.int32
U32 = mybir.dt.uint32
ALU = mybir.AluOpType
ACT = mybir.ActivationFunctionType
AX = mybir.AxisListType

P = 128
NB = 32
BB = 4
TURNS = NB // BB
TXT = 128
IMG = 25
SLOT = 32
SEQ = TXT + IMG
SPAN = TXT + SLOT
TILES = BB + 1
D = 192
DB = D - P
PIX = 768
KP = PIX // P
HEADS, HD = 12, 16
HT = HEADS // 4
QK = 768
KQ = QK // P
E, HID = 16, 128
ES = E + 1
G = 8
NQ = 6
NS = 1 << NQ
FF = BB * SEQ
HALF = FF // 2
FFPAD = TILES * P
NPROD = 512
RB = NPROD // P
WR = SLOT + ES
SLOTS = 2 * ES
TWO_PI = 6.283185
ROUND = 12582912.0
BIG = 3.0e38
EPS = 1e-5

C1, S1, CP1, SP1, C2, S2, CP2, SP2, C3, S3 = [NQ * i for i in range(10)]
NTRIG = NQ * 10

DVE_FRONT_CHAIN = 94
ACT_FRONT_CHAIN = 2
POOL_CHAIN = 146


class Chain:

    def __init__(self, eng, sem, turn=None, per=0, name=""):
        self.eng, self.sem, self.turn, self.per, self.n, self.name = eng, sem, turn, per, 0, name

    def mark(self, ins):
        self.n += 1
        ins.then_inc(self.sem, 1)

    def wait(self):
        base = 0 if self.turn is None else self.turn * self.per
        self.eng.wait_ge(self.sem, base + self.n)

    def link(self, ins):
        self.mark(ins)
        self.wait()


def early_fusion(nc, patches, tokens, conv_w, conv_b, wq, wk, wv, wo, tok_const, params, post_w,
                 wq_big, wk_big, wv_big, wout_big, bout_big, gate_w, bias, wuA_in, wuB_in, bu,
                 wgA_in, wgB_in, bg, wd, bd, reduce_w, ident_in, out):
    ctx = ExitStack()
    with ctx:
        def sb(name, shape, dt=F32):
            return ctx.enter_context(nc.sbuf_tensor(name, shape, dt))

        def sem(name):
            return ctx.enter_context(nc.semaphore(name))

        bank = [ctx.enter_context(nc.psum_tensor(f"bank{i}", [P, 512], F32)) for i in range(8)]
        UP, GATE, WEIGHT, YA, YB = bank[0:5]
        b5, b6, b7 = bank[5:8]

        ident = sb("ident", [P, P])
        ident2 = sb("ident2", [P, DB])
        conv_sb = sb("conv_sb", [P, KP, D])
        conv_bA = sb("conv_bA", [P, 1])
        conv_bB = sb("conv_bB", [DB, 1])
        KB = DB + 1 + 2 * BB
        wqA, wqB = sb("wqA", [P, HT * P]), sb("wqB", [KB, HT * P])
        wkA, wkB = sb("wkA", [P, HT * P]), sb("wkB", [KB, HT * P])
        wvA, wvB = sb("wvA", [P, D]), sb("wvB", [DB + 1, D])
        woA, woB = sb("woA", [P, D]), sb("woB", [DB + 1, D])
        pw_sb = sb("pw_sb", [NQ + 1, D])
        red_sb = sb("red_sb", [P, RB, 2 * NQ])
        gwA, gwB = sb("gwA", [P, E]), sb("gwB", [DB + 1, E])
        bias_sb = sb("bias_sb", [P, E])
        sel = sb("sel", [WR, ES + 1], F32R)
        wu_h, wu_l, wu_b = (sb(f"wu_{x}", [P, ES, HID], F32R) for x in "hlb")
        wg_h, wg_l, wg_b = (sb(f"wg_{x}", [P, ES, HID], F32R) for x in "hlb")
        wd_h, wd_l, wd_b = (sb(f"wd_{x}", [HID, ES, P], F32R) for x in "hlb")
        bd_h, bd_l, bd_b = (sb(f"bd_{x}", [WR, P], F32R) for x in "hlb")
        bu_sb, bg_sb = sb("bu_sb", [HID, ES]), sb("bg_sb", [HID, ES])
        MA, MB = sb("MA", [P, D + 1]), sb("MB", [DB + 1, D + 1])
        OA, OB = sb("OA", [P, D]), sb("OB", [DB + 1, D])
        idx_sb = sb("idx_sb", [P, NB], I32)
        trig = sb("trig", [P, NTRIG, NB])
        V1 = sb("V1", [P, 2, NQ, BB])
        GG = sb("GG", [P, 2, 4, BB])
        X0 = sb("X0", [P, 2, NS, BB])
        X1 = sb("X1", [P, 2, NS, BB])
        ST = sb("ST", [P, 2, NS, BB])
        EA, EB = (ST[:, i, :, :].rearrange("p (c s) t -> p c s t", c=2) for i in range(2))
        prods = sb("prods", [P, BB, NPROD])
        yz_all = [sb("yzA", [P, FFPAD]), sb("yzB", [P, FFPAD])]
        yz = [yz_all[0][:, :], yz_all[1][0:DB + 1, :]]
        qT, v_sb = yz_all[0][:, 0:HT * P], yz_all[0][:, HT * P:HT * P + D]
        ioA, io = yz_all[1][:, 0:P], yz_all[1][:, P:P + D]
        patch_sb = sb("patch_sb", [P, KP, P])
        tA, tB = sb("tA", [P, P]), sb("tB", [KB, P])
        kdiag = sb("kdiag", [P, HT, 4, P])
        imax = sb("imax", [P, HEADS])
        isum = sb("isum", [P, HEADS])
        irec = sb("irec", [P, HEADS])
        ioB = sb("ioB", [DB + 1, P])
        prodT = sb("prodT", [P, RB, BB, P])
        prodT_flat = prodT[:, :, :, :].rearrange("p r t n -> p (r t n)")
        iprobT = prodT_flat[:, 0:HEADS * P].rearrange("p (h n) -> p h n", h=HEADS)
        iprob_t = sb("iprob", [P, HEADS, P])
        iprob = iprob_t[:, :, :]
        iprob_flat = iprob.rearrange("p h n -> p (h n)")
        pTA, pTB = (iprob_flat[:, i * FFPAD:(i + 1) * FFPAD].rearrange("p (b s) -> p b s", b=BB) for i in range(2))
        evt = sb("evt", [P, 2, BB, NQ])
        ev = sb("ev", [P, BB, NQ + 1])
        h = sb("h", [P, TILES, D])
        stats = sb("stats", [P, TILES, 6])
        mv = sb("mv", [P, TILES, 2])
        vare = sb("vare", [P, TILES])
        lnv = sb("lnv", [P, TILES])
        rstd = sb("rstd", [P, TILES])
        nt = sb("nt", [P, TILES])
        xn = sb("xn", [P, TILES, D + 1])
        xTA, xTB = sb("xTA", [P, BB, SPAN]), sb("xTB", [DB + 1, BB, SPAN])
        x2A, x2B = (x[:, :, :].rearrange("p b s -> p (b s)") for x in (xTA, xTB))
        zA, zB = yz
        yA, yB = (x.rearrange("p (b s) -> p b s", b=BB) for x in yz)
        evT = yz[0][0:NQ + 1, 0:BB * P]
        nmax = sb("nmax", [P, TILES])
        nbias = sb("nbias", [P, TILES])
        asum = sb("asum", [P, TILES])
        arec = sb("arec", [P, TILES])
        prob = prodT_flat[:, 0:TILES * SEQ].rearrange("p (t k) -> p t k", t=TILES)
        pimg = sb("pimg", [P, TILES, P])
        h2 = [sb(f"h2_{i}", [P, TILES, D]) for i in range(2)]
        lmax = sb("lmax", [P, TILES])
        lg = sb("lg", [P, TILES, E])
        lsum = sb("lsum", [P, TILES])
        score = sb("score", [P, TILES, E])
        sbias = sb("sbias", [P, TILES, E])
        gsum = sb("gsum", [P, TILES, G])
        top8 = sb("top8", [P, TILES, 8])
        cmp_g = sb("cmp_g", [P, TILES, E])
        cmp_e = sb("cmp_e", [P, TILES, E])
        scan_a = sb("scan_a", [P, TILES, E])
        scan_b = sb("scan_b", [P, TILES, E])
        ngt = sb("ngt", [P, TILES])
        keep = sb("keep", [P, TILES, E])
        wfull = sb("wfull", [P, TILES, ES])
        wtok = sb("wtok", [P, TILES, WR], F32R)

        def halves(name, rows):
            first, even, odd = (sb(f"{name}_{x}", [rows, HALF], F32R) for x in ("first", "even", "odd"))
            return [[first, even], [first, odd]]

        x_h, x_l = halves("x_h", P), halves("x_l", P)
        xb_h, xb_l = halves("xb_h", P), halves("xb_l", DB)
        w_hl = halves("w_hl", WR)
        sl = sb("sl", [HID, HALF])
        gated = sb("gated", [HID, HALF])
        act_w = sb("act_w", [HID, HALF])
        a_h = sb("a_h", [HID, 2, HALF], F32R)
        a_l = sb("a_l", [HID, 2, HALF], F32R)
        yT = sb("yT", [P, 2 * FFPAD])
        yTA, yTB = yT[:, 0:FFPAD], yT[:, FFPAD:2 * FFPAD]
        o_sb = yT[:, 0:TILES * D].rearrange("p (t d) -> p t d", t=TILES)
        spare = sb("spare", [P, 1])

        par_sb = iprob_flat[:, 0:NB * 36].rearrange("p (t k) -> p t k", t=NB)
        trig_k = prodT_flat[:, 0:NTRIG * NB]
        wbig = [kdiag[:, :, :, :].rearrange("p t h k -> p (t h k)")[:, 0:KQ * (D + 1)],
                yT[:, 0:KQ * (D + 1)]]
        bo_row = h[0:DB + 1, 0, :]
        bd_raw = io[0:WR, :]
        prods_flat = prods[:, :, :].rearrange("p t n -> p (t n)")
        stage = [prods_flat[:, i * 1024:(i + 1) * 1024] for i in range(2)]

        names = """loads_tok loads_txt loads_big loads_ffn idx_in par_in consts_ready products_ready mm_big
            stage0_in stage1_in stage_high stage_free weights_ready
            trig_ready trig_raw patches_in conv_done tA_ready tB_ready tproj_done qv_ready kdiag_ready
            iscore_done iprob_sub iprob_exp iprobT_done iprobT_act iprobT_dve ipv_done io_ready ioT_done ioA_ready ioB_ready
            iout_done prods_ready prodT_done prodT_act prodT_dve expval_done ev_ready evT_done evT_ready emb_done h_ready
            var_ready rstd0_ready xn_ready xT_done xT_act xT_dve y_done y_act y_dve ascore_done nbias_ready prob_ready
            pimg_ready pT_done pT_act pT_dve z_done z_act z_dve aout_done h2_ready x2_done x2_act x2_dve
            gate_done lsub_ready lexp_ready high_ready split_ready wtok_ready wT_done w_ready
            u_done g_done w_done sl_ready gated_ready act_ready a_high_ready a_low_ready down_done ya_ready yb_ready
            fin_done o_ready out_stored dve_own dve_setup pool_own pool_setup act_own act_setup""".split()
        S = {n: sem(n) for n in names}

        def at(eng, name, turn, per, n=None):
            count = turn * per + (per if n is None else n) + (name == "prodT_done")
            if not (isinstance(count, int) and count <= 0):
                eng.wait_ge(S[name], count)

        def ln_root(act, own, turn, which):
            at(act, "var_ready", turn, 2, which + 1)
            own.link(nc.scalar.activation(lnv[:, :], vare[:, :], ACT.Ln))
            nc.scalar.activation(rstd[:, :], lnv[:, :], ACT.Exp, scale=-0.5).then_inc(S["rstd0_ready"], 1)

        def turns(eng, experts, front, chain):
            own = chain(0)
            for s in range(SLOTS):
                front(s, 0, 0, own, False)
            assert own is None or own.n == own.per, f"{own.name} = {own.n}"

            def beside(turn, parity, first):
                own = chain(turn + 1)
                for s in range(SLOTS):
                    front(s, turn + 1, 1 - parity, own, not first)
                    experts(s, turn, parity, first)
                experts(SLOTS, turn, parity, first)

            beside(0, 0, True)
            with eng.Fori(0, (TURNS - 2) // 2) as pair:
                beside(pair * 2 + 1, 1, False)
                beside(pair * 2 + 2, 0, False)
            for s in range(SLOTS + 1):
                experts(s, TURNS - 1, 1, False)

        block = ctx.enter_context(nc.Block())

        def chunks(width):
            step = 1024 // width
            return [(e, min(ES, e + step)) for e in range(0, ES, step)]

        UG_CHUNKS, WD_CHUNKS = chunks(HID), chunks(D)
        staged = [(kind, e0, e1) for kind in ("uA", "gA", "uB", "gB") for e0, e1 in UG_CHUNKS] \
            + [("d", e0, e1) for e0, e1 in WD_CHUNKS]

        @block.sync
        def _(sp):
            def load(dst, src, name):
                sp.dma_start(dst, src).then_inc(S[name], 16)

            load(idx_sb[:, :], tokens, "idx_in")
            load(wbig[0], wq_big, "loads_big")
            load(wbig[1], wk_big, "loads_big")
            load(bo_row[DB:DB + 1, :], bout_big, "loads_big")
            load(ident[:, :], ident_in, "loads_ffn")
            load(bd_raw, bd, "loads_ffn")
            load(conv_sb[:, :, :], conv_w, "loads_tok")
            load(patch_sb[:, :, :], patches[0], "patches_in")
            load(conv_bA[:, :], conv_b[0:P, :], "loads_tok")
            load(conv_bB[:, :], conv_b[P:D, :], "loads_tok")
            for w, a, b in ((wq, wqA, wqB), (wk, wkA, wkB), (wv, wvA, wvB), (wo, woA, woB)):
                load(a[:, :], w[0:P, :], "loads_tok")
                load(b[:, :], w[P:w.shape[0], :], "loads_tok")
            load(tB[DB:KB, :], tok_const, "loads_tok")
            load(ioB[DB:DB + 1, :], tok_const[0:1, :], "loads_tok")
            load(pw_sb[:, :], post_w, "loads_txt")
            load(red_sb[:, :, :], reduce_w, "loads_txt")
            load(gwA[:, :], gate_w[0:P, :], "loads_txt")
            load(gwB[:, :], gate_w[P:D + 1, :], "loads_txt")
            load(bias_sb[:, :], bias.partition_broadcast(P), "loads_txt")
            load(bu_sb[:, :], bu, "loads_txt")
            load(bg_sb[:, :], bg, "loads_txt")
            sp.wait_ge(S["mm_big"], 2)
            load(wbig[0], wv_big, "loads_big")
            load(wbig[1][:, 0:KQ * D], wout_big, "loads_big")
            for i, (kind, e0, e1) in enumerate(staged):
                if i >= 2:
                    sp.wait_ge(S["stage_free"], i - 1)
                src, width = {"uA": (wuA_in, HID), "gA": (wgA_in, HID), "uB": (wuB_in, HID), "gB": (wgB_in, HID),
                              "d": (wd, D)}[kind]
                load(stage[i % 2][:, 0:(e1 - e0) * width], src[:, e0 * width:e1 * width], f"stage{i % 2}_in")

            def load_patches(t):
                at(sp, "conv_done", t - 1, 1)
                src = patches[t] if isinstance(t, int) else patches[bass.ds(t, 1)].rearrange("a p k n -> (a p) k n")
                sp.dma_start(patch_sb[:, :, :], src).then_inc(S["patches_in"], 16)

            def store(it):
                at(sp, "o_ready", it, 3)
                sp.dma_start(out[bass.ds(it * BB, BB), IMG:SEQ, :].rearrange("b s d -> s b d"),
                             o_sb[:, 0:BB, :]).then_inc(S["out_stored"], 16)
                for j in range(BB):
                    sp.dma_start(out[bass.ds(it * BB + j, 1), 0:IMG, :].rearrange("b s d -> (b s) d"),
                                 o_sb[j * SLOT:j * SLOT + IMG, BB, :]).then_inc(S["out_stored"], 16)

            load_patches(1)
            with sp.Fori(0, TURNS - 2) as it:
                load_patches(it + 2)
                store(it)
            store(TURNS - 2)
            store(TURNS - 1)
            sp.wait_ge(S["out_stored"], 16 * (BB + 1) * TURNS)

        @block.gpsimd
        def _(pool):
            pool.wait_ge(S["idx_in"], 16)
            for t in range(NB):
                pool.indirect_dma_start(out=par_sb[:, t, :], out_offset=None, in_=params,
                                        in_offset=bass.IndirectOffsetOnAxis(ap=idx_sb[:, t:t + 1].bitcast(U32), axis=0))\
                    .then_inc(S["par_in"], 16)
            for buf in (pimg[:, :, :], wtok[:, :, :].bitcast(F32)):
                pool.memset(buf, 0.0).then_inc(S["pool_setup"], 1)
            for buf in (ev[:, :, NQ:NQ + 1], xn[:, :, D:D + 1], wfull[:, :, E:ES]):
                pool.memset(buf, 1.0).then_inc(S["pool_setup"], 1)
            pool.wait_ge(S["mm_big"], 4)
            pool.memset(kdiag[:, :, :, :], 0.0).then_inc(S["pool_setup"], 1)
            pool.memset(yT[:, :], 0.0).then_inc(S["consts_ready"], 1)
            pool.wait_ge(S["trig_ready"], 1)

            with pool.Fori(0, TURNS) as it:
                own = Chain(pool, S["pool_own"], it, POOL_CHAIN)

                def co(row, shape):
                    a = trig[:, row, bass.ds(it * BB, BB)]
                    for n in shape:
                        a = a.unsqueeze(1)
                    return a.to_broadcast([P, *shape, BB])

                def bc(ap, shape):
                    for n in shape:
                        ap = ap.unsqueeze(1)
                    return ap.to_broadcast([P, *shape, BB])

                def tt(out_, a, b, op):
                    own.mark(pool.tensor_tensor(out_, a, b, op))

                t6 = slice(0, NQ)
                for c, row in ((0, CP1), (1, SP1)):
                    tt(V1[:, c, :, :], trig[:, S1:S1 + NQ, bass.ds(it * BB, BB)],
                       trig[:, row:row + NQ, bass.ds(it * BB, BB)], ALU.mult)
                own.wait()
                for i in (0, 3):
                    own.mark(pool.tensor_copy(EA[:, 0, i, :], co(C1 + 5, [])))
                    own.mark(pool.memset(EA[:, 1, i, :], 0.0))
                for i in (1, 2):
                    for c in range(2):
                        own.mark(pool.tensor_copy(EA[:, c, i, :], V1[:, c, 5, :]))
                own.wait()
                src, dst, n = EA, EB, 4
                for k in (4, 3, 2):
                    hn = n // 2
                    for c in range(2):
                        o = dst[:, c, 0:2 * n, :].rearrange("p (a r) t -> p a r t", r=hn)[:, 0:4:3]
                        tt(o, src[:, c, 0:n, :].rearrange("p (b r) t -> p b r t", b=2), co(C1 + k, [2, hn]), ALU.mult)
                    for c, x in ((0, X0), (1, X1)):
                        for cc in range(2):
                            tt(x[:, cc, 0:n, :], src[:, cc, 0:n, :], bc(V1[:, c, k, :], [n]), ALU.mult)
                    own.wait()
                    for c, op, other in ((0, ALU.subtract, 1), (1, ALU.add, 0)):
                        for b in range(2):
                            o0 = n if b == 0 else hn
                            tt(dst[:, c, o0:o0 + hn, :], X0[:, c, b * hn:(b + 1) * hn, :],
                               X1[:, other, b * hn:(b + 1) * hn, :], op)
                    own.wait()
                    src, dst, n = dst, src, 2 * n
                c0, c1 = co(C1, []), co(C1 + 1, [])
                v = lambda c, k: V1[:, c, k, :]
                tt(GG[:, 0, 0, :], c0, c1, ALU.mult)
                own.mark(pool.memset(GG[:, 1, 0, :], 0.0))
                for c in range(2):
                    tt(GG[:, c, 1, :], c0, v(c, 1), ALU.mult)
                    tt(GG[:, c, 3, :], c1, v(c, 0), ALU.mult)
                for c in range(2):
                    tt(X0[:, c, 0, :], v(0, 0), v(c, 1), ALU.mult)
                    tt(X1[:, c, 0, :], v(1, 0), v(c, 1), ALU.mult)
                own.wait()
                tt(GG[:, 0, 2, :], X0[:, 0, 0, :], X1[:, 1, 0, :], ALU.subtract)
                tt(GG[:, 1, 2, :], X0[:, 1, 0, :], X1[:, 0, 0, :], ALU.add)
                own.wait()
                for g, x in ((0, X0), (1, X1)):
                    for c in range(2):
                        for b0 in range(2):
                            gg = GG[:, g, 2 * b0:2 * b0 + 2, :].unsqueeze(2).to_broadcast([P, 2, 16, BB])
                            tt(x[:, c, 32 * b0:32 * b0 + 32, :].rearrange("p (a r) t -> p a r t", a=2),
                               src[:, c, 0:32, :].rearrange("p (a r) t -> p a r t", a=2), gg, ALU.mult)
                own.wait()
                for c, op, other in ((0, ALU.subtract, 1), (1, ALU.add, 0)):
                    for p5 in range(2):
                        for b0 in range(2):
                            p0 = b0 ^ p5
                            pick = lambda x, cc, b: x[:, cc, 32 * b + p5:32 * b + 32:2, :]
                            tt(pick(ST, c, p0), pick(X0, c, b0), pick(X1, other, b0), op)
                own.wait()
                for k in range(NQ):
                    flat = lambda x: x[:, :, :, :].rearrange("p c s t -> p (c s) t")
                    tt(flat(X0), flat(ST), co(C2 + k, [2 * NS]), ALU.mult)
                    tt(flat(X1), flat(ST), co(S2 + k, [2 * NS]), ALU.mult)
                    own.wait()
                    half = lambda x, b: x[:, :, :, :].rearrange("p c (l b r) t -> p (c l) b (r t)", l=1 << k, b=2)[:, :, b]
                    tt(half(ST, 0), half(X0, 0), half(X1, 1), ALU.subtract)
                    tt(half(ST, 1), half(X0, 1), half(X1, 0), ALU.add)
                    own.wait()
                for k in range(NQ):
                    L, R = 1 << k, NS >> (k + 1)
                    one = lambda x, c: x[:, c, :, :].rearrange("p (l b r) t -> p l b r t", l=L, b=2)[:, :, 1]
                    for c in range(2):
                        for x, row in ((X0, CP2), (X1, SP2)):
                            o = x[:, c, 0:32, :].rearrange("p (l r) t -> p l r t", l=L)
                            tt(o, one(ST, c), co(row + k, [L, R]), ALU.mult)
                    own.wait()
                    for c, op, other in ((0, ALU.subtract, 1), (1, ALU.add, 0)):
                        tt(one(ST, c), X0[:, c, 0:32, :].rearrange("p (l r) t -> p l r t", l=L),
                           X1[:, other, 0:32, :].rearrange("p (l r) t -> p l r t", l=L), op)
                    own.wait()
                at(pool, "prodT_done", it, RB, 0)
                pt = prods[:, :, :].rearrange("p t n -> p n t")
                stf = ST[:, :, :, :].rearrange("p c s t -> p (c s) t")
                tt(pt[:, 0:2 * NS, :], stf, stf, ALU.mult)
                for k in range(NQ - 1):
                    L, R = 2 << k, NS >> (k + 2)
                    for b in range(2):
                        w = ST[:, :, :, :].rearrange("p c (l q r) t -> p (c l) q r t", l=1 << k, q=4)
                        base = 2 * NS + NS * k
                        o = pt[:, base:base + NS, :].rearrange("p (l q r) t -> p l q r t", l=L, q=2)
                        tt(o[:, :, b], w[:, :, b], w[:, :, 3 - b], ALU.mult)
                for c in range(2):
                    for d in range(2):
                        for b in range(2):
                            w = ST[:, c, :, :].rearrange("p (a b m d) t -> p a b m d t", a=2, b=2, m=8)
                            base = 2 * NS + NS * (NQ - 1) + 32 * c + 16 * d + 8 * b
                            ins = pool.tensor_tensor(pt[:, base:base + 8, :], w[:, 0, b, :, d], w[:, 1, 1 - b, :, 1 - d], ALU.mult)
                            if (c, d, b) == (1, 1, 1):
                                own.wait()
                                ins.then_inc(S["prods_ready"], 1)
                            else:
                                own.mark(ins)
                pool.wait_ge(S["prods_ready"], it + 1)
            assert own.n == POOL_CHAIN, f"POOL_CHAIN = {own.n}"

        @block.scalar
        def _(act):
            def copy(dst, src, name):
                nc.scalar.copy(dst, src).then_inc(S[name], 1)

            act.wait_ge(S["loads_ffn"], 32)
            for dst, a, b in ((bd_h[:, :], 0, P), (bd_l[:, :], 0, P), (bd_b[:, 0:DB], P, D), (bd_b[:, DB:P], P, D)):
                copy(dst, bd_raw[:, a:b], "stage_high")
            for i, (kind, e0, e1) in enumerate(staged):
                act.wait_ge(S[f"stage{i % 2}_in"], 16 * (i // 2 + 1))
                raw = stage[i % 2]
                if kind == "d":
                    r = raw[:, 0:(e1 - e0) * D].rearrange("p (e d) -> p e d", d=D)
                    copy(wd_h[:, e0:e1, :], r[:, :, 0:P], "stage_high")
                    copy(wd_b[:, e0:e1, 0:DB], r[:, :, P:D], "stage_high")
                else:
                    dst = {"uA": wu_h, "gA": wg_h, "uB": wu_b, "gB": wg_b}[kind]
                    r = raw[:, 0:(e1 - e0) * HID].rearrange("p (e d) -> p e d", d=HID)
                    copy(dst[:, e0:e1, :], r, "stage_high")
                if i == 2:
                    act.wait_ge(S["trig_raw"], 1)
                    nc.scalar.activation(trig[:, :, :], trig_k.rearrange("p (a t) -> p a t", t=NB), ACT.Sin, scale=TWO_PI)\
                      .then_inc(S["trig_ready"], 1)
            act.wait_ge(S["loads_tok"], 16 * 13)
            act.wait_ge(S["loads_txt"], 16 * 7)
            act.wait_ge(S["consts_ready"], 1)

            def front(s, turn, par, own, busy):
                if s == 0:
                    at(act, "conv_done", turn, 1)
                    nc.scalar.activation(tA[:, :], b5[:, 0:P], ACT.Identity, bias=conv_bA[:, 0:1]).then_inc(S["tA_ready"], 1)
                if s == 1:
                    at(act, "tproj_done", turn, 1)
                    copy(qT[:, :], b5[:, 0:HT * P], "qv_ready")
                    copy(v_sb[:, :], b7[:, 0:D], "qv_ready")
                if s == 4:
                    for t in range(HT):
                        at(act, "iprob_sub", turn, HT, t + 1)
                        nc.scalar.activation(iprob[:, 4 * t:4 * t + 4, :], iprob[:, 4 * t:4 * t + 4, :], ACT.Exp, scale=HD ** -0.5)\
                          .then_inc(S["iprob_exp"], 1)
                if s == 5:
                    at(act, "iprobT_done", turn, 1)
                    for t, b in ((0, b5), (2, b7)):
                        copy(iprobT[:, 4 * t:4 * t + 4, :], b[:, :].rearrange("p (h q) -> p h q", h=4), "iprobT_act")
                if s == 7:
                    at(act, "ioT_done", turn, 1)
                    copy(ioA[:, :], b5[:, 0:P], "ioA_ready")
                if s in (7, 8):
                    r = 0 if s == 7 else 2
                    at(act, "prodT_done", turn, RB, r + 1)
                    copy(prodT[:, r, :, :], b7[:, :].rearrange("p (t n) -> p t n", t=BB), "prodT_act")
                if s == 11:
                    at(act, "evT_done", turn, 1)
                    copy(evT, b5[0:NQ + 1, :], "evT_ready")
                if s == 14:
                    ln_root(act, own, turn, 0)
                if s == 15:
                    at(act, "xT_done", turn, 1)
                    copy(xTA[:, :, 0:TXT], b5[:, :].rearrange("p (b q) -> p b q", b=BB), "xT_act")
                    copy(xTB[:, :, 0:TXT], b7[0:DB + 1, :].rearrange("p (b q) -> p b q", b=BB), "xT_act")
                if s == 16:
                    at(act, "y_done", turn, 2, 1)
                    copy(yz[0][:, 0:320], b5[:, 0:320], "y_act")
                    copy(yz[0][:, 320:640], b6[:, 0:320], "y_act")
                if s == 17:
                    at(act, "y_done", turn, 2, 2)
                    copy(yz[1][:, 320:640], b5[0:DB + 1, 0:320], "y_act")
                if s == 19:
                    at(act, "nbias_ready", turn, 1)
                    for t in range(TILES):
                        src = b6[:, t * SEQ:(t + 1) * SEQ] if t < 3 else b7[:, (t - 3) * SEQ:(t - 2) * SEQ]
                        nc.scalar.activation(prob[:, t, :], src, ACT.Exp, bias=nbias[:, t:t + 1], scale=0.125,
                                             accum_out=asum[:, t:t + 1]).then_inc(S["prob_ready"], 1)
                if s == 20:
                    at(act, "pT_done", turn, 1)
                    copy(pTA[:, :, 0:TXT], b5[:, :].rearrange("p (b q) -> p b q", b=BB), "pT_act")
                    copy(pTA[:, :, TXT:SPAN], b7[:, 0:P].rearrange("p (b q) -> p b q", b=BB), "pT_act")
                    copy(pTB[:, :, TXT:SPAN], b7[:, P:2 * P].rearrange("p (b q) -> p b q", b=BB), "pT_act")
                if s == 21:
                    at(act, "z_done", turn, 1)
                    copy(zA[:, 0:BB * TXT], b5[:, :], "z_act")
                    copy(zB[:, 0:BB * TXT], b7[0:DB + 1, :], "z_act")
                if s == 24:
                    ln_root(act, own, turn, 1)
                if s == 25:
                    at(act, "x2_done", turn, 1)
                    copy(x2A[:, 0:BB * TXT], b5[:, :], "x2_act")
                    copy(x2B[:, 0:BB * TXT], b7[0:DB + 1, :], "x2_act")
                if s == 27:
                    at(act, "lsub_ready", turn, 1)
                    nc.scalar.activation(lg[:, :, :], lg[:, :, :], ACT.Exp).then_inc(S["lexp_ready"], 1)
                if s in (26, 27):
                    if s == 26:
                        at(act, "x2_act", turn, 2)
                        at(act, "x2_dve", turn, 2)
                    hf = s - 26
                    c = slice(hf * HALF, (hf + 1) * HALF)
                    copy(x_h[par][hf][:, :], x2A[:, c], "high_ready")
                    copy(xb_h[par][hf][0:DB, :], x2B[0:DB, c], "high_ready")
                    copy(xb_h[par][hf][DB:P, :], x2B[0:DB, c], "high_ready")
                if s == 30:
                    at(act, "wT_done", turn, 1)
                    k = BB * TXT - HALF
                    copy(w_hl[par][0][:, :], b5[0:WR, 0:HALF], "w_ready")
                    copy(w_hl[par][1][:, 0:k], b5[0:WR, HALF:BB * TXT], "w_ready")
                    copy(w_hl[par][1][:, k:HALF], b6[0:WR, 0:HALF - k], "w_ready")

            def experts(s, turn, par, first):
                if s in (1, ES + 1) and not (s == 1 and first):
                    half_out(s != 1, turn, first)
                if s == SLOTS:
                    return
                e = s % ES
                at(act, "u_done", turn, SLOTS, s + 1)
                at(act, "gated_ready", turn, SLOTS, s)
                nc.scalar.activation(sl[:, :], UP[:, 0:HALF], ACT.Silu, bias=bu_sb[:, e:e + 1]).then_inc(S["sl_ready"], 1)
                at(act, "act_ready", turn, SLOTS, s + 1)
                at(act, "down_done", turn, SLOTS, s - 1)
                copy(a_h[:, s % 2, :], act_w[:, :], "a_high_ready")

            def half_out(is_first_half, turn, first):
                if is_first_half:
                    at(act, "down_done", turn, SLOTS, ES)
                    if not first:
                        at(act, "out_stored", turn, 16 * (BB + 1), 0)
                    copy(yTA[:, 0:HALF], YA[:, 0:HALF], "ya_ready")
                else:
                    at(act, "down_done", turn, SLOTS, 0)
                    k = BB * TXT - HALF
                    copy(yTA[:, HALF:BB * TXT], YA[:, 0:k], "ya_ready")
                    copy(yTA[:, BB * TXT:FFPAD].rearrange("p (b q) -> p b q", b=BB)[:, :, 0:IMG],
                         YA[:, k:HALF].rearrange("p (b q) -> p b q", b=BB), "ya_ready")

            turns(act, experts, front, lambda turn: Chain(act, S["act_own"], turn, ACT_FRONT_CHAIN, "ACT_FRONT_CHAIN"))
            half_out(False, TURNS, False)

        @block.vector
        def _(dve):
            v = nc.vector
            setup = Chain(dve, S["dve_setup"])
            dve.wait_ge(S["loads_ffn"], 32)
            setup.mark(v.tensor_tensor(ident2[:, :], ident[:, 0:DB], ident[:, DB:P], ALU.add))
            setup.mark(v.tensor_tensor(sel[:, 0:ES], ident[0:WR, 0:ES], ident[0:WR, WR - ES:WR], ALU.add))
            dve.wait_ge(S["stage_high"], 4)
            for dst, a, b in ((bd_l[:, :], 0, P), (bd_b[:, DB:P], P, D)):
                setup.mark(v.tensor_tensor(dst, bd_raw[:, a:b], dst.bitcast(F32), ALU.subtract))
            highs = 4

            def low_parts(i, kind, e0, e1):
                raw = stage[i % 2]
                dve.wait_ge(S["stage_high"], highs)
                if kind == "d":
                    r = raw[:, 0:(e1 - e0) * D].rearrange("p (e d) -> p e d", d=D)
                    setup.mark(v.tensor_tensor(wd_l[:, e0:e1, :], r[:, :, 0:P], wd_h[:, e0:e1, :].bitcast(F32), ALU.subtract))
                    v.tensor_tensor(wd_b[:, e0:e1, DB:P], r[:, :, P:D], wd_b[:, e0:e1, 0:DB].bitcast(F32), ALU.subtract)\
                     .then_inc(S["stage_free"], 1)
                    return
                r = raw[:, 0:(e1 - e0) * HID].rearrange("p (e d) -> p e d", d=HID)
                if kind in ("uA", "gA"):
                    hi, lo = (wu_h, wu_l) if kind == "uA" else (wg_h, wg_l)
                    v.tensor_tensor(lo[:, e0:e1, :], r, hi[:, e0:e1, :].bitcast(F32), ALU.subtract).then_inc(S["stage_free"], 1)
                else:
                    low = (wu_b if kind == "uB" else wg_b)[DB:P, e0:e1, :]
                    v.tensor_tensor(low, r[DB:P], low.bitcast(F32), ALU.subtract).then_inc(S["stage_free"], 1)

            dve.wait_ge(S["mm_big"], 2)
            v.tensor_copy(MA[:, :], bank[0][:, 0:D + 1]).then_inc(S["products_ready"], 1)
            v.tensor_copy(MB[:, :], bank[1][0:DB + 1, 0:D + 1]).then_inc(S["products_ready"], 1)
            dve.wait_ge(S["mm_big"], 4)
            v.tensor_copy(OA[:, :], bank[2][:, 0:D]).then_inc(S["products_ready"], 1)
            setup.link(v.tensor_copy(OB[:, :], bank[3][0:DB + 1, 0:D]))
            v.tensor_tensor(OB[DB:DB + 1, :], OB[DB:DB + 1, :], bo_row[DB:DB + 1, :], ALU.add)\
             .then_inc(S["products_ready"], 1)
            for i, (kind, e0, e1) in enumerate(staged):
                if i == 2:
                    dve.wait_ge(S["par_in"], 16 * NB)
                    pv = par_sb.rearrange("p t (l q k) -> p l k q t", l=3, k=2)
                    half, full = 1 / (4 * np.pi), 1 / (2 * np.pi)
                    for row, layer, kd, scale, lead in (
                            (C1, 0, 0, half, .25), (S1, 0, 0, half, 0.), (CP1, 0, 1, full, .25), (SP1, 0, 1, full, 0.),
                            (C2, 1, 0, half, .25), (S2, 1, 0, half, 0.), (CP2, 1, 1, full, .25), (SP2, 1, 1, full, 0.),
                            (C3, 2, 0, full, .25), (S3, 2, 0, full, 0.)):
                        setup.mark(v.tensor_scalar(trig[:, row:row + NQ, :], pv[:, layer, kd], float(scale), lead, ALU.mult, ALU.add))
                    setup.wait()
                    tf = trig[:, :, :].rearrange("p a t -> p (a t)")
                    setup.link(v.tensor_scalar(trig_k, tf, ROUND, None, ALU.add))
                    setup.link(v.tensor_scalar(trig_k, trig_k, ROUND, None, ALU.subtract))
                    v.tensor_tensor(trig_k, tf, trig_k, ALU.subtract).then_inc(S["trig_raw"], 1)
                highs += 2 if kind == "d" else 1
                low_parts(i, kind, e0, e1)
            dve.wait_ge(S["stage_free"], len(staged))
            setup.wait()
            v.memset(spare[:, :], 0.0).then_inc(S["weights_ready"], 1)
            dve.wait_ge(S["loads_tok"], 16 * 13)
            dve.wait_ge(S["loads_txt"], 16 * 7)
            dve.wait_ge(S["consts_ready"], 1)

            def copy(dst, src, name):
                v.tensor_copy(dst, src).then_inc(S[name], 1)

            def carry_wait(own):
                own.mark(v.memset(spare[:, :], 0.0))

            def ln_stats(src, own):
                for t in range(TILES):
                    own.mark(v.bn_stats(stats[:, t, :], src[:, t, :]))
                own.wait()
                carry_wait(own)
                for t in range(TILES):
                    own.mark(v.bn_aggr(mv[:, t, :], stats[:, t, :]))
                own.wait()
                v.tensor_scalar(vare[:, :], mv[:, :, 1], EPS, None, ALU.add).then_inc(S["var_ready"], 1)

            def ln_rows(src, turn, which, own):
                at(dve, "rstd0_ready", turn, 2, which + 1)
                own.link(v.tensor_tensor(nt[:, :], rstd[:, :], rstd[:, :], ALU.mult))
                own.link(v.tensor_tensor(nt[:, :], nt[:, :], vare[:, :], ALU.mult))
                own.link(v.tensor_scalar(nt[:, :], nt[:, :], -0.5, 1.5, ALU.mult, ALU.add))
                own.link(v.tensor_tensor(rstd[:, :], rstd[:, :], nt[:, :], ALU.mult))
                for t in range(TILES):
                    v.tensor_scalar(xn[:, t, 0:D], src[:, t, :], mv[:, t, 0:1], rstd[:, t:t + 1],
                                    ALU.subtract, ALU.mult).then_inc(S["xn_ready"], 1)

            def top4(vals, n, own):
                carry_wait(own)
                for t in range(TILES):
                    own.mark(v.max(top8[:, t, :], vals[:, t, 0:n]))
                own.wait()
                fourth = top8[:, :, 3:4].to_broadcast([P, TILES, n])
                own.mark(v.tensor_tensor(cmp_g[:, :, 0:n], vals[:, :, 0:n], fourth, ALU.is_gt))
                own.mark(v.tensor_tensor(cmp_e[:, :, 0:n], vals[:, :, 0:n], fourth, ALU.is_equal))
                own.wait()
                own.mark(v.tensor_reduce(ngt[:, :], cmp_g[:, :, 0:n], AX.X, ALU.add))
                src, dst, step = cmp_e, scan_a, 1
                while step < n:
                    own.mark(v.tensor_copy(dst[:, :, 0:step], src[:, :, 0:step]))
                    own.mark(v.tensor_tensor(dst[:, :, step:n], src[:, :, step:n], src[:, :, 0:n - step], ALU.add))
                    own.wait()
                    src, dst, step = dst, (scan_b if dst is scan_a else scan_a), step * 2
                own.link(v.tensor_tensor(dst[:, :, 0:n], src[:, :, 0:n], ngt[:, :].unsqueeze(2).to_broadcast([P, TILES, n]), ALU.add))
                own.link(v.tensor_scalar(dst[:, :, 0:n], dst[:, :, 0:n], 4.0, None, ALU.is_le))
                own.link(v.tensor_tensor(dst[:, :, 0:n], dst[:, :, 0:n], cmp_e[:, :, 0:n], ALU.mult))
                own.link(v.tensor_tensor(keep[:, :, 0:n], dst[:, :, 0:n], cmp_g[:, :, 0:n], ALU.add))

            heads4 = lambda b: b[:, :].rearrange("p (h k) -> p h k", h=4)
            four = lambda t: slice(4 * t, 4 * t + 4)

            def front(s, turn, par, own, busy):
                if s == 0:
                    at(dve, "conv_done", turn, 1)
                    v.tensor_scalar(tB[0:DB, :], b6[0:DB, 0:P], conv_bB[:, 0:1], None, ALU.add).then_inc(S["tB_ready"], 1)
                if s == 1:
                    at(dve, "tproj_done", turn, 1)
                    for j in range(4):
                        v.tensor_copy(kdiag[32 * j:32 * j + 32, :, j, :],
                                      b6[32 * j:32 * j + 32, 0:HT * P].rearrange("p (t k) -> p t k", t=HT))\
                         .then_inc(S["kdiag_ready"], 1)
                if s == 2:
                    at(dve, "iscore_done", turn, 1)
                    for t, b in enumerate((b5, b6, b7)):
                        own.mark(v.tensor_reduce(imax[:, four(t)], heads4(b), AX.X, ALU.max))
                if s == 3:
                    own.wait()
                    for t, b in enumerate((b5, b6, b7)):
                        v.tensor_tensor(iprob[:, four(t), :], heads4(b), imax[:, four(t)].unsqueeze(2).to_broadcast([P, 4, P]),
                                        ALU.subtract).then_inc(S["iprob_sub"], 1)
                if s == 5:
                    at(dve, "iprobT_done", turn, 1)
                    copy(iprobT[:, 4:8, :], heads4(b6), "iprobT_dve")
                    for t in (0, 1):
                        own.mark(v.tensor_reduce(isum[:, four(t)], iprob[:, four(t), :], AX.X, ALU.add))
                if s == 6:
                    own.link(v.tensor_reduce(isum[:, four(2)], iprob[:, four(2), :], AX.X, ALU.add))
                    own.link(v.reciprocal(irec[:, :], isum[:, :]))
                    at(dve, "ipv_done", turn, 1)
                    v.tensor_tensor(io[:, :].rearrange("p (h d) -> p h d", h=HEADS),
                                    b5[:, 0:D].rearrange("p (h d) -> p h d", h=HEADS),
                                    irec[:, :].unsqueeze(2).to_broadcast([P, HEADS, HD]), ALU.mult).then_inc(S["io_ready"], 1)
                if s == 7:
                    at(dve, "ioT_done", turn, 1)
                    copy(ioB[0:DB, :], b6[0:DB, 0:P], "ioB_ready")
                if s == 8:
                    at(dve, "iout_done", turn, 1)
                    copy(h[:, BB, :], b5[:, 0:D], "h_ready")
                if s in (8, 9):
                    r = 1 if s == 8 else 3
                    at(dve, "prodT_done", turn, RB, r + 1)
                    copy(prodT[:, r, :, :], b6[:, :].rearrange("p (t n) -> p t n", t=BB), "prodT_dve")
                if s == 10:
                    at(dve, "expval_done", turn, 1)
                    zx = b7[:, 0:BB * 2 * NQ].rearrange("p (t c q) -> p c t q", t=BB, c=2)
                    for c, row in ((0, C3), (1, S3)):
                        own.mark(v.tensor_tensor(evt[:, c], zx[:, c],
                                                 trig[:, row:row + NQ, bass.ds(turn * BB, BB)].rearrange("p q t -> p t q"), ALU.mult))
                    own.wait()
                    v.tensor_tensor(ev[:, :, 0:NQ], evt[:, 0], evt[:, 1], ALU.subtract).then_inc(S["ev_ready"], 1)
                if s == 12:
                    at(dve, "emb_done", turn, 1)
                    for i, b in ((0, b6), (1, b7)):
                        copy(h[:, 2 * i:2 * i + 2, :], b[:, 0:2 * D].rearrange("p (t d) -> p t d", t=2), "h_ready")
                if s == 13:
                    at(dve, "h_ready", turn, 3)
                    ln_stats(h, own)
                if s == 14:
                    ln_rows(h, turn, 0, own)
                if s == 15:
                    at(dve, "xT_done", turn, 1)
                    copy(xTA[:, :, TXT:SPAN], b6[:, 0:P].rearrange("p (b q) -> p b q", b=BB), "xT_dve")
                    copy(xTB[:, :, TXT:SPAN], b6[0:DB + 1, P:2 * P].rearrange("p (b q) -> p b q", b=BB), "xT_dve")
                if s == 17:
                    at(dve, "y_done", turn, 2, 2)
                    copy(yz[1][:, 0:320], b7[0:DB + 1, 0:320], "y_dve")
                if s == 18:
                    at(dve, "ascore_done", turn, 1)
                    own.mark(v.tensor_reduce(nmax[:, 0:3], b6[:, 0:3 * SEQ].rearrange("p (t k) -> p t k", t=3),
                                             AX.X, ALU.max, negate=True))
                    own.link(v.tensor_reduce(nmax[:, 3:5], b7[:, 0:2 * SEQ].rearrange("p (t k) -> p t k", t=2),
                                             AX.X, ALU.max, negate=True))
                    v.tensor_scalar(nbias[:, :], nmax[:, :], 0.125, None, ALU.mult).then_inc(S["nbias_ready"], 1)
                if s == 19:
                    at(dve, "prob_ready", turn, TILES)
                    for b in range(BB):
                        v.tensor_copy(pimg[:, b, b * SLOT:b * SLOT + IMG], prob[:, b, TXT:SEQ]).then_inc(S["pimg_ready"], 1)
                    for b in range(BB):
                        rows = slice(b * SLOT, (b + 1) * SLOT)
                        v.tensor_copy(pimg[rows, BB, b * SLOT:b * SLOT + IMG], prob[rows, BB, TXT:SEQ]).then_inc(S["pimg_ready"], 1)
                    own.mark(v.reciprocal(arec[:, :], asum[:, :]))
                if s == 20:
                    at(dve, "pT_done", turn, 1)
                    copy(pTB[:, :, 0:TXT], b6[:, :].rearrange("p (b q) -> p b q", b=BB), "pT_dve")
                if s == 21:
                    at(dve, "z_done", turn, 1)
                    copy(zA[:, BB * TXT:FFPAD], b6[:, 0:P], "z_dve")
                    copy(zB[:, BB * TXT:FFPAD], b6[0:DB + 1, P:2 * P], "z_dve")
                if s == 22:
                    at(dve, "aout_done", turn, 1)
                    own.wait()
                    for t in range(TILES):
                        b, c = ((b5, 0), (b5, D), (b6, 0), (b6, D), (b7, 0))[t]
                        v.scalar_tensor_tensor(out=h2[par][:, t, :], in0=b[:, c:c + D], scalar=arec[:, t:t + 1],
                                               in1=h[:, t, :], op0=ALU.mult, op1=ALU.add).then_inc(S["h2_ready"], 1)
                if s == 23:
                    at(dve, "h2_ready", turn, TILES)
                    ln_stats(h2[par], own)
                if s == 24:
                    ln_rows(h2[par], turn, 1, own)
                if s == 25:
                    at(dve, "x2_done", turn, 1)
                    for dst, rows, c in ((x2A, P, 0), (x2B, DB + 1, P)):
                        v.tensor_copy(dst[:, BB * TXT:FF].rearrange("p (b q) -> p b q", b=BB),
                                      b6[0:rows, c:c + P].rearrange("p (b q) -> p b q", b=BB)[:, :, 0:IMG])\
                         .then_inc(S["x2_dve"], 1)
                if s == 26:
                    at(dve, "gate_done", turn, 1)
                    lp = b5[:, 0:TILES * E].rearrange("p (t e) -> p t e", t=TILES)
                    own.link(v.tensor_reduce(lmax[:, :], lp, AX.X, ALU.max))
                    v.tensor_tensor(lg[:, :, :], lp, lmax[:, :].unsqueeze(2).to_broadcast([P, TILES, E]), ALU.subtract)\
                     .then_inc(S["lsub_ready"], 1)
                sp2 = sbias[:, :, :].rearrange("p t (g i) -> p t g i", i=2)
                if s == 27:
                    at(dve, "lexp_ready", turn, 1)
                    own.link(v.tensor_reduce(lsum[:, :], lg[:, :, :], AX.X, ALU.add))
                    own.link(v.reciprocal(lsum[:, :], lsum[:, :]))
                    own.link(v.tensor_tensor(score[:, :, :], lg[:, :, :], lsum[:, :].unsqueeze(2).to_broadcast([P, TILES, E]), ALU.mult))
                    own.link(v.tensor_tensor(sbias[:, :, :], score[:, :, :],
                                             bias_sb[:, :].unsqueeze(1).to_broadcast([P, TILES, E]), ALU.add))
                    own.link(v.tensor_tensor(gsum[:, :, :], sp2[:, :, :, 0], sp2[:, :, :, 1], ALU.add))
                if s == 28:
                    top4(gsum, G, own)
                    kept = keep[:, :, 0:G].unsqueeze(3).to_broadcast([P, TILES, G, 2])
                    own.mark(v.tensor_tensor(sp2, sp2, kept, ALU.mult))
                    own.link(v.tensor_scalar(scan_b[:, :, 0:G], keep[:, :, 0:G], BIG, -BIG, ALU.mult, ALU.add))
                    own.link(v.tensor_tensor(sp2, sp2, scan_b[:, :, 0:G].unsqueeze(3).to_broadcast([P, TILES, G, 2]), ALU.add))
                if s == 29:
                    top4(sbias, E, own)
                    own.link(v.tensor_tensor(score[:, :, :], score[:, :, :], keep[:, :, :], ALU.mult))
                    own.link(v.tensor_scalar(wfull[:, :, 0:E], score[:, :, :], 2.5, None, ALU.mult))
                    own.link(v.tensor_copy(wtok[:, :, 0:ES], wfull[:, :, :]))
                    v.tensor_tensor(wtok[:, :, WR - ES:WR], wfull[:, :, :], wtok[:, :, 0:ES].bitcast(F32), ALU.subtract)\
                     .then_inc(S["wtok_ready"], 1)
                if s in (31, 32):
                    hf = s - 31
                    c = slice(hf * HALF, (hf + 1) * HALF)
                    at(dve, "high_ready", turn, 6, 3 * hf + 3)
                    v.tensor_tensor(x_l[par][hf][:, :], x2A[:, c], x_h[par][hf][:, :].bitcast(F32), ALU.subtract)\
                     .then_inc(S["split_ready"], 1)
                    v.tensor_tensor(xb_l[par][hf][:, :], x2B[0:DB, c], xb_h[par][hf][0:DB, :].bitcast(F32), ALU.subtract)\
                     .then_inc(S["split_ready"], 1)

            def experts(s, turn, par, first):
                if s >= 1:
                    at(dve, "a_high_ready", turn, SLOTS, s)
                    at(dve, "down_done", turn, SLOTS, s - 2)
                    v.tensor_tensor(a_l[:, (s - 1) % 2, :], act_w[:, :], a_h[:, (s - 1) % 2, :].bitcast(F32), ALU.subtract)\
                     .then_inc(S["a_low_ready"], 1)
                if s in (1, ES + 1) and not (s == 1 and first):
                    half_out(s != 1, turn, first)
                if s == SLOTS:
                    return
                if s == 4 and not first:
                    finish(turn - 1, 1 - par)
                e = s % ES
                at(dve, "g_done", turn, SLOTS, s + 1)
                at(dve, "sl_ready", turn, SLOTS, s + 1)
                v.scalar_tensor_tensor(out=gated[:, :], in0=GATE[:, 0:HALF], scalar=bg_sb[:, e:e + 1],
                                       in1=sl[:, :], op0=ALU.add, op1=ALU.mult).then_inc(S["gated_ready"], 1)
                at(dve, "w_done", turn, SLOTS, s + 1)
                at(dve, "gated_ready", turn, SLOTS, s + 1)
                v.tensor_tensor(act_w[:, :], gated[:, :], WEIGHT[:, 0:HALF], ALU.mult).then_inc(S["act_ready"], 1)

            def half_out(is_first_half, turn, first):
                if is_first_half:
                    at(dve, "down_done", turn, SLOTS, ES)
                    if not first:
                        at(dve, "out_stored", turn, 16 * (BB + 1), 0)
                    copy(yTB[:, 0:HALF], YB[:, 0:HALF], "yb_ready")
                else:
                    at(dve, "down_done", turn, SLOTS, 0)
                    k = BB * TXT - HALF
                    copy(yTB[:, HALF:BB * TXT], YB[:, 0:k], "yb_ready")
                    copy(yTB[:, BB * TXT:FFPAD].rearrange("p (b q) -> p b q", b=BB)[:, :, 0:IMG],
                         YB[:, k:HALF].rearrange("p (b q) -> p b q", b=BB), "yb_ready")

            def finish(turn, par):
                at(dve, "fin_done", turn, 1)
                for i, b in enumerate((b5, b6, b7)):
                    n = 2 if i < 2 else 1
                    v.tensor_tensor(o_sb[:, 2 * i:2 * i + n, :], b[:, 0:n * D].rearrange("p (t d) -> p t d", t=n),
                                    h2[par][:, 2 * i:2 * i + n, :], ALU.add).then_inc(S["o_ready"], 1)

            turns(dve, experts, front, lambda turn: Chain(dve, S["dve_own"], turn, DVE_FRONT_CHAIN, "DVE_FRONT_CHAIN"))
            half_out(False, TURNS, False)
            finish(TURNS - 1, 1)

        @block.tensor
        def _(pe):
            mm = nc.tensor.matmul

            def tr(dst, src, n=P):
                return nc.tensor.transpose(dst, src, ident[0:n, 0:n])

            for first, w1 in ((0, D + 1), (2, D)):
                pe.wait_ge(S["loads_big"], 48 if first == 0 else 80)
                l = wbig[0].rearrange("p (k n) -> p k n", k=KQ)
                r = wbig[1][:, 0:KQ * w1].rearrange("p (k n) -> p k n", k=KQ)
                for i, (a, b) in enumerate(((0, P), (P, D + 1))):
                    for k in range(KQ):
                        ins = mm(bank[first + i][0:b - a, 0:w1], l[:, k, a:b], r[:, k, :], start=(k == 0), stop=(k == KQ - 1))
                    ins.then_inc(S["mm_big"], 1)
            pe.wait_ge(S["products_ready"], 4)
            pe.wait_ge(S["loads_tok"], 16 * 13)
            pe.wait_ge(S["loads_txt"], 16 * 7)
            pe.wait_ge(S["loads_ffn"], 32)
            pe.wait_ge(S["consts_ready"], 1)
            pe.wait_ge(S["weights_ready"], 1)
            pe.sem_inc(S["prodT_done"], 1)

            def front(s, turn, par, own, busy):
                if s == 0:
                    at(pe, "patches_in", turn, 16)
                    at(pe, "w_ready", turn, 3, 0)
                    for b, lo, hi in ((b5, 0, P), (b6, P, D)):
                        for k in range(KP):
                            ins = mm(b[0:hi - lo, 0:P], conv_sb[:, k, lo:hi], patch_sb[:, k, :], start=(k == 0), stop=(k == KP - 1))
                    ins.then_inc(S["conv_done"], 1)
                if s == 1:
                    at(pe, "tA_ready", turn, 1)
                    at(pe, "tB_ready", turn, 1)
                    for b, wa, wb in ((b5, wqA, wqB), (b6, wkA, wkB)):
                        for t in range(HT):
                            cols = slice(t * P, (t + 1) * P)
                            mm(b[:, cols], wa[:, cols], tA[:, :], start=True, stop=False)
                            mm(b[:, cols], wb[:, cols], tB[:, :], start=False, stop=True)
                    mm(b7[:, 0:D], tA[:, :], wvA[:, :], start=True, stop=False)
                    mm(b7[:, 0:D], tB[0:DB + 1, :], wvB[:, :], start=False, stop=True).then_inc(S["tproj_done"], 1)
                if s == 2:
                    at(pe, "qv_ready", turn, 2)
                    at(pe, "kdiag_ready", turn, 4)
                    for t, b in enumerate((b5, b6, b7)):
                        ins = mm(b[:, :], qT[:, t * P:(t + 1) * P], kdiag[:, t, :, :].rearrange("p h k -> p (h k)"),
                                 start=True, stop=True)
                    ins.then_inc(S["iscore_done"], 1)
                if s == 5:
                    at(pe, "iprob_exp", turn, HT)
                    if busy:
                        at(pe, "o_ready", turn - 2, 3)
                    for t, b in enumerate((b5, b6, b7)):
                        for j in range(4):
                            ins = tr(b[:, j * P:(j + 1) * P], iprob[:, 4 * t + j, :])
                    ins.then_inc(S["iprobT_done"], 1)
                if s == 6:
                    at(pe, "iprobT_act", turn, 2)
                    at(pe, "iprobT_dve", turn, 1)
                    for hd in range(HEADS):
                        c = slice(hd * HD, (hd + 1) * HD)
                        ins = mm(b5[:, c], iprobT[:, hd, :], v_sb[:, c], start=True, stop=True)
                    ins.then_inc(S["ipv_done"], 1)
                if s == 7:
                    at(pe, "io_ready", turn, 1)
                    tr(b5[:, 0:P], io[:, 0:P])
                    tr(b6[0:DB, 0:P], io[:, P:D]).then_inc(S["ioT_done"], 1)
                    at(pe, "prods_ready", turn, 1)
                    prod_rows(0, b7)
                if s == 8:
                    at(pe, "ioA_ready", turn, 1)
                    at(pe, "ioB_ready", turn, 1)
                    mm(b5[:, 0:D], ioA[:, :], woA[:, :], start=True, stop=False)
                    mm(b5[:, 0:D], ioB[:, :], woB[:, :], start=False, stop=True).then_inc(S["iout_done"], 1)
                    prod_rows(1, b6)
                    at(pe, "prodT_act", turn, 2, 1)
                    prod_rows(2, b7)
                if s == 9:
                    at(pe, "prodT_dve", turn, 2, 1)
                    prod_rows(3, b6)
                if s == 10:
                    at(pe, "prodT_act", turn, 2)
                    at(pe, "prodT_dve", turn, 2)
                    for t in range(BB):
                        for r in range(RB):
                            ins = mm(b7[:, t * 2 * NQ:(t + 1) * 2 * NQ], prodT[:, r, t, :], red_sb[:, r, :],
                                     start=(r == 0), stop=(r == RB - 1))
                    ins.then_inc(S["expval_done"], 1)
                if s == 11:
                    at(pe, "ev_ready", turn, 1)
                    at(pe, "h_ready", turn, 3, 1)
                    for t in range(BB):
                        ins = tr(b5[0:NQ + 1, t * P:(t + 1) * P], ev[:, t, :])
                    ins.then_inc(S["evT_done"], 1)
                if s == 12:
                    at(pe, "evT_ready", turn, 1)
                    for t in range(BB):
                        ins = mm((b6, b7)[t // 2][:, (t % 2) * D:(t % 2 + 1) * D], evT[:, t * P:(t + 1) * P], pw_sb[:, :],
                                 start=True, stop=True)
                    ins.then_inc(S["emb_done"], 1)
                if s in (15, 25):
                    at(pe, "xn_ready", turn, 2 * TILES, TILES if s == 15 else 2 * TILES)
                    for t in range(TILES):
                        oa, ob = (b5[:, t * P:(t + 1) * P], b7[0:DB + 1, t * P:(t + 1) * P]) if t < BB \
                            else (b6[:, 0:P], b6[0:DB + 1, P:2 * P])
                        tr(oa, xn[:, t, 0:P])
                        ins = tr(ob, xn[:, t, P:D + 1])
                    ins.then_inc(S["xT_done" if s == 15 else "x2_done"], 1)
                if s in (16, 17):
                    if s == 16:
                        at(pe, "xT_act", turn, 2)
                        at(pe, "xT_dve", turn, 2)
                        lo, hi, banks = 0, P, (b5, b6)
                    else:
                        at(pe, "y_act", turn, 3, 1)
                        lo, hi, banks = P, D + 1, (b7, b5)
                    for i in range(2):
                        c = slice(320 * i, 320 * i + 320)
                        mm(banks[i][0:hi - lo, 0:320], MA[:, lo:hi], x2A[:, c], start=True, stop=False)
                        ins = mm(banks[i][0:hi - lo, 0:320], MB[:, lo:hi], x2B[:, c], start=False, stop=True)
                    ins.then_inc(S["y_done"], 1)
                if s == 18:
                    at(pe, "y_act", turn, 3)
                    at(pe, "y_dve", turn, 1)
                    for b in range(BB):
                        o = b6[:, b * SEQ:(b + 1) * SEQ] if b < 3 else b7[:, 0:SEQ]
                        mm(o, yA[:, b, 0:TXT], xTA[:, b, 0:SEQ], start=True, stop=False)
                        mm(o, yB[:, b, 0:TXT], xTB[:, b, 0:SEQ], start=False, stop=True)
                    for b in range(BB):
                        o = b7[b * SLOT:(b + 1) * SLOT, SEQ:2 * SEQ]
                        mm(o, yA[:, b, TXT:SPAN], xTA[:, b, 0:SEQ], start=True, stop=False, tile_position=(0, b * SLOT))
                        ins = mm(o, yB[:, b, TXT:SPAN], xTB[:, b, 0:SEQ], start=False, stop=True, tile_position=(0, b * SLOT))
                    ins.then_inc(S["ascore_done"], 1)
                if s == 20:
                    at(pe, "prob_ready", turn, TILES)
                    at(pe, "pimg_ready", turn, 2 * BB)
                    for t in range(BB):
                        tr(b5[:, t * P:(t + 1) * P], prob[:, t, 0:TXT])
                        tr(b6[:, t * P:(t + 1) * P], pimg[:, t, :])
                    tr(b7[:, 0:P], prob[:, BB, 0:TXT])
                    tr(b7[:, P:2 * P], pimg[:, BB, :]).then_inc(S["pT_done"], 1)
                if s == 21:
                    at(pe, "pT_act", turn, 3)
                    at(pe, "pT_dve", turn, 1)
                    for lo, hi, text, col in ((0, P, b5, 0), (P, D + 1, b7, P)):
                        for b in range(BB):
                            for bk, c, q0, q1 in ((text, b * TXT, 0, TXT), (b6, col + b * SLOT, TXT, SPAN)):
                                o = bk[0:hi - lo, c:c + q1 - q0]
                                mm(o, xn[:, b, lo:hi], pTA[:, b, q0:q1], start=True, stop=False)
                                ins = mm(o, xn[:, BB, lo:hi], pTB[:, b, q0:q1], start=False, stop=True)
                    ins.then_inc(S["z_done"], 1)
                if s == 22:
                    at(pe, "z_act", turn, 2)
                    at(pe, "z_dve", turn, 2)
                    for t in range(TILES):
                        b, c = ((b5, 0), (b5, D), (b6, 0), (b6, D), (b7, 0))[t]
                        q = slice(t * P, (t + 1) * P)
                        mm(b[:, c:c + D], zA[:, q], OA[:, :], start=True, stop=False)
                        ins = mm(b[:, c:c + D], zB[:, q], OB[:, :], start=False, stop=True)
                    ins.then_inc(S["aout_done"], 1)
                if s == 26:
                    at(pe, "x2_act", turn, 2)
                    at(pe, "x2_dve", turn, 2)
                    for t in range(TILES):
                        c = slice(t * P, (t + 1) * P)
                        mm(b5[:, t * E:(t + 1) * E], x2A[:, c], gwA[:, :], start=True, stop=False)
                        ins = mm(b5[:, t * E:(t + 1) * E], x2B[:, c], gwB[:, :], start=False, stop=True)
                    ins.then_inc(S["gate_done"], 1)
                if s == 30:
                    at(pe, "wtok_ready", turn, 1)
                    for t in range(TILES):
                        o = b5[0:WR, t * P:(t + 1) * P] if t < BB else b6[0:WR, 0:P]
                        ins = mm(o, wtok[:, t, :].bitcast(F32), ident[:, :], start=True, stop=True)
                    ins.then_inc(S["wT_done"], 1)

            def prod_rows(r, b):
                for t in range(BB):
                    ins = tr(b[:, t * P:(t + 1) * P], prods[:, t, r * P:(r + 1) * P])
                ins.then_inc(S["prodT_done"], 1)

            def down(s, turn, par):
                e, hf = s % ES, s // ES
                if e == 0:
                    at(pe, "ya_ready", turn, 3, hf)
                    at(pe, "yb_ready", turn, 3, hf)
                    w = w_hl[par][hf][:, :]
                    mm(YA[:, 0:HALF], bd_h[:, :], w, start=True, stop=False)
                    mm(YA[:, 0:HALF], bd_l[:, :], w, start=False, stop=False)
                    mm(YB[:, 0:HALF], bd_b[:, :], w, start=True, stop=False)
                at(pe, "a_high_ready", turn, SLOTS, s + 1)
                high, low = a_h[:, s % 2, :], a_l[:, s % 2, :]
                mm(YA[:, 0:HALF], wd_h[:, e, :], high, start=False, stop=False)
                mm(YA[:, 0:HALF], wd_l[:, e, :], high, start=False, stop=False)
                mm(YB[:, 0:HALF], wd_b[:, e, :], high, start=False, stop=False)
                at(pe, "a_low_ready", turn, SLOTS, s + 1)
                mm(YA[:, 0:HALF], wd_h[:, e, :], low, start=False, stop=(e == ES - 1))
                mm(YB[:, 0:HALF], wd_b[:, e, :], low, start=False, stop=(e == ES - 1)).then_inc(S["down_done"], 1)

            def experts(s, turn, par, first):
                if s == 4 and not first:
                    alone = isinstance(turn, int) and turn == TURNS - 1
                    finish(turn - 1, None if alone else turn + 1)
                if s == SLOTS:
                    down(s - 1, turn, par)
                    return
                e, hf = s % ES, s // ES
                if s == 0:
                    at(pe, "high_ready", turn, 6)
                    at(pe, "split_ready", turn, 4)
                    at(pe, "w_ready", turn, 3)
                for o, h_, l_, b_, name, read in ((UP, wu_h, wu_l, wu_b, "u_done", "sl_ready"),
                                                  (GATE, wg_h, wg_l, wg_b, "g_done", "gated_ready")):
                    at(pe, read, turn, SLOTS, s)
                    o = o[:, 0:HALF]
                    mm(o, h_[:, e, :], x_h[par][hf][:, :], start=True, stop=False)
                    mm(o, l_[:, e, :], x_h[par][hf][:, :], start=False, stop=False)
                    mm(o, h_[:, e, :], x_l[par][hf][:, :], start=False, stop=False)
                    mm(o, b_[:, e, :], xb_h[par][hf][:, :], start=False, stop=False)
                    mm(o, b_[0:DB, e, :], xb_l[par][hf][:, :], start=False, stop=True).then_inc(S[name], 1)
                at(pe, "act_ready", turn, SLOTS, s)
                mm(WEIGHT[:, 0:HALF], sel[:, e:e + 1].to_broadcast([WR, P]), w_hl[par][hf][:, :], start=True, stop=True).then_inc(S["w_done"], 1)
                if s >= 1:
                    down(s - 1, turn, par)

            def finish(turn, upcoming):
                at(pe, "ya_ready", turn, 3)
                at(pe, "yb_ready", turn, 3)
                if upcoming is not None:
                    at(pe, "iprob_sub", upcoming, HT)
                for t in range(TILES):
                    b, c = (b5, b6, b7)[t // 2], (t % 2) * D
                    tr(b[:, c:c + P], yTA[:, t * P:(t + 1) * P])
                    ins = mm(b[:, c + P:c + D], yTB[:, t * P:(t + 1) * P], ident2[:, :], start=True, stop=True)
                ins.then_inc(S["fin_done"], 1)

            turns(pe, experts, front, lambda turn: None)
            finish(TURNS - 1, None)


def reduction_matrix():
    basis = np.arange(NS)
    out = np.zeros((NPROD, 2 * NQ), np.float32)
    for q in range(NQ):
        bits = range(1, NQ) if q == 0 else range(q + 1)
        parity = sum((basis >> (NQ - 1 - b)) & 1 for b in bits) % 2
        out[:2 * NS, q] = np.tile(1.0 - 2.0 * parity, 2)
        out[2 * NS + NS * q:2 * NS + NS * (q + 1), NQ + q] = 2.0
    return out


_ORDER = ["patches", "tokens", "conv_w", "conv_b", "wq", "wk", "wv", "wo", "tok_const", "params", "post_w",
          "wq_big", "wk_big", "wv_big", "wout_big", "bout_big", "gate_w", "bias",
          "wuA_in", "wuB_in", "bu", "wgA_in", "wgB_in", "bg", "wd", "bd", "reduce_w", "ident_in"]


def kernel(**inputs):
    import concourse.bacc as _bacc
    from concourse.bass_utils import run_bass_kernel_spmd as _run

    a = {k: np.asarray(v) for k, v in inputs.items()}
    f = np.float32

    def stack(w, b):
        return np.concatenate([w, b[None]], 0)

    x = a["x"][:, :, :80, :80].reshape(NB, 3, 5, 16, 5, 16).transpose(1, 3, 5, 0, 2, 4).reshape(PIX, NB, IMG)
    pad = np.zeros((PIX, NB, SLOT), f)
    pad[:, :, :IMG] = x
    patches = np.ascontiguousarray(pad.reshape(KP, P, TURNS, BB * SLOT).transpose(2, 1, 0, 3))

    def heads(w, b, extra_row):
        full = stack(w.T, b).reshape(D + 1, HEADS, HD)
        out = np.zeros((D + 1 + 2 * BB, HEADS, 32), f)
        out[:D + 1, :, :HD] = full
        for i in range(BB):
            out[D + 1 + extra_row + i, :, HD + i] = 1.0
        return out.reshape(D + 1 + 2 * BB, HT * P)

    tok_const = np.zeros((1 + 2 * BB, P), f)
    tok_const[0] = 1.0
    tok_const[1 + BB:] = -1e30
    for i in range(BB):
        tok_const[1 + i, i * SLOT:(i + 1) * SLOT] = 1.0
        tok_const[1 + BB + i, i * SLOT:i * SLOT + IMG] = 0.0

    def rows(w, n):
        return np.ascontiguousarray(w.reshape(n, P, -1).transpose(1, 0, 2).reshape(P, -1))

    qkv, bqkv = a["L0_attn_w_qkv"], a["L0_attn_b_qkv"]
    big = [rows(stack(qkv[:, i * QK:(i + 1) * QK], bqkv[i * QK:(i + 1) * QK]).T, KQ) for i in range(3)]

    def experts(w, shared):
        return np.concatenate([w, shared[None]], 0)

    wu, wg, wd = (experts(a[f"L0_ffn_W{n}"], a[f"L0_ffn_sW{n}"]) for n in "ugd")
    bu, bg, bd = (experts(a[f"L0_ffn_b{n}"], a[f"L0_ffn_sb{n}"]) for n in "ugd")

    def by_block(w):
        rows_ = w.transpose(1, 0, 2).reshape(D, ES * HID)
        return rows_[:P], np.concatenate([rows_[P:], rows_[P:]], 0)

    bd2 = np.zeros((WR, D), f)
    bd2[:ES] = bd2[WR - ES:] = bd
    arrays = {
        "patches": patches,
        "tokens": np.ascontiguousarray(a["x_txt"].T),
        "conv_w": rows(a["L0_tok_conv_w"].reshape(D, PIX).T, KP).reshape(P, KP, D),
        "conv_b": a["L0_tok_conv_b"].reshape(D, 1),
        "wq": heads(a["L0_tok_wq"], a["L0_tok_bq"], 0),
        "wk": heads(a["L0_tok_wk"], a["L0_tok_bk"], BB),
        "wv": stack(a["L0_tok_wv"].T, a["L0_tok_bv"]),
        "wo": stack(a["L0_tok_wo"].T, a["L0_tok_bo"]),
        "tok_const": tok_const,
        "params": a["L0_txt_quantum_params"].reshape(-1, 36),
        "post_w": stack(a["L0_txt_post_w"].T, a["L0_txt_post_b"]),
        "wq_big": big[0], "wk_big": big[1], "wv_big": big[2],
        "wout_big": rows(a["L0_attn_w_out"], KQ),
        "bout_big": a["L0_attn_b_out"].reshape(1, D),
        "gate_w": stack(a["L0_ffn_gate_w"], a["L0_ffn_gate_b"]),
        "bias": a["L0_ffn_bias"],
        "wuA_in": by_block(wu)[0], "wuB_in": by_block(wu)[1], "bu": bu.T,
        "wgA_in": by_block(wg)[0], "wgB_in": by_block(wg)[1], "bg": bg.T,
        "wd": wd.transpose(1, 0, 2).reshape(HID, ES * D), "bd": bd2,
        "reduce_w": reduction_matrix().reshape(RB, P, 2 * NQ).transpose(1, 0, 2),
        "ident_in": np.eye(P, dtype=f),
    }
    nc = _bacc.Bacc("TRN2", target_bir_lowering=False, num_devices=1)
    feed, args = {}, []
    for name in _ORDER:
        arr = np.ascontiguousarray(arrays[name])
        feed[f"in_{name}_dram"] = arr
        args.append(nc.dram_tensor(f"in_{name}_dram", arr.shape, mybir.dt.from_np(arr.dtype), kind="ExternalInput").ap())
    args.append(nc.dram_tensor("out_0_dram", (NB, SEQ, D), F32, kind="ExternalOutput").ap())
    early_fusion(nc, *args)
    r = _run(nc, [feed], core_ids=[0])
    return r.results[0]["out_0_dram"]
```

```python
from contextlib import ExitStack

import numpy as np
import concourse.bass as bass
from concourse import mybir

F32 = mybir.dt.float32
F32R = mybir.dt.float32r
I32 = mybir.dt.int32
U32 = mybir.dt.uint32
ALU = mybir.AluOpType
ACT = mybir.ActivationFunctionType
AX = mybir.AxisListType

P = 128
NB = 32
BB = 4
TURNS = NB // BB
TXT = 128
IMG = 25
SLOT = 32
SEQ = TXT + IMG
SPAN = TXT + SLOT
TILES = BB + 1
D = 192
DB = D - P
PIX = 768
KP = PIX // P
HEADS, HD = 12, 16
HT = HEADS // 4
QK = 768
KQ = QK // P
E, HID = 16, 128
ES = E + 1
G = 8
NQ = 6
NS = 1 << NQ
FF = BB * SEQ
HALF = FF // 2
FFPAD = TILES * P
NPROD = 512
RB = NPROD // P
WR = SLOT + ES
AHEAD_SLOTS = {20: -2, 29: -1}
ANGLES_SLOT = 8
SLOTS = 2 * ES
TWO_PI = 6.283185
EARLY = 2 * BB
ROUND = 12582912.0
BIG = 3.0e38
SENTINEL, PICKED = -3.2e38, 3.2e38
EPS = 1e-5
RSQRT_MAGIC = float(0x5f3759df)

C1, S1, CP1, SP1, C2, S2, CP2, SP2, C3, S3 = [NQ * i for i in range(10)]
NTRIG = NQ * 10

DVE_FRONT_CHAIN = 113
POOL_CHAIN = 146


class Chain:

    def __init__(self, eng, sem, turn=None, per=0, name=""):
        self.eng, self.sem, self.turn, self.per, self.n, self.name = eng, sem, turn, per, 0, name

    def mark(self, ins):
        self.n += 1
        ins.then_inc(self.sem, 1)

    def wait(self):
        base = 0 if self.turn is None else self.turn * self.per
        self.eng.wait_ge(self.sem, base + self.n)

    def link(self, ins):
        self.mark(ins)
        self.wait()


def early_fusion(nc, patches, tokens, conv_w, conv_b, wq, wk, wv, wo, tok_const, params, post_w,
                 wq_big, wk_big, wv_big, wout_big, bout_big, gate_w, bias, wuA_in, wuB_in, bu,
                 wgA_in, wgB_in, bg, wd, bd, reduce_w, ident_in, out):
    ctx = ExitStack()
    with ctx:
        def sb(name, shape, dt=F32):
            return ctx.enter_context(nc.sbuf_tensor(name, shape, dt))

        def sem(name):
            return ctx.enter_context(nc.semaphore(name))

        bank = [ctx.enter_context(nc.psum_tensor(f"bank{i}", [P, 512], F32)) for i in range(8)]
        UP, GATE, WEIGHT, YA, YB = bank[0:5]
        b5, b6, b7 = bank[5:8]

        ident = sb("ident", [P, P])
        ident2 = sb("ident2", [P, DB])
        conv_sb = sb("conv_sb", [P, KP, D])
        conv_bA = sb("conv_bA", [P, 1])
        conv_bB = sb("conv_bB", [DB, 1])
        KB = DB + 1 + 2 * BB
        wqA, wqB = sb("wqA", [P, HT * P]), sb("wqB", [KB, HT * P])
        wkA, wkB = sb("wkA", [P, HT * P]), sb("wkB", [KB, HT * P])
        wvA, wvB = sb("wvA", [P, D]), sb("wvB", [DB + 1, D])
        woA, woB = sb("woA", [P, D]), sb("woB", [DB + 1, D])
        pw_sb = sb("pw_sb", [NQ + 1, D])
        red_sb = sb("red_sb", [P, RB, 2 * NQ])
        gwA, gwB = sb("gwA", [P, E]), sb("gwB", [DB + 1, E])
        bias_sb = sb("bias_sb", [P, E])
        sel = sb("sel", [WR, ES + 1], F32R)
        wu_h, wu_l, wu_b = (sb(f"wu_{x}", [P, ES, HID], F32R) for x in "hlb")
        wg_h, wg_l, wg_b = (sb(f"wg_{x}", [P, ES, HID], F32R) for x in "hlb")
        wd_h, wd_l, wd_b = (sb(f"wd_{x}", [HID, ES, P], F32R) for x in "hlb")
        bd_h, bd_l, bd_b = (sb(f"bd_{x}", [WR, P], F32R) for x in "hlb")
        bu_sb, bg_sb = sb("bu_sb", [HID, ES]), sb("bg_sb", [HID, ES])
        MA, MB = sb("MA", [P, D + 1]), sb("MB", [DB + 1, D + 1])
        OA, OB = sb("OA", [P, D]), sb("OB", [DB + 1, D])
        idx_sb = sb("idx_sb", [P, NB], I32)
        trig = sb("trig", [P, NTRIG, NB])
        V1 = sb("V1", [P, 2, NQ, BB])
        GG = sb("GG", [P, 2, 4, BB])
        X0 = sb("X0", [P, 2, NS, BB])
        X1 = sb("X1", [P, 2, NS, BB])
        ST = sb("ST", [P, 2, NS, BB])
        EA, EB = (ST[:, i, :, :].rearrange("p (c s) t -> p c s t", c=2) for i in range(2))
        prods = sb("prods", [P, BB, NPROD])
        yz_all = [sb("yzA", [P, FFPAD]), sb("yzB", [P, FFPAD])]
        yz = [yz_all[0][:, :], yz_all[1][0:DB + 1, :]]
        qT = yz_all[0][:, 0:HT * P]
        ioA, io, v_sb = (yz_all[1][:, a:a + n] for a, n in ((0, P), (P, D), (P + D, D)))
        patch_sb = sb("patch_sb", [P, KP, P])
        tA, tB = sb("tA", [P, P]), sb("tB", [KB, P])
        kdiag = sb("kdiag", [P, HT, 4, P])
        imax = sb("imax", [P, HEADS])
        isum = sb("isum", [P, HEADS])
        irec = sb("irec", [P, HEADS])
        ioB = sb("ioB", [DB + 1, P])
        prodT = sb("prodT", [P, RB, BB, P])
        prodT_flat = prodT[:, :, :, :].rearrange("p r t n -> p (r t n)")
        iprobT = prodT_flat[:, 0:HEADS * P].rearrange("p (h n) -> p h n", h=HEADS)
        iprob_t = sb("iprob", [P, HEADS, P])
        iprob = iprob_t[:, :, :]
        iprob_flat = iprob.rearrange("p h n -> p (h n)")
        pTA, pTB = (iprob_flat[:, i * FFPAD:(i + 1) * FFPAD].rearrange("p (b s) -> p b s", b=BB) for i in range(2))
        evt = sb("evt", [P, 2, BB, NQ])
        ev = sb("ev", [P, BB, NQ + 1])
        h = sb("h", [P, TILES, D])
        stats = sb("stats", [P, TILES, 6])
        mv = sb("mv", [P, TILES, 2])
        vare = sb("vare", [P, TILES])
        nhalf = sb("nhalf", [P, TILES])
        rstd = sb("rstd", [P, TILES])
        nt = sb("nt", [P, TILES])
        nmr = sb("nmr", [P, TILES])
        xn = sb("xn", [P, TILES, D + 1])
        xTA, xTB = sb("xTA", [P, BB, SPAN]), sb("xTB", [DB + 1, BB, SPAN])
        x2A, x2B = (x[:, :, :].rearrange("p b s -> p (b s)") for x in (xTA, xTB))
        zA, zB = yz
        yA, yB = (x.rearrange("p (b s) -> p b s", b=BB) for x in yz)
        evT = yz[0][0:NQ + 1, 0:BB * P]
        zxT = yz[0][0:2 * NQ, 0:BB * P]
        nmax = sb("nmax", [P, TILES])
        nbias = sb("nbias", [P, TILES])
        asum = sb("asum", [P, TILES])
        arec = sb("arec", [P, TILES])
        prob = prodT_flat[:, 0:TILES * SEQ].rearrange("p (t k) -> p t k", t=TILES)
        pimg = sb("pimg", [P, TILES, P])
        h2 = [sb(f"h2_{i}", [P, TILES, D]) for i in range(2)]
        lmax = sb("lmax", [P, TILES])
        lg = sb("lg", [P, TILES, E])
        lsum = sb("lsum", [P, TILES])
        score = sb("score", [P, TILES, E])
        sbias = sb("sbias", [P, TILES, E + 4])
        gsum = sb("gsum", [P, TILES, G + 4])
        top8 = sb("top8", [P, TILES, 8])
        picked = sb("picked", [P, TILES, E + 4])
        drop = sb("drop", [P, TILES, G])
        keep = sb("keep", [P, TILES, E])
        wfull = sb("wfull", [P, TILES, ES])
        wtok = sb("wtok", [P, TILES, WR], F32R)

        def halves(name, rows):
            first, even, odd = (sb(f"{name}_{x}", [rows, HALF], F32R) for x in ("first", "even", "odd"))
            return [[first, even], [first, odd]]

        x_h, x_l = halves("x_h", P), halves("x_l", P)
        xb_h, xb_l = halves("xb_h", P), halves("xb_l", DB)
        w_hl = halves("w_hl", WR)
        sl = sb("sl", [HID, HALF])
        gated = sb("gated", [HID, HALF])
        act_w = sb("act_w", [HID, HALF])
        a_h = sb("a_h", [HID, 2, HALF], F32R)
        a_l = sb("a_l", [HID, 2, HALF], F32R)
        yT = sb("yT", [P, 2 * FFPAD])
        yTA, yTB = yT[:, 0:FFPAD], yT[:, FFPAD:2 * FFPAD]
        o_sb = yT[:, 0:TILES * D].rearrange("p (t d) -> p t d", t=TILES)
        spare = sb("spare", [P, 1])

        yT_flat, h2_odd = yT[:, :], h2[1][:, :, :].rearrange("p t d -> p (t d)")
        par_early = h2_odd[:, 0:EARLY * 36].rearrange("p (t k) -> p t k", t=EARLY)
        round_early = [h2_odd[:, EARLY * 36 + i * BB * NTRIG:EARLY * 36 + (i + 1) * BB * NTRIG] for i in range(EARLY // BB)]
        par_late = yT_flat[:, 0:(NB - EARLY) * 36].rearrange("p (t k) -> p t k", t=NB - EARLY)
        round_late = h2_odd[:, 0:NTRIG // 2 * (NB - EARLY)]
        BIGW = KQ * (D + 1)
        wbig = [iprob_flat[:, 0:BIGW], yT_flat[:, 0:BIGW]]
        bo_row = h[0:DB + 1, 0, :]
        bd_raw = io[0:WR, :]
        prods_flat = prods[:, :, :].rearrange("p t n -> p (t n)")
        stage = [x[:, i * 1024:(i + 1) * 1024] for x in (prods_flat, prodT_flat) for i in range(2)]
        STAGES = len(stage)

        names = """loads_tok loads_txt loads_big loads_ffn idx_in par_first_in par_in consts_ready products_ready mm_big
            stage0_in stage1_in stage2_in stage3_in stage_high stage_free weights_ready
            trig_ready trig_raw patches_in conv_done t_ready tproj_done qv_ready kdiag_ready
            iscore_done iprob_sub iprob_exp iprobT_done iprobT_act iprobT_dve ipv_done io_ready ioT_done ioA_ready ioB_ready
            iout_done prods_ready prodT_done prodT_act prodT_dve zx_done zxT_ready expval_done ev_ready evT_done evT_ready emb_done h_ready
            nmr_ready xn_act xn_dve xT_done xT_act xT_dve y_done y_act y_dve ascore_done nbias_ready prob_ready
            pimg_ready pT_done pT_act pT_dve z_done z_act z_dve aout_done h2_ready x2_done x2_act x2_dve
            gate_done lsub_ready lexp_ready high_ready split_ready wtok_ready wT_done w_ready
            u_done g_done w_done sl_ready gated_ready act_ready a_high_ready a_low_ready down_done down_low_done ya_ready yb_ready
            fin_done o_ready out_stored dve_own dve_setup pool_own pool_setup act_own act_setup""".split()
        S = {n: sem(n) for n in names}

        def at(eng, name, turn, per, n=None):
            count = turn * per + (per if n is None else n) + (name == "prodT_done")
            if not (isinstance(count, int) and count <= 0):
                eng.wait_ge(S[name], count)

        def turns(eng, chain, front, experts, late=None, low=None, half_out=None, angles=None):
            own = chain(0)

            def both(steps):
                for s in steps:
                    front(s, 0, 0, own, False)
                    if late:
                        late(s, 0, 0, own)

            for s in (-2, -1):
                front(s, 0, 0, own, False)
            both(range(0, 5))
            if late:
                for s in range(5, 10):
                    late(s, 0, 0, own)
            for s in (11, 12, 13, 5, 6, 7, 8, 9):
                front(s, 0, 0, own, False)
            both([10])
            if late:
                for s in range(11, 14):
                    late(s, 0, 0, own)
            for s in range(14, SLOTS):
                both([s])
                if s in AHEAD_SLOTS:
                    front(AHEAD_SLOTS[s], 1, 1, None, False)
            assert own is None or own.n == own.per, f"{own.name} = {own.n}"

            def step(s, turn, parity, own, first=False, alone=False, ahead=True):
                if low and s:
                    low(s - 1, turn)
                if half_out and (s == ES + 1 or s == 1 and not first):
                    half_out(s != 1, turn, first)
                if not alone:
                    front(s, turn + 1, 1 - parity, own, not first)
                if not alone and ahead and s in AHEAD_SLOTS:
                    front(AHEAD_SLOTS[s], turn + 2, parity, None, False)
                experts(s, turn, parity, first)
                if late and not alone:
                    late(s, turn + 1, 1 - parity, own)
                if angles and first and s == ANGLES_SLOT:
                    angles()

            def beside(turn, parity, first=False, ahead=True):
                own = chain(turn + 1)
                for s in range(SLOTS):
                    step(s, turn, parity, own, first=first, ahead=ahead)
                if low:
                    low(SLOTS - 1, turn)

            beside(0, 0, first=True)
            with eng.Fori(0, (TURNS - 4) // 2) as pair:
                beside(pair * 2 + 1, 1)
                beside(pair * 2 + 2, 0)
            beside(TURNS - 3, 1)
            beside(TURNS - 2, 0, ahead=False)
            for s in range(SLOTS):
                step(s, TURNS - 1, 1, None, alone=True)
            if low:
                low(SLOTS - 1, TURNS - 1)
            if half_out:
                half_out(False, TURNS, False)

        block = ctx.enter_context(nc.Block())

        def chunks(width):
            step = 1024 // width
            return [(e, min(ES, e + step)) for e in range(0, ES, step)]

        UG_CHUNKS, WD_CHUNKS = chunks(HID), chunks(D)
        staged = [(kind, e0, e1) for kind in ("uA", "gA", "uB", "gB") for e0, e1 in UG_CHUNKS] \
            + [("d", e0, e1) for e0, e1 in WD_CHUNKS]

        @block.sync
        def _(sp):
            def load(dst, src, name):
                sp.dma_start(dst, src).then_inc(S[name], 16)

            def load_stage(i):
                kind, e0, e1 = staged[i]
                if i >= STAGES:
                    sp.wait_ge(S["stage_free"], i - STAGES + 1)
                src, width = {"uA": (wuA_in, HID), "gA": (wgA_in, HID), "uB": (wuB_in, HID), "gB": (wgB_in, HID),
                              "d": (wd, D)}[kind]
                load(stage[i % STAGES][:, 0:(e1 - e0) * width], src[:, e0 * width:e1 * width], f"stage{i % STAGES}_in")

            load(idx_sb[:, :], tokens, "idx_in")
            load(ident[:, :], ident_in, "loads_ffn")
            load(bd_raw, bd, "loads_ffn")
            load(wbig[0], wq_big, "loads_big")
            load(wbig[1], wk_big, "loads_big")
            load(bo_row[DB:DB + 1, :], bout_big, "loads_big")
            for i in range(STAGES):
                load_stage(i)
            load(conv_sb[:, :, :], conv_w, "loads_tok")
            load(patch_sb[:, :, :], patches[0], "patches_in")
            load(conv_bA[:, :], conv_b[0:P, :], "loads_tok")
            load(conv_bB[:, :], conv_b[P:D, :], "loads_tok")
            sp.wait_ge(S["mm_big"], 2)
            load(wbig[0], wv_big, "loads_big")
            load(wbig[1][:, 0:KQ * D], wout_big, "loads_big")
            for i in range(STAGES, len(staged)):
                load_stage(i)
            for w, a, b in ((wq, wqA, wqB), (wk, wkA, wkB), (wv, wvA, wvB), (wo, woA, woB)):
                load(a[:, :], w[0:P, :], "loads_tok")
                load(b[:, :], w[P:w.shape[0], :], "loads_tok")
            load(tB[DB:KB, :], tok_const, "loads_tok")
            load(ioB[DB:DB + 1, :], tok_const[0:1, :], "loads_tok")
            load(pw_sb[:, :], post_w, "loads_txt")
            load(red_sb[:, :, :], reduce_w, "loads_txt")
            load(gwA[:, :], gate_w[0:P, :], "loads_txt")
            load(gwB[:, :], gate_w[P:D + 1, :], "loads_txt")
            load(bias_sb[:, :], bias.partition_broadcast(P), "loads_txt")
            load(bu_sb[:, :], bu, "loads_txt")
            load(bg_sb[:, :], bg, "loads_txt")

            def load_patches(t):
                at(sp, "conv_done", t - 1, 1)
                src = patches[t] if isinstance(t, int) else patches[bass.ds(t, 1)].rearrange("a p k n -> (a p) k n")
                sp.dma_start(patch_sb[:, :, :], src).then_inc(S["patches_in"], 16)

            def store(it):
                at(sp, "o_ready", it, 3)
                sp.dma_start(out[bass.ds(it * BB, BB), IMG:SEQ, :].rearrange("b s d -> s b d"),
                             o_sb[:, 0:BB, :]).then_inc(S["out_stored"], 16)
                for j in range(BB):
                    sp.dma_start(out[bass.ds(it * BB + j, 1), 0:IMG, :].rearrange("b s d -> (b s) d"),
                                 o_sb[j * SLOT:j * SLOT + IMG, BB, :]).then_inc(S["out_stored"], 16)

            load_patches(1)
            with sp.Fori(0, TURNS - 2) as it:
                load_patches(it + 2)
                store(it)
            store(TURNS - 2)
            store(TURNS - 1)
            sp.wait_ge(S["out_stored"], 16 * (BB + 1) * TURNS)

        @block.gpsimd
        def _(pool):
            def gather(par, t0, t1, name):
                for t in range(t0, t1):
                    pool.indirect_dma_start(out=par[:, t - t0, :], out_offset=None, in_=params,
                                            in_offset=bass.IndirectOffsetOnAxis(ap=idx_sb[:, t:t + 1].bitcast(U32), axis=0))\
                        .then_inc(S[name], 16)

            def circuit(it):
                own = Chain(pool, S["pool_own"], it, POOL_CHAIN)

                def co(row, shape):
                    a = trig[:, row, bass.ds(it * BB, BB)]
                    for n in shape:
                        a = a.unsqueeze(1)
                    return a.to_broadcast([P, *shape, BB])

                def bc(ap, shape):
                    for n in shape:
                        ap = ap.unsqueeze(1)
                    return ap.to_broadcast([P, *shape, BB])

                def tt(out_, a, b, op):
                    own.mark(pool.tensor_tensor(out_, a, b, op))

                t6 = slice(0, NQ)
                for c, row in ((0, CP1), (1, SP1)):
                    tt(V1[:, c, :, :], trig[:, S1:S1 + NQ, bass.ds(it * BB, BB)],
                       trig[:, row:row + NQ, bass.ds(it * BB, BB)], ALU.mult)
                own.wait()
                for i in (0, 3):
                    own.mark(pool.tensor_copy(EA[:, 0, i, :], co(C1 + 5, [])))
                    own.mark(pool.memset(EA[:, 1, i, :], 0.0))
                for i in (1, 2):
                    for c in range(2):
                        own.mark(pool.tensor_copy(EA[:, c, i, :], V1[:, c, 5, :]))
                own.wait()
                src, dst, n = EA, EB, 4
                for k in (4, 3, 2):
                    hn = n // 2
                    for c in range(2):
                        o = dst[:, c, 0:2 * n, :].rearrange("p (a r) t -> p a r t", r=hn)[:, 0:4:3]
                        tt(o, src[:, c, 0:n, :].rearrange("p (b r) t -> p b r t", b=2), co(C1 + k, [2, hn]), ALU.mult)
                    for c, x in ((0, X0), (1, X1)):
                        for cc in range(2):
                            tt(x[:, cc, 0:n, :], src[:, cc, 0:n, :], bc(V1[:, c, k, :], [n]), ALU.mult)
                    own.wait()
                    for c, op, other in ((0, ALU.subtract, 1), (1, ALU.add, 0)):
                        for b in range(2):
                            o0 = n if b == 0 else hn
                            tt(dst[:, c, o0:o0 + hn, :], X0[:, c, b * hn:(b + 1) * hn, :],
                               X1[:, other, b * hn:(b + 1) * hn, :], op)
                    own.wait()
                    src, dst, n = dst, src, 2 * n
                c0, c1 = co(C1, []), co(C1 + 1, [])
                v = lambda c, k: V1[:, c, k, :]
                tt(GG[:, 0, 0, :], c0, c1, ALU.mult)
                own.mark(pool.memset(GG[:, 1, 0, :], 0.0))
                for c in range(2):
                    tt(GG[:, c, 1, :], c0, v(c, 1), ALU.mult)
                    tt(GG[:, c, 3, :], c1, v(c, 0), ALU.mult)
                for c in range(2):
                    tt(X0[:, c, 0, :], v(0, 0), v(c, 1), ALU.mult)
                    tt(X1[:, c, 0, :], v(1, 0), v(c, 1), ALU.mult)
                own.wait()
                tt(GG[:, 0, 2, :], X0[:, 0, 0, :], X1[:, 1, 0, :], ALU.subtract)
                tt(GG[:, 1, 2, :], X0[:, 1, 0, :], X1[:, 0, 0, :], ALU.add)
                own.wait()
                for g, x in ((0, X0), (1, X1)):
                    for c in range(2):
                        for b0 in range(2):
                            gg = GG[:, g, 2 * b0:2 * b0 + 2, :].unsqueeze(2).to_broadcast([P, 2, 16, BB])
                            tt(x[:, c, 32 * b0:32 * b0 + 32, :].rearrange("p (a r) t -> p a r t", a=2),
                               src[:, c, 0:32, :].rearrange("p (a r) t -> p a r t", a=2), gg, ALU.mult)
                own.wait()
                for c, op, other in ((0, ALU.subtract, 1), (1, ALU.add, 0)):
                    for p5 in range(2):
                        for b0 in range(2):
                            p0 = b0 ^ p5
                            pick = lambda x, cc, b: x[:, cc, 32 * b + p5:32 * b + 32:2, :]
                            tt(pick(ST, c, p0), pick(X0, c, b0), pick(X1, other, b0), op)
                own.wait()
                for k in range(NQ):
                    flat = lambda x: x[:, :, :, :].rearrange("p c s t -> p (c s) t")
                    tt(flat(X0), flat(ST), co(C2 + k, [2 * NS]), ALU.mult)
                    tt(flat(X1), flat(ST), co(S2 + k, [2 * NS]), ALU.mult)
                    own.wait()
                    half = lambda x, b: x[:, :, :, :].rearrange("p c (l b r) t -> p (c l) b (r t)", l=1 << k, b=2)[:, :, b]
                    tt(half(ST, 0), half(X0, 0), half(X1, 1), ALU.subtract)
                    tt(half(ST, 1), half(X0, 1), half(X1, 0), ALU.add)
                    own.wait()
                for k in range(NQ):
                    L, R = 1 << k, NS >> (k + 1)
                    one = lambda x, c: x[:, c, :, :].rearrange("p (l b r) t -> p l b r t", l=L, b=2)[:, :, 1]
                    for c in range(2):
                        for x, row in ((X0, CP2), (X1, SP2)):
                            o = x[:, c, 0:32, :].rearrange("p (l r) t -> p l r t", l=L)
                            tt(o, one(ST, c), co(row + k, [L, R]), ALU.mult)
                    own.wait()
                    for c, op, other in ((0, ALU.subtract, 1), (1, ALU.add, 0)):
                        tt(one(ST, c), X0[:, c, 0:32, :].rearrange("p (l r) t -> p l r t", l=L),
                           X1[:, other, 0:32, :].rearrange("p (l r) t -> p l r t", l=L), op)
                    own.wait()
                at(pool, "prodT_done", it, RB, 0)
                pt = prods[:, :, :].rearrange("p t n -> p n t")
                stf = ST[:, :, :, :].rearrange("p c s t -> p (c s) t")
                tt(pt[:, 0:2 * NS, :], stf, stf, ALU.mult)
                for k in range(NQ - 1):
                    L, R = 2 << k, NS >> (k + 2)
                    for b in range(2):
                        w = ST[:, :, :, :].rearrange("p c (l q r) t -> p (c l) q r t", l=1 << k, q=4)
                        base = 2 * NS + NS * k
                        o = pt[:, base:base + NS, :].rearrange("p (l q r) t -> p l q r t", l=L, q=2)
                        tt(o[:, :, b], w[:, :, b], w[:, :, 3 - b], ALU.mult)
                for c in range(2):
                    for d in range(2):
                        for b in range(2):
                            w = ST[:, c, :, :].rearrange("p (a b m d) t -> p a b m d t", a=2, b=2, m=8)
                            base = 2 * NS + NS * (NQ - 1) + 32 * c + 16 * d + 8 * b
                            ins = pool.tensor_tensor(pt[:, base:base + 8, :], w[:, 0, b, :, d], w[:, 1, 1 - b, :, 1 - d], ALU.mult)
                            if (c, d, b) == (1, 1, 1):
                                own.wait()
                                ins.then_inc(S["prods_ready"], 1)
                            else:
                                own.mark(ins)
                pool.wait_ge(S["prods_ready"], it + 1)
                assert own.n == POOL_CHAIN, f"POOL_CHAIN = {own.n}"

            pool.wait_ge(S["idx_in"], 16)
            gather(par_early, 0, BB, "par_first_in")
            gather(par_early[:, BB:EARLY], BB, EARLY, "par_in")
            for buf in (pimg[:, :, :], wtok[:, :, :].bitcast(F32), kdiag[:, :, :, :], yT[:, BIGW:2 * FFPAD]):
                pool.memset(buf, 0.0).then_inc(S["pool_setup"], 1)
            for buf in (ev[:, :, NQ:NQ + 1], xn[:, :, D:D + 1]):
                pool.memset(buf, 1.0).then_inc(S["pool_setup"], 1)
            for buf in (sbias[:, :, E:E + 4], gsum[:, :, G:G + 4]):
                pool.memset(buf, SENTINEL).then_inc(S["pool_setup"], 1)
            pool.memset(wfull[:, :, E:ES], 1.0).then_inc(S["consts_ready"], 1)
            pool.wait_ge(S["trig_ready"], 1)
            circuit(0)
            pool.wait_ge(S["trig_ready"], 2)
            circuit(1)
            pool.wait_ge(S["mm_big"], 4)
            gather(par_late, EARLY, NB, "par_in")
            pool.wait_ge(S["trig_ready"], 4)
            with pool.Fori(2, TURNS) as it:
                circuit(it)

        @block.scalar
        def _(act):
            def copy(dst, src, name):
                nc.scalar.copy(dst, src).then_inc(S[name], 1)

            def sines(dst, src, n):
                act.wait_ge(S["trig_raw"], n)
                nc.scalar.activation(dst, src.rearrange("p (a t) -> p a t", t=dst.shape[2]), ACT.Sin, scale=TWO_PI)\
                  .then_inc(S["trig_ready"], 1)

            def angles():
                for i in range(2):
                    rows = slice(i * NTRIG // 2, (i + 1) * NTRIG // 2)
                    sines(trig[:, rows, EARLY:NB], round_late, 3 + i)

            for i in range(EARLY // BB):
                sines(trig[:, :, i * BB:(i + 1) * BB], round_early[i], 1 + i)
            act.wait_ge(S["loads_ffn"], 32)
            for dst, a, b in ((bd_h[:, :], 0, P), (bd_l[:, :], 0, P), (bd_b[:, 0:DB], P, D), (bd_b[:, DB:P], P, D)):
                copy(dst, bd_raw[:, a:b], "stage_high")
            for i, (kind, e0, e1) in enumerate(staged):
                act.wait_ge(S[f"stage{i % STAGES}_in"], 16 * (i // STAGES + 1))
                raw = stage[i % STAGES]
                if kind == "d":
                    r = raw[:, 0:(e1 - e0) * D].rearrange("p (e d) -> p e d", d=D)
                    copy(wd_h[:, e0:e1, :], r[:, :, 0:P], "stage_high")
                    copy(wd_b[:, e0:e1, 0:DB], r[:, :, P:D], "stage_high")
                else:
                    dst = {"uA": wu_h, "gA": wg_h, "uB": wu_b, "gB": wg_b}[kind]
                    r = raw[:, 0:(e1 - e0) * HID].rearrange("p (e d) -> p e d", d=HID)
                    copy(dst[:, e0:e1, :], r, "stage_high")
            act.wait_ge(S["loads_tok"], 16 * 13)
            act.wait_ge(S["loads_txt"], 16 * 7)
            act.wait_ge(S["consts_ready"], 1)

            def front(s, turn, par, own, busy):
                if s == -1:
                    at(act, "tproj_done", turn, 1)
                    for j in range(4):
                        copy(kdiag[32 * j:32 * j + 32, :, j, :],
                             b6[32 * j:32 * j + 32, 0:HT * P].rearrange("p (t k) -> p t k", t=HT), "kdiag_ready")
                if s == 4:
                    for t in range(HT):
                        at(act, "iprob_sub", turn, HT, t + 1)
                        nc.scalar.activation(iprob[:, 4 * t:4 * t + 4, :], iprob[:, 4 * t:4 * t + 4, :], ACT.Exp, scale=HD ** -0.5)\
                          .then_inc(S["iprob_exp"], 1)
                if s in (5, 6):
                    r, b = (0, b5) if s == 5 else (2, b7)
                    at(act, "prodT_done", turn, RB, r + 1)
                    copy(prodT[:, r, :, :], b[:, :].rearrange("p (t n) -> p t n", t=BB), "prodT_act")
                if s == 7:
                    at(act, "zx_done", turn, 1)
                    copy(zxT, b5[0:2 * NQ, :], "zxT_ready")
                if s == 9:
                    at(act, "evT_done", turn, 1)
                    copy(evT, b7[0:NQ + 1, :], "evT_ready")
                if s == 11:
                    at(act, "iprobT_done", turn, 1)
                    for t, b in ((0, b5), (2, b7)):
                        copy(iprobT[:, 4 * t:4 * t + 4, :], b[:, :].rearrange("p (h q) -> p h q", h=4), "iprobT_act")
                if s == 13:
                    at(act, "ioT_done", turn, 1)
                    copy(ioA, b5[:, 0:P], "ioA_ready")
                if s == 16:
                    at(act, "xT_done", turn, TILES, BB)
                    copy(xTA[:, :, 0:TXT], b5[:, :].rearrange("p (b q) -> p b q", b=BB), "xT_act")
                    copy(xTB[:, :, 0:TXT], b7[0:DB + 1, :].rearrange("p (b q) -> p b q", b=BB), "xT_act")
                if s == 18:
                    for n, y_, b, rows in ((1, yA, b5, P), (2, yB, b7, DB + 1)):
                        at(act, "y_done", turn, 4, n)
                        copy(y_[:, :, 0:TXT], b[0:rows, :].rearrange("p (b q) -> p b q", b=BB), "y_act")
                if s == 20:
                    at(act, "nbias_ready", turn, 1)
                    for t in range(TILES):
                        src = b6[:, t * SEQ:(t + 1) * SEQ] if t < 3 else b7[:, (t - 3) * SEQ:(t - 2) * SEQ]
                        nc.scalar.activation(prob[:, t, :], src, ACT.Exp, bias=nbias[:, t:t + 1], scale=0.125,
                                             accum_out=asum[:, t:t + 1]).then_inc(S["prob_ready"], 1)
                if s == 21:
                    at(act, "pT_done", turn, 1)
                    copy(pTA[:, :, 0:TXT], b5[:, :].rearrange("p (b q) -> p b q", b=BB), "pT_act")
                    copy(pTA[:, :, TXT:SPAN], b7[:, 0:P].rearrange("p (b q) -> p b q", b=BB), "pT_act")
                    copy(pTB[:, :, TXT:SPAN], b7[:, P:2 * P].rearrange("p (b q) -> p b q", b=BB), "pT_act")
                if s == 22:
                    at(act, "z_done", turn, 2, 1)
                    three = b5[:, 0:3 * SPAN].rearrange("p (b s) -> p b s", b=3)
                    copy(zA[:, 0:3 * TXT].rearrange("p (b s) -> p b s", b=3), three[:, :, 0:TXT], "z_act")
                    copy(zA[:, BB * TXT:BB * TXT + 3 * SLOT].rearrange("p (b s) -> p b s", b=3), three[:, :, TXT:SPAN], "z_act")
                if s == 26:
                    at(act, "x2_done", turn, 1)
                    copy(x2A[:, 0:BB * TXT], b5[:, :], "x2_act")
                    copy(x2B[:, 0:BB * TXT], b7[0:DB + 1, :], "x2_act")
                if s == 28:
                    at(act, "lsub_ready", turn, 1)
                    nc.scalar.activation(lg[:, :, :], lg[:, :, :], ACT.Exp).then_inc(S["lexp_ready"], 1)
                if s == 33:
                    at(act, "wT_done", turn, 1)
                    k = BB * TXT - HALF
                    copy(w_hl[par][0][:, :], b5[0:WR, 0:HALF], "w_ready")
                    copy(w_hl[par][1][:, 0:k], b5[0:WR, HALF:BB * TXT], "w_ready")
                    copy(w_hl[par][1][:, k:HALF], b6[0:WR, 0:HALF - k], "w_ready")

            def late(s, turn, par, own):
                if s in (14, 24):
                    src = h if s == 14 else h2[par]
                    at(act, "nmr_ready", turn, 2, 1 if s == 14 else 2)
                    for t in range(0, BB) if s == 14 else (2, 3, 4):
                        nc.scalar.activation(xn[:, t, 0:D], src[:, t, :], ACT.Identity, bias=nmr[:, t:t + 1],
                                             scale=rstd[:, t:t + 1]).then_inc(S["xn_act"], 1)
                if s in (26, 27):
                    if s == 26:
                        at(act, "x2_act", turn, 2)
                        at(act, "x2_dve", turn, 2)
                    hf = s - 26
                    c = slice(hf * HALF, (hf + 1) * HALF)
                    copy(x_h[par][hf][:, :], x2A[:, c], "high_ready")
                    copy(xb_h[par][hf][0:DB, :], x2B[0:DB, c], "high_ready")
                    copy(xb_h[par][hf][DB:P, :], x2B[0:DB, c], "high_ready")

            def experts(s, turn, par, first):
                e = s % ES
                at(act, "u_done", turn, SLOTS, s + 1)
                at(act, "gated_ready", turn, SLOTS, s)
                nc.scalar.activation(sl[:, :], UP[:, 0:HALF], ACT.Silu, bias=bu_sb[:, e:e + 1]).then_inc(S["sl_ready"], 1)
                at(act, "act_ready", turn, SLOTS, s + 1)
                at(act, "down_done", turn, SLOTS, s - 1)
                copy(a_h[:, s % 2, :], act_w[:, :], "a_high_ready")

            def half_out(is_first_half, turn, first):
                if is_first_half:
                    at(act, "down_low_done", turn, SLOTS, ES)
                    if not first:
                        at(act, "out_stored", turn, 16 * (BB + 1), 0)
                    copy(yTA[:, 0:HALF], YA[:, 0:HALF], "ya_ready")
                else:
                    at(act, "down_low_done", turn, SLOTS, 0)
                    k = BB * TXT - HALF
                    copy(yTA[:, HALF:BB * TXT], YA[:, 0:k], "ya_ready")
                    copy(yTA[:, BB * TXT:FFPAD].rearrange("p (b q) -> p b q", b=BB)[:, :, 0:IMG],
                         YA[:, k:HALF].rearrange("p (b q) -> p b q", b=BB), "ya_ready")

            turns(act, lambda turn: None, front, experts, late, half_out=half_out, angles=angles)

        @block.vector
        def _(dve):
            v = nc.vector
            setup = Chain(dve, S["dve_setup"])
            highs = 4

            def low_parts(i, kind, e0, e1):
                raw = stage[i % STAGES]
                dve.wait_ge(S["stage_high"], highs)
                if kind == "d":
                    r = raw[:, 0:(e1 - e0) * D].rearrange("p (e d) -> p e d", d=D)
                    setup.mark(v.tensor_tensor(wd_l[:, e0:e1, :], r[:, :, 0:P], wd_h[:, e0:e1, :].bitcast(F32), ALU.subtract))
                    v.tensor_tensor(wd_b[:, e0:e1, DB:P], r[:, :, P:D], wd_b[:, e0:e1, 0:DB].bitcast(F32), ALU.subtract)\
                     .then_inc(S["stage_free"], 1)
                    return
                r = raw[:, 0:(e1 - e0) * HID].rearrange("p (e d) -> p e d", d=HID)
                if kind in ("uA", "gA"):
                    hi, lo = (wu_h, wu_l) if kind == "uA" else (wg_h, wg_l)
                    v.tensor_tensor(lo[:, e0:e1, :], r, hi[:, e0:e1, :].bitcast(F32), ALU.subtract).then_inc(S["stage_free"], 1)
                else:
                    low = (wu_b if kind == "uB" else wg_b)[DB:P, e0:e1, :]
                    v.tensor_tensor(low, r[DB:P], low.bitcast(F32), ALU.subtract).then_inc(S["stage_free"], 1)

            def angles(par, t0, rounded, parts, chain, read=0):
                n = par.shape[1]
                pv = par.rearrange("p t (l q k) -> p l k q t", l=3, k=2)
                half, full = 1 / (4 * np.pi), 1 / (2 * np.pi)
                for row, layer, kd, scale, lead in (
                        (C1, 0, 0, half, .25), (S1, 0, 0, half, 0.), (CP1, 0, 1, full, .25), (SP1, 0, 1, full, 0.),
                        (C2, 1, 0, half, .25), (S2, 1, 0, half, 0.), (CP2, 1, 1, full, .25), (SP2, 1, 1, full, 0.),
                        (C3, 2, 0, full, .25), (S3, 2, 0, full, 0.)):
                    chain.mark(v.tensor_scalar(trig[:, row:row + NQ, t0:t0 + n], pv[:, layer, kd], float(scale), lead, ALU.mult, ALU.add))
                chain.wait()
                for i in range(parts):
                    tf = trig[:, i * NTRIG // parts:(i + 1) * NTRIG // parts, t0:t0 + n]
                    r = rounded.rearrange("p (a t) -> p a t", t=n)
                    if read:
                        dve.wait_ge(S["trig_ready"], read + i)
                    chain.link(v.tensor_scalar(r, tf, ROUND, None, ALU.add))
                    chain.link(v.tensor_scalar(r, r, ROUND, None, ALU.subtract))
                    v.tensor_tensor(r, tf, r, ALU.subtract).then_inc(S["trig_raw"], 1)

            dve.wait_ge(S["par_first_in"], 16 * BB)
            angles(par_early[:, 0:BB], 0, round_early[0], 1, setup)
            dve.wait_ge(S["par_in"], 16 * (EARLY - BB))
            angles(par_early[:, BB:EARLY], BB, round_early[1], 1, setup)
            dve.wait_ge(S["loads_ffn"], 32)
            setup.mark(v.tensor_tensor(ident2[:, :], ident[:, 0:DB], ident[:, DB:P], ALU.add))
            setup.mark(v.tensor_tensor(sel[:, 0:ES], ident[0:WR, 0:ES], ident[0:WR, WR - ES:WR], ALU.add))
            dve.wait_ge(S["stage_high"], 4)
            for dst, a, b in ((bd_l[:, :], 0, P), (bd_b[:, DB:P], P, D)):
                setup.mark(v.tensor_tensor(dst, bd_raw[:, a:b], dst.bitcast(F32), ALU.subtract))
            dve.wait_ge(S["mm_big"], 2)
            v.tensor_copy(MA[:, :], bank[0][:, 0:D + 1]).then_inc(S["products_ready"], 1)
            v.tensor_copy(MB[:, :], bank[1][0:DB + 1, 0:D + 1]).then_inc(S["products_ready"], 1)
            for i, (kind, e0, e1) in enumerate(staged):
                if i == STAGES + 2:
                    dve.wait_ge(S["mm_big"], 4)
                    v.tensor_copy(OA[:, :], bank[2][:, 0:D]).then_inc(S["products_ready"], 1)
                    setup.link(v.tensor_copy(OB[:, :], bank[3][0:DB + 1, 0:D]))
                    v.tensor_tensor(OB[DB:DB + 1, :], OB[DB:DB + 1, :], bo_row[DB:DB + 1, :], ALU.add)\
                     .then_inc(S["products_ready"], 1)
                highs += 2 if kind == "d" else 1
                low_parts(i, kind, e0, e1)
            dve.wait_ge(S["stage_free"], len(staged))
            setup.wait()
            v.memset(spare[:, :], 0.0).then_inc(S["weights_ready"], 1)
            dve.wait_ge(S["loads_tok"], 16 * 13)
            dve.wait_ge(S["loads_txt"], 16 * 7)
            dve.wait_ge(S["consts_ready"], 1)

            def copy(dst, src, name):
                v.tensor_copy(dst, src).then_inc(S[name], 1)

            def carry_wait(own):
                own.mark(v.memset(spare[:, :], 0.0))

            def ln_stats(src, tiles, own):
                for t in tiles:
                    own.mark(v.bn_stats(stats[:, t, :], src[:, t, :]))

            def ln_variance(a, b, own):
                own.wait()
                carry_wait(own)
                for t in range(a, b):
                    own.mark(v.bn_aggr(mv[:, t, :], stats[:, t, :]))
                own.wait()
                own.link(v.tensor_scalar(vare[:, a:b], mv[:, a:b, 1], EPS, None, ALU.add))
                own.mark(v.tensor_scalar(nhalf[:, a:b], vare[:, a:b], -0.5, None, ALU.mult))

            def ln_root_start(a, b, own):
                root = rstd[:, a:b].bitcast(I32)
                own.wait()
                own.link(v.tensor_scalar(root, vare[:, a:b].bitcast(I32), 1, None, ALU.logical_shift_right))
                own.link(v.tensor_scalar(root, root, -1.0, RSQRT_MAGIC, ALU.mult, ALU.add))

            def ln_root_step(a, b, own):
                root = rstd[:, a:b]
                own.link(v.tensor_tensor(nt[:, a:b], root, root, ALU.mult))
                own.link(v.tensor_tensor(nt[:, a:b], nt[:, a:b], nhalf[:, a:b], ALU.mult))
                own.link(v.scalar_tensor_tensor(out=root, in0=nt[:, a:b], scalar=1.5, in1=root, op0=ALU.add, op1=ALU.mult))

            def ln_shift(a, b):
                v.scalar_tensor_tensor(out=nmr[:, a:b], in0=mv[:, a:b, 0], scalar=-1.0, in1=rstd[:, a:b],
                                       op0=ALU.mult, op1=ALU.mult).then_inc(S["nmr_ready"], 1)

            def ln_rows(src, tiles):
                for t in tiles:
                    v.tensor_scalar(xn[:, t, 0:D], src[:, t, :], mv[:, t, 0:1], rstd[:, t:t + 1],
                                    ALU.subtract, ALU.mult).then_inc(S["xn_dve"], 1)

            def top4(vals, n, own):
                carry_wait(own)
                for t in range(TILES):
                    own.mark(v.max(top8[:, t, :], vals[:, t, 0:n]))
                own.wait()
                own.mark(v.memset(top8[:, :, 4:8], SENTINEL))
                own.wait()
                carry_wait(own)
                for t in range(TILES):
                    own.mark(v.match_replace(out=picked[:, t, 0:n + 4], in_to_replace=top8[:, t, :],
                                             in_values=vals[:, t, 0:n + 4], imm_value=PICKED))
                own.wait()
                own.link(v.tensor_scalar(keep[:, :, 0:n], picked[:, :, 0:n], PICKED, None, ALU.is_equal))

            heads4 = lambda b: b[:, :].rearrange("p (h k) -> p h k", h=4)
            four = lambda t: slice(4 * t, 4 * t + 4)
            groups = sbias[:, :, 0:E].rearrange("p t (g i) -> p t g i", i=2)

            def front(s, turn, par, own, busy):
                if s == -2:
                    at(dve, "conv_done", turn, 1)
                    v.tensor_scalar(tA[:, :], b5[:, 0:P], conv_bA[:, 0:1], None, ALU.add).then_inc(S["t_ready"], 1)
                    v.tensor_scalar(tB[0:DB, :], b5[0:DB, P:2 * P], conv_bB[:, 0:1], None, ALU.add).then_inc(S["t_ready"], 1)
                if s == -1:
                    at(dve, "tproj_done", turn, 1)
                    copy(qT, b5[:, 0:HT * P], "qv_ready")
                    copy(v_sb, b7[:, 0:D], "qv_ready")
                if s == 1:
                    for t in (0, 1):
                        at(dve, "iscore_done", turn, HT, t + 1)
                        own.mark(v.tensor_reduce(imax[:, four(t)], heads4(b5 if t == 0 else b6), AX.X, ALU.max))
                if s in (5, 6):
                    r = 1 if s == 5 else 3
                    at(dve, "prodT_done", turn, RB, r + 1)
                    copy(prodT[:, r, :, :], b6[:, :].rearrange("p (t n) -> p t n", t=BB), "prodT_dve")
                if s == 8:
                    at(dve, "expval_done", turn, 1)
                    zx = b7[:, 0:BB * 2 * NQ].rearrange("p (t c q) -> p c t q", t=BB, c=2)
                    for c, row in ((0, C3), (1, S3)):
                        own.mark(v.tensor_tensor(evt[:, c], zx[:, c],
                                                 trig[:, row:row + NQ, bass.ds(turn * BB, BB)].rearrange("p q t -> p t q"), ALU.mult))
                    own.wait()
                    v.tensor_tensor(ev[:, :, 0:NQ], evt[:, 0], evt[:, 1], ALU.subtract).then_inc(S["ev_ready"], 1)
                if s == 10:
                    at(dve, "emb_done", turn, 1)
                    for i, b in ((0, b5), (1, b6)):
                        copy(h[:, 2 * i:2 * i + 2, :], b[:, 0:2 * D].rearrange("p (t d) -> p t d", t=2), "h_ready")
                if s == 11:
                    at(dve, "iprobT_done", turn, 1)
                    copy(iprobT[:, 4:8, :], heads4(b6), "iprobT_dve")
                if s == 12:
                    at(dve, "ipv_done", turn, 1)
                    own.wait()
                    v.tensor_tensor(io.rearrange("p (h d) -> p h d", h=HEADS),
                                    b5[:, 0:D].rearrange("p (h d) -> p h d", h=HEADS),
                                    irec[:, :].unsqueeze(2).to_broadcast([P, HEADS, HD]), ALU.mult).then_inc(S["io_ready"], 1)
                if s == 13:
                    at(dve, "ioT_done", turn, 1)
                    copy(ioB[0:DB, :], b6[0:DB, 0:P], "ioB_ready")
                if s == 14:
                    at(dve, "iout_done", turn, 1)
                    copy(h[:, BB, :], b7[:, 0:D], "h_ready")
                if s == 18:
                    at(dve, "xT_done", turn, TILES)
                    copy(xTA[:, :, TXT:SPAN], b6[:, 0:P].rearrange("p (b q) -> p b q", b=BB), "xT_dve")
                    copy(xTB[:, :, TXT:SPAN], b6[0:DB + 1, P:2 * P].rearrange("p (b q) -> p b q", b=BB), "xT_dve")
                    at(dve, "y_done", turn, 4)
                    copy(yA[:, :, TXT:SPAN], b6[:, 0:P].rearrange("p (b q) -> p b q", b=BB), "y_dve")
                    copy(yB[:, :, TXT:SPAN], b6[0:DB + 1, P:2 * P].rearrange("p (b q) -> p b q", b=BB), "y_dve")
                if s == 19:
                    at(dve, "ascore_done", turn, 2, 1)
                    own.mark(v.tensor_reduce(nmax[:, 0:3], b6[:, 0:3 * SEQ].rearrange("p (t k) -> p t k", t=3),
                                             AX.X, ALU.max, negate=True))
                if s == 20:
                    for b in range(BB):
                        at(dve, "prob_ready", turn, TILES, b + 1)
                        v.tensor_copy(pimg[:, b, b * SLOT:b * SLOT + IMG], prob[:, b, TXT:SEQ]).then_inc(S["pimg_ready"], 1)
                    at(dve, "prob_ready", turn, TILES)
                    for b in range(BB):
                        rows = slice(b * SLOT, (b + 1) * SLOT)
                        v.tensor_copy(pimg[rows, BB, b * SLOT:b * SLOT + IMG], prob[rows, BB, TXT:SEQ]).then_inc(S["pimg_ready"], 1)
                    own.mark(v.reciprocal(arec[:, :], asum[:, :]))
                if s == 21:
                    at(dve, "pT_done", turn, 1)
                    copy(pTB[:, :, 0:TXT], b6[:, :].rearrange("p (b q) -> p b q", b=BB), "pT_dve")
                if s == 22:
                    at(dve, "z_done", turn, 2)
                    three = b6[0:DB + 1, 0:3 * SPAN].rearrange("p (b s) -> p b s", b=3)
                    copy(zB[:, 0:3 * TXT].rearrange("p (b s) -> p b s", b=3), three[:, :, 0:TXT], "z_dve")
                    copy(zB[:, BB * TXT:BB * TXT + 3 * SLOT].rearrange("p (b s) -> p b s", b=3), three[:, :, TXT:SPAN], "z_dve")
                    for dst, rows, c in ((zA, P, 0), (zB, DB + 1, SPAN)):
                        copy(dst[:, 3 * TXT:BB * TXT], b7[0:rows, c:c + TXT], "z_dve")
                        copy(dst[:, FFPAD - SLOT:FFPAD], b7[0:rows, c + TXT:c + SPAN], "z_dve")
                if s == 23:
                    own.wait()
                    for t in range(TILES):
                        at(dve, "aout_done", turn, TILES, (2, 2, 4, 4, 5)[t])
                        b, c = ((b5, 0), (b5, D), (b6, 0), (b6, D), (b7, 0))[t]
                        v.scalar_tensor_tensor(out=h2[par][:, t, :], in0=b[:, c:c + D], scalar=arec[:, t:t + 1],
                                               in1=h[:, t, :], op0=ALU.mult, op1=ALU.add).then_inc(S["h2_ready"], 1)
                        if t in (1, 3, 4):
                            at(dve, "h2_ready", turn, TILES, t + 1)
                            ln_stats(h2[par], (t - 1, t) if t < BB else (t,), own)
                    ln_variance(0, TILES, own)
                    ln_root_start(0, TILES, own)
                if s == 26:
                    at(dve, "x2_done", turn, 1)
                    for dst, rows, c in ((x2A, P, 0), (x2B, DB + 1, P)):
                        v.tensor_copy(dst[:, BB * TXT:FF].rearrange("p (b q) -> p b q", b=BB),
                                      b6[0:rows, c:c + P].rearrange("p (b q) -> p b q", b=BB)[:, :, 0:IMG])\
                         .then_inc(S["x2_dve"], 1)

            def late(s, turn, par, own):
                if s in (1, 2):
                    if s == 1:
                        at(dve, "iscore_done", turn, HT)
                        own.link(v.tensor_reduce(imax[:, four(2)], heads4(b7), AX.X, ALU.max))
                    for t, b in ((0, b5),) if s == 1 else ((1, b6), (2, b7)):
                        v.tensor_tensor(iprob[:, four(t), :], heads4(b), imax[:, four(t)].unsqueeze(2).to_broadcast([P, 4, P]),
                                        ALU.subtract).then_inc(S["iprob_sub"], 1)
                if s in (5, 6, 7):
                    at(dve, "iprob_exp", turn, HT)
                    own.mark(v.tensor_reduce(isum[:, four(s - 5)], iprob[:, four(s - 5), :], AX.X, ALU.add))
                if s == 8:
                    own.wait()
                    own.mark(v.reciprocal(irec[:, :], isum[:, :]))
                if s == 10:
                    at(dve, "h_ready", turn, 3, 2)
                    ln_stats(h, (0, 1), own)
                if s == 11:
                    ln_stats(h, (2, 3), own)
                    ln_variance(0, BB, own)
                if s == 12:
                    ln_root_start(0, BB, own)
                    ln_root_step(0, BB, own)
                if s == 13:
                    ln_root_step(0, BB, own)
                    ln_root_step(0, BB, own)
                    ln_shift(0, BB)
                if s == 14:
                    at(dve, "h_ready", turn, 3)
                    ln_stats(h, (BB,), own)
                    ln_variance(BB, TILES, own)
                if s == 15:
                    ln_root_start(BB, TILES, own)
                    ln_root_step(BB, TILES, own)
                if s == 16:
                    for _ in range(2):
                        ln_root_step(BB, TILES, own)
                    ln_rows(h, (BB,))
                if s == 19:
                    at(dve, "ascore_done", turn, 2)
                    own.link(v.tensor_reduce(nmax[:, 3:5], b7[:, 0:2 * SEQ].rearrange("p (t k) -> p t k", t=2),
                                             AX.X, ALU.max, negate=True))
                    v.tensor_scalar(nbias[:, :], nmax[:, :], 0.125, None, ALU.mult).then_inc(S["nbias_ready"], 1)
                if s == 23:
                    for _ in range(2):
                        ln_root_step(0, TILES, own)
                if s == 24:
                    ln_root_step(0, TILES, own)
                    ln_shift(0, TILES)
                    ln_rows(h2[par], (0, 1))
                if s == 27:
                    at(dve, "gate_done", turn, 1)
                    lp = b5[:, 0:TILES * E].rearrange("p (t e) -> p t e", t=TILES)
                    own.link(v.tensor_reduce(lmax[:, :], lp, AX.X, ALU.max))
                    v.tensor_tensor(lg[:, :, :], lp, lmax[:, :].unsqueeze(2).to_broadcast([P, TILES, E]), ALU.subtract)\
                     .then_inc(S["lsub_ready"], 1)
                if s == 28:
                    at(dve, "lexp_ready", turn, 1)
                    own.link(v.tensor_reduce(lsum[:, :], lg[:, :, :], AX.X, ALU.add))
                    own.link(v.reciprocal(lsum[:, :], lsum[:, :]))
                    own.link(v.tensor_tensor(score[:, :, :], lg[:, :, :], lsum[:, :].unsqueeze(2).to_broadcast([P, TILES, E]), ALU.mult))
                    own.link(v.tensor_tensor(sbias[:, :, 0:E], score[:, :, :],
                                             bias_sb[:, :].unsqueeze(1).to_broadcast([P, TILES, E]), ALU.add))
                    own.mark(v.tensor_tensor(gsum[:, :, 0:G], groups[:, :, :, 0], groups[:, :, :, 1], ALU.add))
                    own.wait()
                    top4(gsum, G, own)
                if s == 29:
                    kept = keep[:, :, 0:G].unsqueeze(3).to_broadcast([P, TILES, G, 2])
                    own.mark(v.tensor_tensor(groups, groups, kept, ALU.mult))
                    own.link(v.tensor_scalar(drop[:, :, :], keep[:, :, 0:G], BIG, -BIG, ALU.mult, ALU.add))
                    own.mark(v.tensor_tensor(groups, groups, drop[:, :, :].unsqueeze(3).to_broadcast([P, TILES, G, 2]), ALU.add))
                if s == 30:
                    own.wait()
                    top4(sbias, E, own)
                if s == 31:
                    own.wait()
                    own.link(v.scalar_tensor_tensor(out=wfull[:, :, 0:E], in0=score[:, :, :], scalar=2.5, in1=keep[:, :, :],
                                                    op0=ALU.mult, op1=ALU.mult))
                    own.link(v.tensor_copy(wtok[:, :, 0:ES], wfull[:, :, :]))
                    v.tensor_tensor(wtok[:, :, WR - ES:WR], wfull[:, :, :], wtok[:, :, 0:ES].bitcast(F32), ALU.subtract)\
                     .then_inc(S["wtok_ready"], 1)
                if s in (27, 32):
                    hf = int(s == 32)
                    c = slice(hf * HALF, (hf + 1) * HALF)
                    at(dve, "high_ready", turn, 6, 3 * hf + 3)
                    v.tensor_tensor(x_l[par][hf][:, :], x2A[:, c], x_h[par][hf][:, :].bitcast(F32), ALU.subtract)\
                     .then_inc(S["split_ready"], 1)
                    v.tensor_tensor(xb_l[par][hf][:, :], x2B[0:DB, c], xb_h[par][hf][0:DB, :].bitcast(F32), ALU.subtract)\
                     .then_inc(S["split_ready"], 1)

            def low(s, turn):
                at(dve, "a_high_ready", turn, SLOTS, s + 1)
                at(dve, "down_low_done", turn, SLOTS, s - 1)
                v.tensor_tensor(a_l[:, s % 2, :], act_w[:, :], a_h[:, s % 2, :].bitcast(F32), ALU.subtract)\
                 .then_inc(S["a_low_ready"], 1)

            def experts(s, turn, par, first):
                if s == 4 and not first:
                    finish(turn - 1, 1 - par)
                e = s % ES
                at(dve, "g_done", turn, SLOTS, s + 1)
                at(dve, "sl_ready", turn, SLOTS, s + 1)
                v.scalar_tensor_tensor(out=gated[:, :], in0=GATE[:, 0:HALF], scalar=bg_sb[:, e:e + 1],
                                       in1=sl[:, :], op0=ALU.add, op1=ALU.mult).then_inc(S["gated_ready"], 1)
                at(dve, "w_done", turn, SLOTS, s + 1)
                at(dve, "gated_ready", turn, SLOTS, s + 1)
                v.tensor_tensor(act_w[:, :], gated[:, :], WEIGHT[:, 0:HALF], ALU.mult).then_inc(S["act_ready"], 1)

            def half_out(is_first_half, turn, first):
                if is_first_half:
                    at(dve, "down_low_done", turn, SLOTS, ES)
                    if not first:
                        at(dve, "out_stored", turn, 16 * (BB + 1), 0)
                    copy(yTB[:, 0:HALF], YB[:, 0:HALF], "yb_ready")
                else:
                    at(dve, "down_low_done", turn, SLOTS, 0)
                    k = BB * TXT - HALF
                    copy(yTB[:, HALF:BB * TXT], YB[:, 0:k], "yb_ready")
                    copy(yTB[:, BB * TXT:FFPAD].rearrange("p (b q) -> p b q", b=BB)[:, :, 0:IMG],
                         YB[:, k:HALF].rearrange("p (b q) -> p b q", b=BB), "yb_ready")

            def finish(turn, par):
                at(dve, "fin_done", turn, 1)
                for i, b in enumerate((b5, b6, b7)):
                    n = 2 if i < 2 else 1
                    v.tensor_tensor(o_sb[:, 2 * i:2 * i + n, :], b[:, 0:n * D].rearrange("p (t d) -> p t d", t=n),
                                    h2[par][:, 2 * i:2 * i + n, :], ALU.add).then_inc(S["o_ready"], 1)

            def angles_late():
                dve.wait_ge(S["par_in"], 16 * (NB - BB))
                angles(par_late, EARLY, round_late, 2, setup, read=2)

            turns(dve, lambda turn: Chain(dve, S["dve_own"], turn, DVE_FRONT_CHAIN, "DVE_FRONT_CHAIN"),
                  front, experts, late, low, half_out, angles_late)
            finish(TURNS - 1, 1)

        @block.tensor
        def _(pe):
            mm = nc.tensor.matmul

            def tr(dst, src, n=P):
                return nc.tensor.transpose(dst, src, ident[0:n, 0:n])

            for first, w1 in ((0, D + 1), (2, D)):
                pe.wait_ge(S["loads_big"], 48 if first == 0 else 80)
                l = wbig[0].rearrange("p (k n) -> p k n", k=KQ)
                r = wbig[1][:, 0:KQ * w1].rearrange("p (k n) -> p k n", k=KQ)
                for i, (a, b) in enumerate(((0, P), (P, D + 1))):
                    for k in range(KQ):
                        ins = mm(bank[first + i][0:b - a, 0:w1], l[:, k, a:b], r[:, k, :], start=(k == 0), stop=(k == KQ - 1))
                    ins.then_inc(S["mm_big"], 1)
            pe.wait_ge(S["products_ready"], 4)
            pe.wait_ge(S["loads_tok"], 16 * 13)
            pe.wait_ge(S["loads_txt"], 16 * 7)
            pe.wait_ge(S["loads_ffn"], 32)
            pe.wait_ge(S["consts_ready"], 1)
            pe.wait_ge(S["weights_ready"], 1)
            pe.sem_inc(S["prodT_done"], 1)

            def front(s, turn, par, own, busy):
                if s == -2:
                    at(pe, "patches_in", turn, 16)
                    for c, lo, hi in ((0, 0, P), (P, P, D)):
                        for k in range(KP):
                            ins = mm(b5[0:hi - lo, c:c + P], conv_sb[:, k, lo:hi], patch_sb[:, k, :], start=(k == 0), stop=(k == KP - 1))
                    ins.then_inc(S["conv_done"], 1)
                if s == -1:
                    at(pe, "t_ready", turn, 2)
                    at(pe, "lsub_ready", turn, 1, 0)
                    for b, wa, wb in ((b5, wqA, wqB), (b6, wkA, wkB)):
                        for t in range(HT):
                            cols = slice(t * P, (t + 1) * P)
                            mm(b[:, cols], wa[:, cols], tA[:, :], start=True, stop=False)
                            mm(b[:, cols], wb[:, cols], tB[:, :], start=False, stop=True)
                    mm(b7[:, 0:D], tA[:, :], wvA[:, :], start=True, stop=False)
                    mm(b7[:, 0:D], tB[0:DB + 1, :], wvB[:, :], start=False, stop=True).then_inc(S["tproj_done"], 1)
                if s == 1:
                    at(pe, "qv_ready", turn, 2)
                    at(pe, "kdiag_ready", turn, 4)
                    at(pe, "w_ready", turn, 3, 0)
                    for t, b in enumerate((b5, b6, b7)):
                        mm(b[:, :], qT[:, t * P:(t + 1) * P], kdiag[:, t, :, :].rearrange("p h k -> p (h k)"),
                           start=True, stop=True).then_inc(S["iscore_done"], 1)
                if s == 5:
                    at(pe, "iprob_sub", turn, HT)
                    if isinstance(turn, int) and turn == 0:
                        at(pe, "ioA_ready", turn, 1)
                        at(pe, "ioB_ready", turn, 1)
                    at(pe, "prods_ready", turn, 1)
                    for r, b in enumerate((b5, b6, b7)):
                        if busy:
                            at(pe, "o_ready", turn - 2, 3, r + 1)
                        prod_rows(r, b)
                if s == 6:
                    at(pe, "prodT_dve", turn, 2, 1)
                    prod_rows(3, b6)
                if s == 7:
                    at(pe, "prodT_act", turn, 2)
                    at(pe, "prodT_dve", turn, 2)
                    for r in range(RB):
                        ins = mm(b5[0:2 * NQ, :], red_sb[:, r, :], prodT[:, r, :, :].rearrange("p t n -> p (t n)"),
                                 start=(r == 0), stop=(r == RB - 1))
                    ins.then_inc(S["zx_done"], 1)
                if s == 8:
                    at(pe, "zxT_ready", turn, 1)
                    for t in range(BB):
                        ins = mm(b7[:, t * 2 * NQ:(t + 1) * 2 * NQ], zxT[:, t * P:(t + 1) * P],
                                 ident[0:2 * NQ, 0:2 * NQ], start=True, stop=True)
                    ins.then_inc(S["expval_done"], 1)
                if s == 9:
                    at(pe, "ev_ready", turn, 1)
                    for t in range(BB):
                        ins = tr(b7[0:NQ + 1, t * P:(t + 1) * P], ev[:, t, :])
                    ins.then_inc(S["evT_done"], 1)
                if s == 10:
                    at(pe, "evT_ready", turn, 1)
                    for t in range(BB):
                        ins = mm((b5, b6)[t // 2][:, (t % 2) * D:(t % 2 + 1) * D], evT[:, t * P:(t + 1) * P], pw_sb[:, :],
                                 start=True, stop=True)
                    ins.then_inc(S["emb_done"], 1)
                if s == 11:
                    at(pe, "iprob_exp", turn, HT)
                    if not (isinstance(turn, int) and turn == 0):
                        at(pe, "h_ready", turn, 3, 2)
                    for t, b in enumerate((b5, b6, b7)):
                        for j in range(4):
                            ins = tr(b[:, j * P:(j + 1) * P], iprob[:, 4 * t + j, :])
                    ins.then_inc(S["iprobT_done"], 1)
                if s == 12:
                    at(pe, "iprobT_act", turn, 2)
                    at(pe, "iprobT_dve", turn, 1)
                    for hd in range(HEADS):
                        c = slice(hd * HD, (hd + 1) * HD)
                        ins = mm(b5[:, c], iprobT[:, hd, :], v_sb[:, c], start=True, stop=True)
                    ins.then_inc(S["ipv_done"], 1)
                if s == 13:
                    at(pe, "io_ready", turn, 1)
                    tr(b5[:, 0:P], io[:, 0:P])
                    tr(b6[0:DB, 0:P], io[:, P:D]).then_inc(S["ioT_done"], 1)
                if s == 14:
                    at(pe, "ioA_ready", turn, 1)
                    at(pe, "ioB_ready", turn, 1)
                    mm(b7[:, 0:D], ioA, woA[:, :], start=True, stop=False)
                    mm(b7[:, 0:D], ioB[:, :], woB[:, :], start=False, stop=True).then_inc(S["iout_done"], 1)
                if s == 16:
                    at(pe, "h_ready", turn, 3)
                    for t in range(BB):
                        at(pe, "xn_act", turn, 7, t + 1)
                        rows_up(t, b5[:, t * P:(t + 1) * P], b7[0:DB + 1, t * P:(t + 1) * P]).then_inc(S["xT_done"], 1)
                if s == 18:
                    at(pe, "xn_dve", turn, 3, 1)
                    rows_up(BB, b6[:, 0:P], b6[0:DB + 1, P:2 * P]).then_inc(S["xT_done"], 1)
                    at(pe, "xT_act", turn, 2)
                    query_key(slice(0, TXT), b5[:, :], b7[0:DB + 1, :])
                    at(pe, "xT_dve", turn, 2)
                    query_key(slice(TXT, SPAN), b6[:, 0:P], b6[0:DB + 1, P:2 * P])
                if s == 26:
                    for t in range(TILES):
                        at(pe, "xn_dve", turn, 3, t + 2) if t < 2 else at(pe, "xn_act", turn, 7, BB + t - 1)
                        oa, ob = (b5[:, t * P:(t + 1) * P], b7[0:DB + 1, t * P:(t + 1) * P]) if t < BB \
                            else (b6[:, 0:P], b6[0:DB + 1, P:2 * P])
                        ins = rows_up(t, oa, ob)
                    ins.then_inc(S["x2_done"], 1)
                if s == 19:
                    at(pe, "y_act", turn, 2)
                    at(pe, "y_dve", turn, 2)
                    for b in range(BB):
                        o = b6[:, b * SEQ:(b + 1) * SEQ] if b < 3 else b7[:, 0:SEQ]
                        mm(o, yA[:, b, 0:TXT], xTA[:, b, 0:SEQ], start=True, stop=False)
                        ins = mm(o, yB[:, b, 0:TXT], xTB[:, b, 0:SEQ], start=False, stop=True)
                        if b == 2:
                            ins.then_inc(S["ascore_done"], 1)
                    for b in range(BB):
                        o = b7[b * SLOT:(b + 1) * SLOT, SEQ:2 * SEQ]
                        mm(o, yA[:, b, TXT:SPAN], xTA[:, b, 0:SEQ], start=True, stop=False, tile_position=(0, b * SLOT))
                        ins = mm(o, yB[:, b, TXT:SPAN], xTB[:, b, 0:SEQ], start=False, stop=True, tile_position=(0, b * SLOT))
                    ins.then_inc(S["ascore_done"], 1)
                if s == 21:
                    at(pe, "prob_ready", turn, TILES)
                    if not (isinstance(turn, int) and turn == TURNS - 1):
                        at(pe, "t_ready", turn + 1, 2)
                    for t in range(BB):
                        tr(b5[:, t * P:(t + 1) * P], prob[:, t, 0:TXT])
                    tr(b7[:, 0:P], prob[:, BB, 0:TXT])
                    at(pe, "pimg_ready", turn, 2 * BB)
                    for t in range(BB):
                        tr(b6[:, t * P:(t + 1) * P], pimg[:, t, :])
                    tr(b7[:, P:2 * P], pimg[:, BB, :]).then_inc(S["pT_done"], 1)
                if s == 22:
                    at(pe, "pT_act", turn, 3)
                    at(pe, "pT_dve", turn, 1)
                    for lo, hi, three, col in ((0, P, b5, 0), (P, D + 1, b6, SPAN)):
                        for b in range(BB):
                            o = three[0:hi - lo, b * SPAN:(b + 1) * SPAN] if b < 3 else b7[0:hi - lo, col:col + SPAN]
                            mm(o, xn[:, b, lo:hi], pTA[:, b, :], start=True, stop=False)
                            ins = mm(o, xn[:, BB, lo:hi], pTB[:, b, :], start=False, stop=True)
                        ins.then_inc(S["z_done"], 1)
                if s == 23:
                    at(pe, "z_act", turn, 2)
                    at(pe, "z_dve", turn, 6)
                    for t in range(TILES):
                        b, c = ((b5, 0), (b5, D), (b6, 0), (b6, D), (b7, 0))[t]
                        q = slice(t * P, (t + 1) * P)
                        mm(b[:, c:c + D], zA[:, q], OA[:, :], start=True, stop=False)
                        mm(b[:, c:c + D], zB[:, q], OB[:, :], start=False, stop=True).then_inc(S["aout_done"], 1)
                if s == 27:
                    at(pe, "x2_act", turn, 2)
                    at(pe, "x2_dve", turn, 2)
                    for t in range(TILES):
                        c = slice(t * P, (t + 1) * P)
                        mm(b5[:, t * E:(t + 1) * E], x2A[:, c], gwA[:, :], start=True, stop=False)
                        ins = mm(b5[:, t * E:(t + 1) * E], x2B[:, c], gwB[:, :], start=False, stop=True)
                    ins.then_inc(S["gate_done"], 1)
                if s == 33:
                    at(pe, "wtok_ready", turn, 1)
                    if not (isinstance(turn, int) and turn == TURNS - 1):
                        at(pe, "qv_ready", turn + 1, 2)
                        at(pe, "kdiag_ready", turn + 1, 4)
                    for t in range(TILES):
                        o = b5[0:WR, t * P:(t + 1) * P] if t < BB else b6[0:WR, 0:P]
                        ins = mm(o, wtok[:, t, :].bitcast(F32), ident[:, :], start=True, stop=True)
                    ins.then_inc(S["wT_done"], 1)

            def rows_up(t, oa, ob):
                tr(oa, xn[:, t, 0:P])
                return tr(ob, xn[:, t, P:D + 1])

            def query_key(tokens, oa, ob):
                for o, lo, hi in ((oa, 0, P), (ob, P, D + 1)):
                    mm(o, MA[:, lo:hi], xTA[:, :, tokens], start=True, stop=False)
                    mm(o, MB[:, lo:hi], xTB[:, :, tokens], start=False, stop=True).then_inc(S["y_done"], 1)

            def prod_rows(r, b):
                for t in range(BB):
                    ins = tr(b[:, t * P:(t + 1) * P], prods[:, t, r * P:(r + 1) * P])
                ins.then_inc(S["prodT_done"], 1)

            def down(s, turn, par):
                e, hf = s % ES, s // ES
                if e == 0:
                    at(pe, "ya_ready", turn, 3, hf)
                    at(pe, "yb_ready", turn, 3, hf)
                    w = w_hl[par][hf][:, :]
                    mm(YA[:, 0:HALF], bd_h[:, :], w, start=True, stop=False)
                    mm(YA[:, 0:HALF], bd_l[:, :], w, start=False, stop=False)
                    mm(YB[:, 0:HALF], bd_b[:, :], w, start=True, stop=False)
                at(pe, "a_high_ready", turn, SLOTS, s + 1)
                high = a_h[:, s % 2, :]
                mm(YA[:, 0:HALF], wd_h[:, e, :], high, start=False, stop=False)
                mm(YA[:, 0:HALF], wd_l[:, e, :], high, start=False, stop=False)
                mm(YB[:, 0:HALF], wd_b[:, e, :], high, start=False, stop=False).then_inc(S["down_done"], 1)
                for k in (s - 1, s) if e == ES - 1 else (s - 1,) if e else ():
                    at(pe, "a_low_ready", turn, SLOTS, k + 1)
                    low = a_l[:, k % 2, :]
                    mm(YA[:, 0:HALF], wd_h[:, k % ES, :], low, start=False, stop=(k % ES == ES - 1))
                    mm(YB[:, 0:HALF], wd_b[:, k % ES, :], low, start=False, stop=(k % ES == ES - 1))\
                        .then_inc(S["down_low_done"], 1)

            def experts(s, turn, par, first):
                e, hf = s % ES, s // ES
                if s == 0:
                    at(pe, "high_ready", turn, 6)
                    at(pe, "split_ready", turn, 4)
                    at(pe, "w_ready", turn, 3)
                for o, h_, l_, b_, name, read in ((UP, wu_h, wu_l, wu_b, "u_done", "sl_ready"),
                                                  (GATE, wg_h, wg_l, wg_b, "g_done", "gated_ready")):
                    at(pe, read, turn, SLOTS, s)
                    o = o[:, 0:HALF]
                    mm(o, h_[:, e, :], x_h[par][hf][:, :], start=True, stop=False)
                    mm(o, l_[:, e, :], x_h[par][hf][:, :], start=False, stop=False)
                    mm(o, h_[:, e, :], x_l[par][hf][:, :], start=False, stop=False)
                    mm(o, b_[:, e, :], xb_h[par][hf][:, :], start=False, stop=False)
                    mm(o, b_[0:DB, e, :], xb_l[par][hf][:, :], start=False, stop=True).then_inc(S[name], 1)
                at(pe, "act_ready", turn, SLOTS, s)
                mm(WEIGHT[:, 0:HALF], sel[:, e:e + 1].to_broadcast([WR, P]), w_hl[par][hf][:, :], start=True, stop=True).then_inc(S["w_done"], 1)
                if s == 4 and not first:
                    alone = isinstance(turn, int) and turn == TURNS - 1
                    finish(turn - 1, None if alone else turn + 1)
                if s >= 1:
                    down(s - 1, turn, par)
                elif not first:
                    down(SLOTS - 1, turn - 1, 1 - par)

            def finish(turn, upcoming):
                at(pe, "ya_ready", turn, 3)
                at(pe, "yb_ready", turn, 3)
                if upcoming is not None:
                    at(pe, "iprob_sub", upcoming, HT)
                for t in range(TILES):
                    b, c = (b5, b6, b7)[t // 2], (t % 2) * D
                    tr(b[:, c:c + P], yTA[:, t * P:(t + 1) * P])
                    ins = mm(b[:, c + P:c + D], yTB[:, t * P:(t + 1) * P], ident2[:, :], start=True, stop=True)
                ins.then_inc(S["fin_done"], 1)

            turns(pe, lambda turn: None, front, experts)
            down(SLOTS - 1, TURNS - 1, 1)
            finish(TURNS - 1, None)


def reduction_matrix():
    basis = np.arange(NS)
    out = np.zeros((NPROD, 2 * NQ), np.float32)
    for q in range(NQ):
        bits = range(1, NQ) if q == 0 else range(q + 1)
        parity = sum((basis >> (NQ - 1 - b)) & 1 for b in bits) % 2
        out[:2 * NS, q] = np.tile(1.0 - 2.0 * parity, 2)
        out[2 * NS + NS * q:2 * NS + NS * (q + 1), NQ + q] = 2.0
    return out


_ORDER = ["patches", "tokens", "conv_w", "conv_b", "wq", "wk", "wv", "wo", "tok_const", "params", "post_w",
          "wq_big", "wk_big", "wv_big", "wout_big", "bout_big", "gate_w", "bias",
          "wuA_in", "wuB_in", "bu", "wgA_in", "wgB_in", "bg", "wd", "bd", "reduce_w", "ident_in"]


def kernel(**inputs):
    import concourse.bacc as _bacc
    from concourse.bass_utils import run_bass_kernel_spmd as _run

    a = {k: np.asarray(v) for k, v in inputs.items()}
    f = np.float32

    def stack(w, b):
        return np.concatenate([w, b[None]], 0)

    x = a["x"][:, :, :80, :80].reshape(NB, 3, 5, 16, 5, 16).transpose(1, 3, 5, 0, 2, 4).reshape(PIX, NB, IMG)
    pad = np.zeros((PIX, NB, SLOT), f)
    pad[:, :, :IMG] = x
    patches = np.ascontiguousarray(pad.reshape(KP, P, TURNS, BB * SLOT).transpose(2, 1, 0, 3))

    def heads(w, b, extra_row):
        full = stack(w.T, b).reshape(D + 1, HEADS, HD)
        out = np.zeros((D + 1 + 2 * BB, HEADS, 32), f)
        out[:D + 1, :, :HD] = full
        for i in range(BB):
            out[D + 1 + extra_row + i, :, HD + i] = 1.0
        return out.reshape(D + 1 + 2 * BB, HT * P)

    tok_const = np.zeros((1 + 2 * BB, P), f)
    tok_const[0] = 1.0
    tok_const[1 + BB:] = -1e30
    for i in range(BB):
        tok_const[1 + i, i * SLOT:(i + 1) * SLOT] = 1.0
        tok_const[1 + BB + i, i * SLOT:i * SLOT + IMG] = 0.0

    def rows(w, n):
        return np.ascontiguousarray(w.reshape(n, P, -1).transpose(1, 0, 2).reshape(P, -1))

    qkv, bqkv = a["L0_attn_w_qkv"], a["L0_attn_b_qkv"]
    big = [rows(stack(qkv[:, i * QK:(i + 1) * QK], bqkv[i * QK:(i + 1) * QK]).T, KQ) for i in range(3)]

    def experts(w, shared):
        return np.concatenate([w, shared[None]], 0)

    wu, wg, wd = (experts(a[f"L0_ffn_W{n}"], a[f"L0_ffn_sW{n}"]) for n in "ugd")
    bu, bg, bd = (experts(a[f"L0_ffn_b{n}"], a[f"L0_ffn_sb{n}"]) for n in "ugd")

    def by_block(w):
        rows_ = w.transpose(1, 0, 2).reshape(D, ES * HID)
        return rows_[:P], np.concatenate([rows_[P:], rows_[P:]], 0)

    bd2 = np.zeros((WR, D), f)
    bd2[:ES] = bd2[WR - ES:] = bd
    arrays = {
        "patches": patches,
        "tokens": np.ascontiguousarray(a["x_txt"].T),
        "conv_w": rows(a["L0_tok_conv_w"].reshape(D, PIX).T, KP).reshape(P, KP, D),
        "conv_b": a["L0_tok_conv_b"].reshape(D, 1),
        "wq": heads(a["L0_tok_wq"], a["L0_tok_bq"], 0),
        "wk": heads(a["L0_tok_wk"], a["L0_tok_bk"], BB),
        "wv": stack(a["L0_tok_wv"].T, a["L0_tok_bv"]),
        "wo": stack(a["L0_tok_wo"].T, a["L0_tok_bo"]),
        "tok_const": tok_const,
        "params": a["L0_txt_quantum_params"].reshape(-1, 36),
        "post_w": stack(a["L0_txt_post_w"].T, a["L0_txt_post_b"]),
        "wq_big": big[0], "wk_big": big[1], "wv_big": big[2],
        "wout_big": rows(a["L0_attn_w_out"], KQ),
        "bout_big": a["L0_attn_b_out"].reshape(1, D),
        "gate_w": stack(a["L0_ffn_gate_w"], a["L0_ffn_gate_b"]),
        "bias": a["L0_ffn_bias"],
        "wuA_in": by_block(wu)[0], "wuB_in": by_block(wu)[1], "bu": bu.T,
        "wgA_in": by_block(wg)[0], "wgB_in": by_block(wg)[1], "bg": bg.T,
        "wd": wd.transpose(1, 0, 2).reshape(HID, ES * D), "bd": bd2,
        "reduce_w": reduction_matrix().reshape(RB, P, 2 * NQ).transpose(1, 0, 2),
        "ident_in": np.eye(P, dtype=f),
    }
    nc = _bacc.Bacc("TRN2", target_bir_lowering=False, num_devices=1)
    feed, args = {}, []
    for name in _ORDER:
        arr = np.ascontiguousarray(arrays[name])
        feed[f"in_{name}_dram"] = arr
        args.append(nc.dram_tensor(f"in_{name}_dram", arr.shape, mybir.dt.from_np(arr.dtype), kind="ExternalInput").ap())
    args.append(nc.dram_tensor("out_0_dram", (NB, SEQ, D), F32, kind="ExternalOutput").ap())
    early_fusion(nc, *args)
    r = _run(nc, [feed], core_ids=[0])
    return r.results[0]["out_0_dram"]
```
